# Optimizing a Trainium2 kernel written in Bass

```python
import numpy as np
import jax
import jax.numpy as jnp

def _softmax(x, axis=-1):
    return jax.nn.softmax(x, axis=axis)

def _gelu(x):
    return jax.nn.gelu(x, approximate=True)

def _silu(x):
    return jax.nn.silu(x)

def _sigmoid(x):
    return jax.nn.sigmoid(x)

def _layernorm(x, axis=-1, eps=1e-05):
    m = jnp.mean(x, axis=axis, keepdims=True)
    v = jnp.var(x, axis=axis, keepdims=True)
    return (x - m) / jnp.sqrt(v + eps)

def _scatter_add(tgt, idx, src, axis=0):
    return tgt.at[idx].add(src)

def _segment_sum(src, seg, n):
    return jax.ops.segment_sum(src, seg, n)
kernel_name = 'mk_xattn_ffn_d4_seqx_r8_631e70'

def setup_inputs(seed: int=0):
    np.random.seed(seed)
    _w = jnp.asarray

    def _rec_inputs():
        import jax
        import jax.numpy as jnp
        _rk = jax.random.key(seed)
        x = -0.0005857 + 0.9999 * jax.random.normal(jax.random.fold_in(_rk, 1), (64, 64, 128), jnp.float32)
        _lenS = 64 - jax.random.randint(jax.random.fold_in(_rk, 7), (64,), 0, max(1, 64 // 4) + 1, jnp.int32)
        _lenS2 = 64 - jax.random.randint(jax.random.fold_in(_rk, 8), (64,), 0, max(1, 64 // 4) + 1, jnp.int32)
        _ctx_1024P = jax.random.normal(jax.random.fold_in(_rk, 11), (64, 16, 128), jnp.float32)
        _ctx_1024c = jax.random.dirichlet(jax.random.fold_in(_rk, 511), 0.3 * jnp.ones((16,), jnp.float32), (64, 64))
        _ctx_1024t = jnp.einsum('bsk,bkd->bsd', _ctx_1024c, _ctx_1024P)
        _ctx_1024t = _ctx_1024t * jax.lax.rsqrt(jnp.mean(jnp.square(_ctx_1024t)) + 1e-12) * 0.953939
        ctx_1024 = -0.000264403 + 1.00002 * (_ctx_1024t + 0.3 * jax.random.normal(jax.random.fold_in(_rk, 611), (64, 64, 128), jnp.float32))
        _validS = jnp.arange(64)[None, :] < _lenS[:, None]
        _validS2 = jnp.arange(64)[None, :] < _lenS2[:, None]
        _causal = jnp.tril(jnp.ones((64, 64), dtype=bool))
        mask_Bx1xSxS2_ff0 = jnp.where(jnp.ones((64, 1, 64, 64), dtype=bool), 0.0, -1000000000.0).astype(jnp.float32)
        return (x, ctx_1024, mask_Bx1xSxS2_ff0)
    x, ctx_1024, mask_Bx1xSxS2_ff0 = _rec_inputs()

    def _L0_xattn_setup():
        import jax, jax.numpy as jnp
        import numpy as np
        D_MODEL = 128
        N_HEADS = 16
        D_K = D_MODEL // N_HEADS
        key = jax.random.key(seed)
        ks = jax.random.split(key, 12)
        B, S, D = (2, 256, D_MODEL)
        lim = 1.0 / np.sqrt(D)

        def lin(k):
            kw, kb = jax.random.split(k)
            W = jax.random.uniform(kw, (D, D), jnp.float32, -lim, lim)
            b = jax.random.uniform(kb, (D,), jnp.float32, -lim, lim)
            return (W, b)
        wq, bq = lin(ks[0])
        wk, bk = lin(ks[1])
        wv, bv = lin(ks[2])
        wo, bo = lin(ks[3])
        return {'query': jax.random.normal(ks[4], (B, S, D), jnp.float32), 'key': jax.random.normal(ks[5], (B, S, D), jnp.float32), 'value': jax.random.normal(ks[6], (B, S, D), jnp.float32), 'wq': wq, 'bq': bq, 'wk': wk, 'bk': bk, 'wv': wv, 'bv': bv, 'wo': wo, 'bo': bo, 'time_decay': jnp.float32(0.1)}
    _L0_xattn_all = _L0_xattn_setup()
    _L0_xattn_in = {k: v for k, v in _L0_xattn_all.items() if k in ('wq', 'bq', 'wk', 'bk', 'wv', 'bv', 'wo', 'bo', 'time_decay')}
    del _L0_xattn_all

    def _L0_ffn_setup():
        import jax, jax.numpy as jnp
        import numpy as np
        NUM_EXPERTS = 8
        TOP_K = 2
        CAP_RATIO = 1.25
        INIT_STD = 0.02
        key = jax.random.key(seed)
        k1, k2, k3, k4 = jax.random.split(key, 4)
        B, T, H, F = (4, 256, 128, 512)
        x = jax.random.normal(k1, (B, T, H), jnp.float32)
        router_w = jax.random.normal(k2, (NUM_EXPERTS, H), jnp.float32) * INIT_STD
        w1 = jax.random.normal(k3, (NUM_EXPERTS, H, F), jnp.float32) * INIT_STD
        w2 = jax.random.normal(k4, (NUM_EXPERTS, F, H), jnp.float32) * INIT_STD
        return {'x': x, 'router_w': router_w, 'w1': w1, 'w2': w2}
    _L0_ffn_all = _L0_ffn_setup()
    _L0_ffn_in = {k: v for k, v in _L0_ffn_all.items() if k in ('router_w', 'w1', 'w2')}
    del _L0_ffn_all

    def _L1_xattn_setup():
        import jax, jax.numpy as jnp
        import numpy as np
        N_HEADS = 16
        NEG_FILL = -1000000000.0
        PADDING = 0.0
        key = jax.random.key(seed)
        kq, kk, kv = jax.random.split(key, 3)
        B, S, D = (2, 256, 128)
        q = jax.random.normal(kq, (B, S, D), dtype=jnp.float32)
        k = jax.random.normal(kk, (B, S, D), dtype=jnp.float32)
        v = jax.random.normal(kv, (B, S, D), dtype=jnp.float32)
        return {'q': q, 'k': k, 'v': v, 'is_masked': 1}
    _L1_xattn_all = _L1_xattn_setup()
    _L1_xattn_in = {k: v for k, v in _L1_xattn_all.items() if k in ()}
    del _L1_xattn_all

    def _L1_ffn_setup():
        import math
        import jax, jax.numpy as jnp
        import numpy as np
        B, L, D, FF, E, K = (4, 256, 128, 512, 8, 2)
        CAPACITY_FACTOR = 1.25
        T = B * L
        CAP = math.ceil(CAPACITY_FACTOR * T * K / E)
        key = jax.random.key(seed)
        ks = jax.random.split(key, 7)
        return {'h': jax.random.normal(ks[0], (B, L, D), dtype=jnp.float32), 'gate_w': 0.02 * jax.random.normal(ks[1], (E, D), dtype=jnp.float32), 'gate_b': jnp.zeros((E,), dtype=jnp.float32), 'W1': 0.02 * jax.random.normal(ks[2], (E, D, FF), dtype=jnp.float32), 'b1': jnp.zeros((E, FF), dtype=jnp.float32), 'W2': 0.02 * jax.random.normal(ks[3], (E, FF, D), dtype=jnp.float32), 'b2': jnp.zeros((E, D), dtype=jnp.float32)}
    _L1_ffn_all = _L1_ffn_setup()
    _L1_ffn_in = {k: v for k, v in _L1_ffn_all.items() if k in ('gate_w', 'gate_b', 'W1', 'b1', 'W2', 'b2')}
    del _L1_ffn_all

    def _L2_xattn_setup():
        import jax, jax.numpy as jnp
        import numpy as np
        HIDDEN = 128
        NUM_HEADS = 16
        DEPTH = HIDDEN // NUM_HEADS
        B, F, T = (2, 256, 256)
        key = jax.random.key(seed)
        ks = jax.random.split(key, 6)
        scale = 1.0 / np.sqrt(HIDDEN)
        return {'query_input': jax.random.normal(ks[0], (B, F, HIDDEN), dtype=jnp.float32), 'source_input': jax.random.normal(ks[1], (B, T, HIDDEN), dtype=jnp.float32), 'bias': jnp.zeros((B, 1, F, T), dtype=jnp.float32), 'wq': jax.random.normal(ks[2], (HIDDEN, NUM_HEADS, DEPTH), dtype=jnp.float32) * scale, 'wk': jax.random.normal(ks[3], (HIDDEN, NUM_HEADS, DEPTH), dtype=jnp.float32) * scale, 'wv': jax.random.normal(ks[4], (HIDDEN, NUM_HEADS, DEPTH), dtype=jnp.float32) * scale, 'wo': jax.random.normal(ks[5], (NUM_HEADS, DEPTH, HIDDEN), dtype=jnp.float32) * scale}
    _L2_xattn_all = _L2_xattn_setup()
    _L2_xattn_in = {k: v for k, v in _L2_xattn_all.items() if k in ('wq', 'wk', 'wv', 'wo')}
    del _L2_xattn_all

    def _L2_ffn_setup():
        import jax, jax.numpy as jnp
        import numpy as np
        BLOCK_SIZE = 32
        FP6_E2M3_MAX = 7.5

        def _build_fp6_e2m3_grid():
            vals = set()
            for bits in range(64):
                s = bits >> 5 & 1
                e = bits >> 3 & 3
                m = bits & 7
                v = m / 8.0 if e == 0 else (1.0 + m / 8.0) * 2.0 ** (e - 1)
                vals.add(-v if s else v)
            return np.array(sorted(vals), dtype=np.float32)
        _GRID = jnp.asarray(_build_fp6_e2m3_grid())

        def _nearest_on_grid(x, grid):
            idx = jnp.clip(jnp.searchsorted(grid, x), 0, grid.shape[0] - 1)
            idx_lo = jnp.maximum(idx - 1, 0)
            v_hi = grid[idx]
            v_lo = grid[idx_lo]
            return jnp.where(jnp.abs(x - v_lo) <= jnp.abs(x - v_hi), v_lo, v_hi)

        def _mx_quantize(t, eps=1e-30):
            rows, K = t.shape
            blocks = t.reshape(rows, K // BLOCK_SIZE, BLOCK_SIZE)
            scales = jnp.maximum(jnp.max(jnp.abs(blocks), axis=-1) / FP6_E2M3_MAX, eps)
            q = _nearest_on_grid(blocks / scales[..., None], _GRID)
            return (q, scales)
        key = jax.random.key(seed)
        k1, k2, k3 = jax.random.split(key, 3)
        x = jax.random.normal(k1, (8, 1024, 128), dtype=jnp.float32)
        weight = jax.random.normal(k2, (128, 128), dtype=jnp.float32) * 0.02
        bias = jax.random.normal(k3, (128,), dtype=jnp.float32) * 0.02
        return {'x': x, 'weight': weight, 'bias': bias}
    _L2_ffn_all = _L2_ffn_setup()
    _L2_ffn_in = {k: v for k, v in _L2_ffn_all.items() if k in ('weight', 'bias')}
    del _L2_ffn_all

    def _L3_xattn_setup():
        import jax, jax.numpy as jnp
        import numpy as np
        DIM = 128
        NH = 8
        HD = DIM // NH
        E = 8
        EPS = 1e-05

        def rope_cos_sin(L, hd):
            inv_freq = 1.0 / 10000.0 ** (jnp.arange(0, hd, 2, dtype=jnp.float32) / hd)
            freqs = jnp.arange(L, dtype=jnp.float32)[:, None] * inv_freq[None, :]
            emb = jnp.concatenate([freqs, freqs], axis=-1)
            return (jnp.cos(emb), jnp.sin(emb))

        def rotate_half(x):
            x1 = x[..., 0::2]
            x2 = x[..., 1::2]
            return jnp.stack((-x2, x1), axis=-1).reshape(x.shape)

        def rope(t, cos, sin):
            return t * cos[None, None] + rotate_half(t) * sin[None, None]

        def heads(t):
            B, L, C = t.shape
            return t.reshape(B, L, NH, HD).transpose(0, 2, 1, 3)
        key = jax.random.key(seed)
        ks = jax.random.split(key, 32)
        std = 0.02
        d = {}
        d['x'] = jax.random.normal(ks[0], (16, 64, DIM), jnp.float32)
        d['h_a'] = jax.random.normal(ks[1], (16, 32, DIM), jnp.float32)
        d['h_t'] = jax.random.normal(ks[2], (16, 32, DIM), jnp.float32)
        names = ['qa', 'ka', 'va', 'qt', 'kt', 'vt', 'o', 'ffn']
        for i, n in enumerate(names):
            d['W_' + n] = jax.random.normal(ks[3 + 2 * i], (E, DIM, DIM), jnp.float32) * std
            d['b_' + n] = jax.random.normal(ks[4 + 2 * i], (E, DIM), jnp.float32) * std
        d['gamma'] = jnp.ones((E, DIM), jnp.float32)
        d['beta'] = jnp.zeros((E, DIM), jnp.float32)
        d['gating_factor'] = jnp.zeros((E,), jnp.float32)
        d['expert_idx'] = 3
        return d
    _L3_xattn_all = _L3_xattn_setup()
    _L3_xattn_in = {k: v for k, v in _L3_xattn_all.items() if k in ('W_qa', 'b_qa', 'W_ka', 'b_ka', 'W_va', 'b_va', 'W_qt', 'b_qt', 'W_kt', 'b_kt', 'W_vt', 'b_vt', 'W_o', 'b_o', 'W_ffn', 'b_ffn', 'gamma', 'beta', 'gating_factor')}
    del _L3_xattn_all

    def _L3_ffn_setup():
        import jax, jax.numpy as jnp
        import numpy as np
        EPS = 1e-06
        N_EXPERTS = 8

        def _rms_norm(x, scale, eps=EPS):
            mean_sq = jnp.mean(x.astype(jnp.float32) ** 2, axis=-1, keepdims=True)
            s = scale.astype(jnp.float32) * jax.lax.rsqrt(mean_sq + eps)
            return x * s.astype(x.dtype)

        def _dist2(x, y):
            nx = jnp.sum(x ** 2, axis=-1)[..., :, None]
            ny = jnp.sum(y ** 2, axis=-1)[..., None, :]
            return nx + ny - 2.0 * (x @ y.T)
        key = jax.random.key(seed)
        ks = jax.random.split(key, 5)
        dim, hidden, E = (128, 256, N_EXPERTS)
        x = jax.random.normal(ks[0], (4, 256, dim), dtype=jnp.float32)
        scale = jnp.ones((dim,), dtype=jnp.float32)
        centroids = jax.random.normal(ks[1], (E, dim), dtype=jnp.float32)
        up_w = jax.random.normal(ks[2], (E, dim, hidden * 2), dtype=jnp.float32) * dim ** (-0.5)
        down_w = jax.random.normal(ks[3], (E, hidden, dim), dtype=jnp.float32) * hidden ** (-0.5)
        return {'x': x, 'scale': scale, 'centroids': centroids, 'up_w': up_w, 'down_w': down_w}
    _L3_ffn_all = _L3_ffn_setup()
    _L3_ffn_in = {k: v for k, v in _L3_ffn_all.items() if k in ('scale', 'centroids', 'up_w', 'down_w')}
    del _L3_ffn_all
    return {'x': x, 'ctx_1024': ctx_1024, 'mask_Bx1xSxS2_ff0': mask_Bx1xSxS2_ff0, 'L0_xattn_wq': _L0_xattn_in['wq'], 'L0_xattn_bq': _L0_xattn_in['bq'], 'L0_xattn_wk': _L0_xattn_in['wk'], 'L0_xattn_bk': _L0_xattn_in['bk'], 'L0_xattn_wv': _L0_xattn_in['wv'], 'L0_xattn_bv': _L0_xattn_in['bv'], 'L0_xattn_wo': _L0_xattn_in['wo'], 'L0_xattn_bo': _L0_xattn_in['bo'], 'L0_xattn_time_decay': _L0_xattn_in['time_decay'], 'L0_ffn_router_w': _L0_ffn_in['router_w'], 'L0_ffn_w1': _L0_ffn_in['w1'], 'L0_ffn_w2': _L0_ffn_in['w2'], 'L1_ffn_gate_w': _L1_ffn_in['gate_w'], 'L1_ffn_gate_b': _L1_ffn_in['gate_b'], 'L1_ffn_W1': _L1_ffn_in['W1'], 'L1_ffn_b1': _L1_ffn_in['b1'], 'L1_ffn_W2': _L1_ffn_in['W2'], 'L1_ffn_b2': _L1_ffn_in['b2'], 'L2_xattn_wq': _L2_xattn_in['wq'], 'L2_xattn_wk': _L2_xattn_in['wk'], 'L2_xattn_wv': _L2_xattn_in['wv'], 'L2_xattn_wo': _L2_xattn_in['wo'], 'L2_ffn_weight': _L2_ffn_in['weight'], 'L2_ffn_bias': _L2_ffn_in['bias'], 'L3_xattn_W_qa': _L3_xattn_in['W_qa'], 'L3_xattn_b_qa': _L3_xattn_in['b_qa'], 'L3_xattn_W_ka': _L3_xattn_in['W_ka'], 'L3_xattn_b_ka': _L3_xattn_in['b_ka'], 'L3_xattn_W_va': _L3_xattn_in['W_va'], 'L3_xattn_b_va': _L3_xattn_in['b_va'], 'L3_xattn_W_qt': _L3_xattn_in['W_qt'], 'L3_xattn_b_qt': _L3_xattn_in['b_qt'], 'L3_xattn_W_kt': _L3_xattn_in['W_kt'], 'L3_xattn_b_kt': _L3_xattn_in['b_kt'], 'L3_xattn_W_vt': _L3_xattn_in['W_vt'], 'L3_xattn_b_vt': _L3_xattn_in['b_vt'], 'L3_xattn_W_o': _L3_xattn_in['W_o'], 'L3_xattn_b_o': _L3_xattn_in['b_o'], 'L3_xattn_W_ffn': _L3_xattn_in['W_ffn'], 'L3_xattn_b_ffn': _L3_xattn_in['b_ffn'], 'L3_xattn_gamma': _L3_xattn_in['gamma'], 'L3_xattn_beta': _L3_xattn_in['beta'], 'L3_xattn_gating_factor': _L3_xattn_in['gating_factor'], 'L3_ffn_scale': _L3_ffn_in['scale'], 'L3_ffn_centroids': _L3_ffn_in['centroids'], 'L3_ffn_up_w': _L3_ffn_in['up_w'], 'L3_ffn_down_w': _L3_ffn_in['down_w']}

def reference(x, ctx_1024, mask_Bx1xSxS2_ff0, L0_xattn_wq, L0_xattn_bq, L0_xattn_wk, L0_xattn_bk, L0_xattn_wv, L0_xattn_bv, L0_xattn_wo, L0_xattn_bo, L0_xattn_time_decay, L0_ffn_router_w, L0_ffn_w1, L0_ffn_w2, L1_ffn_gate_w, L1_ffn_gate_b, L1_ffn_W1, L1_ffn_b1, L1_ffn_W2, L1_ffn_b2, L2_xattn_wq, L2_xattn_wk, L2_xattn_wv, L2_xattn_wo, L2_ffn_weight, L2_ffn_bias, L3_xattn_W_qa, L3_xattn_b_qa, L3_xattn_W_ka, L3_xattn_b_ka, L3_xattn_W_va, L3_xattn_b_va, L3_xattn_W_qt, L3_xattn_b_qt, L3_xattn_W_kt, L3_xattn_b_kt, L3_xattn_W_vt, L3_xattn_b_vt, L3_xattn_W_o, L3_xattn_b_o, L3_xattn_W_ffn, L3_xattn_b_ffn, L3_xattn_gamma, L3_xattn_beta, L3_xattn_gating_factor, L3_ffn_scale, L3_ffn_centroids, L3_ffn_up_w, L3_ffn_down_w):
    import jax
    import jax.numpy as jnp

    def _L0_xattn_ref(query, key, value, wq, bq, wk, bk, wv, bv, wo, bo, time_decay):
        import jax, jax.numpy as jnp
        import numpy as np
        D_MODEL = 128
        N_HEADS = 16
        D_K = D_MODEL // N_HEADS
        B, S, D = query.shape
        H, Dk = (N_HEADS, D_K)

        def proj(x, W, b):
            y = jnp.einsum('bsd,ed->bse', x, W) + b
            return y.reshape(B, S, H, Dk).transpose(0, 2, 1, 3)
        Q = proj(query, wq, bq)
        K = proj(key, wk, bk)
        V = proj(value, wv, bv)
        scores = jnp.einsum('bhqd,bhkd->bhqk', Q, K) / jnp.sqrt(jnp.float32(Dk))
        pos = jnp.arange(S, dtype=jnp.float32)
        decay = -time_decay * jnp.abs(pos[:, None] - pos[None, :])
        scores = scores + decay[None, None, :, :]
        attn = jax.nn.softmax(scores, axis=-1)
        ctx = jnp.einsum('bhqk,bhkd->bhqd', attn, V)
        ctx = ctx.transpose(0, 2, 1, 3).reshape(B, S, D)
        out = jnp.einsum('bsd,ed->bse', ctx, wo) + bo
        return out

    def _L0_ffn_ref(x, router_w, w1, w2):
        import jax, jax.numpy as jnp
        import numpy as np
        NUM_EXPERTS = 8
        TOP_K = 2
        CAP_RATIO = 1.25
        INIT_STD = 0.02
        B, T, H = x.shape
        E, K = (NUM_EXPERTS, TOP_K)
        xf = x.reshape(-1, H)
        N = xf.shape[0]
        P = N * K
        capacity = int(CAP_RATio * N * K / E) + 1 if False else int(CAP_RATIO * N * K / E) + 1
        logits = xf @ router_w.T
        probs = jax.nn.softmax(logits, axis=-1)
        k_probs, k_idx = jax.lax.top_k(probs, K)
        k_probs = k_probs / jnp.sum(k_probs, axis=-1, keepdims=True)
        flat_e = k_idx.reshape(-1)
        onehot = jax.nn.one_hot(flat_e, E, dtype=jnp.int32)
        rank = jnp.take_along_axis(jnp.cumsum(onehot, axis=0) - 1, flat_e[:, None], axis=1)[:, 0]
        keep = rank < capacity
        slot = jnp.minimum(rank, capacity - 1)
        token_id = jnp.arange(P) // K
        dispatched = jnp.where(keep[:, None], xf[token_id], 0.0)
        buf = jnp.zeros((E, capacity, H), x.dtype).at[flat_e, slot].add(dispatched)
        h = jax.nn.silu(jnp.einsum('ech,ehf->ecf', buf, w1))
        out_buf = jnp.einsum('ecf,efh->ech', h, w2)
        pair_out = out_buf[flat_e, slot] * keep[:, None].astype(x.dtype)
        combined = jnp.sum(pair_out.reshape(N, K, H) * k_probs[..., None], axis=1)
        return combined.reshape(B, T, H) + x

    def _L1_xattn_ref(q, k, v, is_masked):
        import jax, jax.numpy as jnp
        import numpy as np
        N_HEADS = 16
        NEG_FILL = -1000000000.0
        PADDING = 0.0
        B, S, D = q.shape
        d_key = D // N_HEADS

        def split_heads(x):
            return x.reshape(B, S, N_HEADS, d_key).transpose(0, 2, 1, 3)
        qh, kh, vh = (split_heads(q), split_heads(k), split_heads(v))
        scale = 1.0 / jnp.sqrt(jnp.asarray(d_key, dtype=q.dtype))
        scores = jnp.einsum('bhqd,bhkd->bhqk', qh, kh) * scale
        mask = scores != PADDING
        if is_masked:
            causal = jnp.tril(jnp.ones((S, S), dtype=bool))
            mask = mask & causal
        scores = jnp.where(mask, scores, jnp.asarray(NEG_FILL, dtype=scores.dtype))
        probs = jax.nn.softmax(scores, axis=-1)
        out = jnp.einsum('bhqk,bhkd->bhqd', probs, vh)
        return out.transpose(0, 2, 1, 3).reshape(B, S, D)

    def _L1_ffn_ref(h, gate_w, gate_b, W1, b1, W2, b2):
        import math
        import jax, jax.numpy as jnp
        import numpy as np
        B, L, D, FF, E, K = (4, 256, 128, 512, 8, 2)
        CAPACITY_FACTOR = 1.25
        T = B * L
        CAP = math.ceil(CAPACITY_FACTOR * T * K / E)
        Bb, Ll, Dm = h.shape
        Tt = Bb * Ll
        x = h.reshape(Tt, Dm)
        logits = x @ gate_w.T + gate_b
        probs = jax.nn.softmax(logits, axis=-1)
        topk_prob, topk_idx = jax.lax.top_k(probs, K)
        y = jnp.zeros((Tt, Dm), dtype=h.dtype)
        n_slots = E * CAP
        for c in range(K):
            idx = topk_idx[:, c]
            prb = topk_prob[:, c]
            oh = jax.nn.one_hot(idx, E, dtype=jnp.int32)
            pos = jnp.take_along_axis(jnp.cumsum(oh, axis=0) - 1, idx[:, None], axis=1)[:, 0]
            keep = pos < CAP
            buf_idx = jnp.where(keep, idx * CAP + pos, n_slots)
            xbuf = jnp.zeros((n_slots, Dm), x.dtype).at[buf_idx].set(x, mode='drop')
            xb = xbuf.reshape(E, CAP, Dm)
            hmid = jax.nn.relu(jnp.einsum('ecd,edf->ecf', xb, W1) + b1[:, None, :])
            yb = jnp.einsum('ecf,efd->ecd', hmid, W2) + b2[:, None, :]
            ytok = yb.reshape(n_slots, Dm)[jnp.clip(buf_idx, 0, n_slots - 1)]
            y = y + ytok * (prb * keep.astype(prb.dtype))[:, None]
        return y.reshape(Bb, Ll, Dm)

    def _L2_xattn_ref(query_input, source_input, bias, wq, wk, wv, wo):
        import jax, jax.numpy as jnp
        import numpy as np
        HIDDEN = 128
        NUM_HEADS = 16
        DEPTH = HIDDEN // NUM_HEADS
        B, F, T = (2, 256, 256)
        q = jnp.einsum('bfh,hnd->bfnd', query_input, wq)
        k = jnp.einsum('bth,hnd->btnd', source_input, wk)
        v = jnp.einsum('bth,hnd->btnd', source_input, wv)
        q = q * DEPTH ** (-0.5)
        logits = jnp.einsum('btnd,bfnd->bnft', k, q) + bias
        weights = jax.nn.softmax(logits, axis=-1)
        attn = jnp.einsum('bnft,btnd->bfnd', weights, v)
        return jnp.einsum('bfnd,ndh->bfh', attn, wo)

    def _L2_ffn_ref(x, weight, bias):
        import jax, jax.numpy as jnp
        import numpy as np
        BLOCK_SIZE = 32
        FP6_E2M3_MAX = 7.5

        def _build_fp6_e2m3_grid():
            vals = set()
            for bits in range(64):
                s = bits >> 5 & 1
                e = bits >> 3 & 3
                m = bits & 7
                v = m / 8.0 if e == 0 else (1.0 + m / 8.0) * 2.0 ** (e - 1)
                vals.add(-v if s else v)
            return np.array(sorted(vals), dtype=np.float32)
        _GRID = jnp.asarray(_build_fp6_e2m3_grid())

        def _nearest_on_grid(x, grid):
            idx = jnp.clip(jnp.searchsorted(grid, x), 0, grid.shape[0] - 1)
            idx_lo = jnp.maximum(idx - 1, 0)
            v_hi = grid[idx]
            v_lo = grid[idx_lo]
            return jnp.where(jnp.abs(x - v_lo) <= jnp.abs(x - v_hi), v_lo, v_hi)

        def _mx_quantize(t, eps=1e-30):
            rows, K = t.shape
            blocks = t.reshape(rows, K // BLOCK_SIZE, BLOCK_SIZE)
            scales = jnp.maximum(jnp.max(jnp.abs(blocks), axis=-1) / FP6_E2M3_MAX, eps)
            q = _nearest_on_grid(blocks / scales[..., None], _GRID)
            return (q, scales)
        batch_shape = x.shape[:-1]
        in_features = x.shape[-1]
        x2 = x.astype(jnp.float32).reshape(-1, in_features)
        w2 = weight.astype(jnp.float32)
        xq, xs = _mx_quantize(x2)
        wq, ws = _mx_quantize(w2)
        xd = (xq * xs[..., None]).reshape(x2.shape)
        wd = (wq * ws[..., None]).reshape(w2.shape)
        out = xd @ wd.T + bias
        return out.reshape(*batch_shape, -1)

    def _L3_xattn_ref(x, h_a, h_t, W_qa, b_qa, W_ka, b_ka, W_va, b_va, W_qt, b_qt, W_kt, b_kt, W_vt, b_vt, W_o, b_o, W_ffn, b_ffn, gamma, beta, gating_factor, expert_idx):
        import jax, jax.numpy as jnp
        import numpy as np
        DIM = 128
        NH = 8
        HD = DIM // NH
        E = 8
        EPS = 1e-05

        def rope_cos_sin(L, hd):
            inv_freq = 1.0 / 10000.0 ** (jnp.arange(0, hd, 2, dtype=jnp.float32) / hd)
            freqs = jnp.arange(L, dtype=jnp.float32)[:, None] * inv_freq[None, :]
            emb = jnp.concatenate([freqs, freqs], axis=-1)
            return (jnp.cos(emb), jnp.sin(emb))

        def rotate_half(x):
            x1 = x[..., 0::2]
            x2 = x[..., 1::2]
            return jnp.stack((-x2, x1), axis=-1).reshape(x.shape)

        def rope(t, cos, sin):
            return t * cos[None, None] + rotate_half(t) * sin[None, None]

        def heads(t):
            B, L, C = t.shape
            return t.reshape(B, L, NH, HD).transpose(0, 2, 1, 3)
        e = expert_idx

        def lin(t, W, b):
            return t @ W[e].T + b[e]
        B, T, C = x.shape
        Ka = h_a.shape[1]
        Kt = h_t.shape[1]
        q_a = heads(lin(x, W_qa, b_qa))
        q_t = heads(lin(x, W_qt, b_qt))
        k_a = heads(lin(h_a, W_ka, b_ka))
        v_a = heads(lin(h_a, W_va, b_va))
        k_t = heads(lin(h_t, W_kt, b_kt))
        v_t = heads(lin(h_t, W_vt, b_vt))
        cos_m, sin_m = rope_cos_sin(T, HD)
        q_a = rope(q_a, cos_m, sin_m)
        q_t = rope(q_t, cos_m, sin_m)
        cos_a, sin_a = rope_cos_sin(Ka, HD)
        k_a = rope(k_a, cos_a, sin_a)
        cos_t, sin_t = rope_cos_sin(Kt, HD)
        k_t = rope(k_t, cos_t, sin_t)
        ratio_g = jax.nn.sigmoid(gating_factor[e])
        s_a = jnp.einsum('bhtd,bhkd->bhtk', q_a, k_a)
        s_t = jnp.einsum('bhtd,bhkd->bhtk', q_t, k_t) * ratio_g
        scores = jnp.concatenate([s_a, s_t], axis=-1) / np.sqrt(HD)
        w = jax.nn.softmax(scores, axis=-1)
        v = jnp.concatenate([v_a, v_t], axis=2)
        out = jnp.einsum('bhtk,bhkd->bhtd', w, v)
        out = out.transpose(0, 2, 1, 3).reshape(B, T, C)
        out = lin(out, W_o, b_o)
        x = out + x
        mu = jnp.mean(x, axis=-1, keepdims=True)
        var = jnp.var(x, axis=-1, keepdims=True)
        xn = (x - mu) / jnp.sqrt(var + EPS) * gamma[e] + beta[e]
        x = jax.nn.relu(lin(xn, W_ffn, b_ffn))
        return x

    def _L3_ffn_ref(x, scale, centroids, up_w, down_w):
        import jax, jax.numpy as jnp
        import numpy as np
        EPS = 1e-06
        N_EXPERTS = 8

        def _rms_norm(x, scale, eps=EPS):
            mean_sq = jnp.mean(x.astype(jnp.float32) ** 2, axis=-1, keepdims=True)
            s = scale.astype(jnp.float32) * jax.lax.rsqrt(mean_sq + eps)
            return x * s.astype(x.dtype)

        def _dist2(x, y):
            nx = jnp.sum(x ** 2, axis=-1)[..., :, None]
            ny = jnp.sum(y ** 2, axis=-1)[..., None, :]
            return nx + ny - 2.0 * (x @ y.T)
        skip = x
        xn = _rms_norm(x, scale)
        ids = jnp.argmin(_dist2(xn, centroids), axis=-1)
        out = jnp.zeros_like(x)
        for e in range(N_EXPERTS):
            h = jnp.einsum('bsd,dh->bsh', xn, up_w[e])
            a, g = jnp.split(h, 2, axis=-1)
            y = jnp.einsum('bsh,hd->bsd', a * jax.nn.silu(g), down_w[e])
            out = jnp.where((ids == e)[..., None], y, out)
        return out + skip
    x = x + _L0_xattn_ref(_layernorm(x, axis=-1), ctx_1024, ctx_1024, L0_xattn_wq, L0_xattn_bq, L0_xattn_wk, L0_xattn_bk, L0_xattn_wv, L0_xattn_bv, L0_xattn_wo, L0_xattn_bo, L0_xattn_time_decay)
    x = x + _L0_ffn_ref(_layernorm(x, axis=-1), L0_ffn_router_w, L0_ffn_w1, L0_ffn_w2)
    x = x + _L1_xattn_ref(_layernorm(x, axis=-1), ctx_1024, ctx_1024, 1)
    x = x + _L1_ffn_ref(_layernorm(x, axis=-1), L1_ffn_gate_w, L1_ffn_gate_b, L1_ffn_W1, L1_ffn_b1, L1_ffn_W2, L1_ffn_b2)
    x = x + _L2_xattn_ref(_layernorm(x, axis=-1), ctx_1024, mask_Bx1xSxS2_ff0, L2_xattn_wq, L2_xattn_wk, L2_xattn_wv, L2_xattn_wo)
    x = x + _L2_ffn_ref(_layernorm(x, axis=-1), L2_ffn_weight, L2_ffn_bias)
    x = x + _L3_xattn_ref(_layernorm(x, axis=-1), ctx_1024, ctx_1024, L3_xattn_W_qa, L3_xattn_b_qa, L3_xattn_W_ka, L3_xattn_b_ka, L3_xattn_W_va, L3_xattn_b_va, L3_xattn_W_qt, L3_xattn_b_qt, L3_xattn_W_kt, L3_xattn_b_kt, L3_xattn_W_vt, L3_xattn_b_vt, L3_xattn_W_o, L3_xattn_b_o, L3_xattn_W_ffn, L3_xattn_b_ffn, L3_xattn_gamma, L3_xattn_beta, L3_xattn_gating_factor, 3)
    x = x + _L3_ffn_ref(_layernorm(x, axis=-1), L3_ffn_scale, L3_ffn_centroids, L3_ffn_up_w, L3_ffn_down_w)
    return x

_drawn_inputs = setup_inputs


def setup_inputs(seed=0):
    import zlib

    import numpy as np

    out = dict(_drawn_inputs(seed))
    spreads = {'L1_ffn_gate_b': (0.0, 0.501),
     'L1_ffn_b1': (0.0, 0.8),
     'L1_ffn_b2': (0.0, 0.428),
     'L3_xattn_gamma': (1.0, 0.6),
     'L3_xattn_beta': (0.0, 0.447),
     'L3_xattn_gating_factor': (0.0, 2.0),
     'L3_ffn_scale': (1.0, 0.2)}
    factors = {'L0_xattn_bq': 6.356,
     'L0_xattn_bk': 64.0,
     'L1_ffn_gate_w': 3.353,
     'L1_ffn_W1': 5.068,
     'L1_ffn_W2': 4.346,
     'L3_xattn_W_qa': 8.0,
     'L3_xattn_b_qa': 25.041,
     'L3_xattn_W_ka': 8.0,
     'L3_xattn_b_ka': 30.779,
     'L3_xattn_W_va': 8.0,
     'L3_xattn_b_va': 34.363,
     'L3_xattn_W_qt': 8.0,
     'L3_xattn_b_qt': 34.813,
     'L3_xattn_W_kt': 8.0,
     'L3_xattn_b_kt': 43.077,
     'L3_xattn_W_vt': 8.0,
     'L3_xattn_b_vt': 41.745,
     'L3_xattn_W_o': 8.0,
     'L3_xattn_b_o': 44.566,
     'L3_xattn_b_ffn': 3.223,
     'L2_ffn_bias': 2.752}
    for name, (base, spread) in spreads.items():
        noise = np.random.default_rng([zlib.crc32(name.encode()), seed]).standard_normal(out[name].shape)
        drawn = base * np.exp(spread * noise) if base else spread * noise
        out[name] = jnp.asarray(drawn.astype(out[name].dtype))
    for name, factor in factors.items():
        out[name] = (out[name] * factor).astype(out[name].dtype)
    return out
```

```python
from contextlib import ExitStack

import concourse.bass as bass
from concourse import mybir

ALU = mybir.AluOpType
ACT = mybir.ActivationFunctionType
F32 = mybir.dt.float32
AX_X = mybir.AxisListType.X

NT = 32
NBK = 8
NEG = -1000000000.0
MAGIC = 12582912.0

SQ = ["L0q", "L0k", "L0v", "L0o", "L2q", "L2k", "L2v", "L2o", "qa", "qar", "ka", "kar", "qt", "qtr", "kt", "ktr",
      "va", "vt", "o3", "ffn3"]
COL = ["bq0", "bk0", "qa", "qar", "ka", "kar", "qt", "qtr", "kt", "ktr", "gamma", "beta", "gf", "td"]
ROW = ["bv0", "bo0", "bv3", "bo3", "bffn3", "b2ffn", "scale3"]
SM = ["r0", "r1", "c3", "gb", "revi", "nh"]
CST = {"ident": 128, "ones": 128, "tri": 128, "cos": 128, "sin": 128, "dist": 64, "causal": 64, "km8": 4, "km16": 2, "jm": 4}


class Queue:

    def __init__(self, name):
        self.name = name
        self.ops = []
        self.sem = None
        self.count = 0


class Plan:

    def __init__(self, nc, ctx):
        self.nc = nc
        self.ctx = ctx
        self.q = {n: Queue(n) for n in ("pe", "act", "dve", "pool", "sp")}
        self.at = {}

    def phase(self, name):
        for n, q in self.q.items():
            if n != "sp":
                q.sem = self.ctx.enter_context(self.nc.semaphore(f"{name}_{n}"))
                q.count = 0

    def dma_sem(self, name):
        return self.ctx.enter_context(self.nc.semaphore(name))

    def op(self, eng, f, *a, w=(), m=None, **kw):
        q = self.q[eng]
        inc = None
        if m is not None:
            assert m not in self.at, m
            q.count += 1
            inc = (q.sem, 1)
            self.at[m] = (q.sem, q.count)
        q.ops.append((f, a, kw, tuple(w), inc))

    def dma(self, f, out, in_, sem, m, n, w=()):
        self.at[m] = (sem, 16 * n)
        self.q["sp"].ops.append((f, (out, in_), {}, tuple(w), (sem, 16)))

    def emit(self, name, eng):
        seen = {}
        for f, a, kw, waits, inc in self.q[name].ops:
            for key in waits:
                sem, v = self.at[key]
                if seen.get(sem.name, 0) < v:
                    eng.wait_ge(sem, v)
                    seen[sem.name] = v
            if f is None:
                continue
            ins = f(*a, **kw)
            if inc is not None:
                ins.then_inc(*inc)


def build(nc, x, ctx_in, mask, wsq, cols, rows, smalls, consts, wq2, w1a, w2a, w1b, w2b, b1, b2, upw, dnw, out):
    with ExitStack() as es:
        def sb(name, shape, dt=F32):
            return es.enter_context(nc.sbuf_tensor(name, shape, dt))

        def psum(name, n):
            return es.enter_context(nc.psum_tensor(name, [128, n], F32))

        P = Plan(nc, es)
        V, S, G, T = nc.vector, nc.scalar, nc.gpsimd, nc.tensor

        def pe(f, *a, **k):
            P.op("pe", f, *a, **k)

        def act(f, *a, **k):
            P.op("act", f, *a, **k)

        def dve(f, *a, **k):
            P.op("dve", f, *a, **k)

        before = []

        def pool(f, *a, w=(), m=None, **k):
            key = m or f"pool.{len(before)}"
            P.op("pool", f, *a, w=tuple(w) + tuple(before[-1:]), m=key, **k)
            before.append(key)

        def link(eng, prefix, first=()):
            state = [0, list(first)]

            def go(f, *a, w=(), m=None, **k):
                key = m or f"{prefix}.{state[0]}"
                P.op(eng, f, *a, w=tuple(state[1]) + tuple(w), m=key, **k)
                state[0] += 1
                state[1] = [key]
                return key
            return go

        X = sb("X", [128, NT, 128])
        CT = sb("CT", [128, NT * 128])
        W = sb("W", [128, len(SQ), 128])
        C = sb("C", [128, len(COL)])
        R = sb("R", [128, len(ROW), 128])
        M = sb("M", [128, len(SM), 8])
        K = {n: sb("k_" + n, [128, c]) for n, c in CST.items()}
        big1 = sb("big1", [128, 4096])
        big2 = sb("big2", [128, 4096])
        B1 = sb("B1", [128, 8, 4])
        B2 = sb("B2", [8, 128])
        dec = sb("dec", [128, 64])
        ratio = sb("ratio", [128, 4])
        km16t = sb("km16t", [128, 2])
        ny = sb("ny", [128, 8])
        csq = sb("csq", [128, 8])
        wdT = sb("wdT", [128, 128])
        xn = [sb(f"xn{i}", [128, 128]) for i in range(6)]
        xnT = [sb(f"xnT{i}", [128, 128]) for i in range(4)]
        stt_ = [sb(f"st{i}", [128, 6]) for i in range(4)]
        mv = [sb(f"mv{i}", [128, 2]) for i in range(4)]
        rs = [sb(f"rs{i}", [128, 1]) for i in range(4)]
        ve = [sb(f"ve{i}", [128, 1]) for i in range(4)]
        uni = sb("uni", [128, 12288])
        Qx = sb("Qx", [128, 2048])
        bqm = sb("bqm", [128, 4])
        jm2 = sb("jm2", [128, 4])
        Kx = [uni[:, 512 + 512 * i:1024 + 512 * i] for i in range(2)]
        sS = [uni[:, 1536 + 1024 * i:2560 + 1024 * i] for i in range(2)]
        PT = [uni[:, 3584 + 1024 * i:4608 + 1024 * i] for i in range(2)]
        Vb = [sb(f"Vb{i}", [128, 288])[:, :] for i in range(4)]
        O = [uni[:, 6208 + 128 * i:6336 + 128 * i] for i in range(2)]
        OT = [uni[:, 6464 + 128 * i:6592 + 128 * i] for i in range(2)]
        mx = [uni[:, 6720 + 16 * i:6736 + 16 * i] for i in range(2)]
        rd = [uni[:, 6752 + 16 * i:6768 + 16 * i] for i in range(2)]
        U = [uni[:, 6784 + 1024 * i:7808 + 1024 * i] for i in range(2)]
        ab = [uni[:, 8832 + 1024 * i:9856 + 1024 * i] for i in range(2)]
        ty = [uni[:, 10880 + 128 * i:11008 + 128 * i] for i in range(4)]
        hS = [uni[:, 2048 * i:2048 * (i + 1)].rearrange("p (c n) -> p c n", c=4) for i in range(2)]
        bxn = [uni[:, 4096 + 512 * i:4608 + 512 * i].rearrange("p (t d) -> p t d", t=4) for i in range(2)]
        bxT = [uni[:, 5120 + 512 * i:5632 + 512 * i] for i in range(2)]
        bxr = [uni[:, 6144 + 512 * i:6656 + 512 * i].rearrange("p (t d) -> p t d", t=4) for i in range(2)]
        gs = [uni[:, 7168 + 512 * i:7680 + 512 * i] for i in range(2)]
        qv = [uni[:, 8192 + 512 * i:8704 + 512 * i] for i in range(6)]
        rt = [[sb(f"rt{i}_{j}", [128, 64]) for j in range(14)] for i in range(2)]
        gate = [sb(f"gate{i}", [128, 4, 8]) for i in range(2)]
        gT = [sb(f"gT{i}", [8, 512]) for i in range(2)]
        carry = sb("carry", [128, 16])

        b0, b1p, b2p = psum("b0", 512), psum("b1", 512), psum("b2", 512)
        bS = psum("bS", 1024)
        bP = psum("bP", 1024)
        b7 = psum("b7", 512)
        HB = [b2p[:, :], bS[:, 0:512], bS[:, 512:1024], b7[:, :]]
        YB = [bP[:, 0:512], bP[:, 512:1024]]

        ident, ones, tri = K["ident"], K["ones"], K["tri"]

        def w_(n):
            i = SQ.index(n)
            return W[:, i, :]

        def col(n):
            i = COL.index(n)
            return C[:, i:i + 1]

        def row(n):
            return R[:, ROW.index(n), :]

        def sm(n):
            return M[:, SM.index(n), :]

        ld = P.dma_sem("ld")
        ldn = [0]
        loads = [(K[n][:, :], consts[n]) for n in CST] + [
            (W[:, :, :], wsq), (C[:, :], cols), (R[:, :, :], rows), (M[:, :, :], smalls)]
        xv = x.rearrange("b s d -> (b s) d").rearrange("(t p) d -> p t d", p=128)
        cv = ctx_in.rearrange("b s d -> (b s) d").rearrange("(t p) d -> p t d", p=128)
        ov = out.rearrange("b s d -> (b s) d").rearrange("(t p) d -> p t d", p=128)
        mv_ = mask.rearrange("b o q k -> (b o q) k").rearrange("(t p) k -> p t k", p=128)
        for i, (o, s_) in enumerate(loads):
            P.dma(nc.sync.dma_start, o, s_, ld, "ld.const", len(loads))
        ldx = P.dma_sem("ldx")
        cin = big2[:, :].rearrange("p (t d) -> p t d", t=NT)
        for q in range(2):
            P.dma(nc.sync.dma_start, cin[:, 16 * q:16 * q + 16, :], cv[:, 16 * q:16 * q + 16, :], ldx, "ld.ctx", 2)
        ldy = P.dma_sem("ldy")
        P.dma(nc.sync.dma_start, X[:, :, :], xv, ldy, "ld.x", 2)
        P.dma(nc.sync.dma_start, wdT[:, :], wq2, ldy, "ld.x", 2)

        prev = [()]

        def begin(name):
            lasts = []
            for n, q in P.q.items():
                if n != "sp" and q.sem is not None and q.count:
                    key = f"end.{n}.{name}"
                    P.at[key] = (q.sem, q.count)
                    lasts.append(key)
            P.phase(name)
            for n in P.q:
                P.q[n].ops.append((None, (), {}, tuple(lasts), None))
            prev[0] = tuple(lasts)

        def layernorm(k, src, dst, r, w=(), free=()):
            statistics(k, src, r, w, free)
            normalise(k, src, dst, r)

        def statistics(k, src, r, w=(), free=()):
            dve(V.bn_stats, stt_[r][:, :], src, w=tuple(w) + tuple(free), m=f"{k}.st")
            dve(V.bn_aggr, mv[r][:, :], stt_[r][:, :], w=[f"{k}.st"], m=f"{k}.ag")
            dve(V.tensor_scalar, ve[r][:, :], mv[r][:, 1:2], 1e-5, None, ALU.add, w=[f"{k}.ag"], m=f"{k}.ve")
            pool(G.tensor_tensor, rs[r][:, :], ve[r][:, :], sm("nh")[:, 0:1], ALU.pow, w=[f"{k}.ve"], m=f"{k}.rs")

        def normalise(k, src, dst, r):
            dve(V.tensor_scalar, dst, src, mv[r][:, 0:1], rs[r][:, :], ALU.subtract, ALU.mult, w=[f"{k}.rs"], m=f"{k}.xn")

        def quantise(k, src, dst, n, am, w=(), free=()):
            nb = n // 32
            a, b_, c, d, e = (q[:, 0:n] for q in qv[0:5])

            def blk(t):
                return t.rearrange("p (n k) -> p n k", k=32)
            go = link("dve", f"{k}.q", first=tuple(w) + tuple(free))
            scb = am[:, 0:nb].unsqueeze(2).to_broadcast([128, nb, 32])
            go(V.tensor_reduce, am[:, 0:nb], blk(src), AX_X, ALU.max, apply_absolute_value=True)
            go(V.tensor_scalar, am[:, 0:nb], am[:, 0:nb], 1.0 / 7.5, 1e-30, ALU.mult, ALU.max)
            go(V.reciprocal, am[:, 32:32 + nb], am[:, 0:nb])
            go(V.tensor_tensor, blk(a), blk(src), am[:, 32:32 + nb].unsqueeze(2).to_broadcast([128, nb, 32]), ALU.mult)
            go(V.scalar_tensor_tensor, b_, a, -1.0, a, ALU.mult, ALU.max)
            go(V.tensor_scalar, c, b_, 2.0, -4.0, ALU.is_ge, ALU.mult)
            go(V.tensor_scalar, d, b_, 4.0, -2.0, ALU.is_ge, ALU.mult)
            go(V.scalar_tensor_tensor, b_, c, 8.0, d, ALU.add, ALU.add)
            go(V.tensor_tensor, a, a, b_, ALU.mult)
            go(V.tensor_scalar, b_, a, MAGIC, MAGIC, ALU.add, ALU.subtract)
            go(V.tensor_tensor, e, b_, a, ALU.subtract)
            go(V.scalar_tensor_tensor, a, e, 0.5, b_, ALU.is_equal, ALU.subtract)
            go(V.tensor_scalar, c, c, 0.03125, -0.125, ALU.mult, ALU.add)
            go(V.scalar_tensor_tensor, b_, d, 0.125, c, ALU.mult, ALU.add)
            go(V.tensor_tensor, a, a, b_, ALU.mult)
            return go(V.tensor_tensor, blk(dst), blk(a), scb, ALU.mult)

        begin("su")
        su = link("dve", "su.v", first=["ld.const"])
        su(V.tensor_scalar, dec[:, :], K["dist"][:, :], col("td"), -1.0, ALU.mult, ALU.mult)
        su(V.tensor_scalar, bqm[:, :], K["jm"][:, :], col("bq0"), None, ALU.mult)
        su(V.tensor_scalar, jm2[:, :], K["jm"][:, :], 8 ** -0.5, None, ALU.mult)
        su(V.tensor_tensor, csq[:, :], sm("c3"), sm("c3"), ALU.mult, m="su.csq")
        act(S.activation, ratio[:, 0:1], col("gf"), ACT.Exp, scale=-1.0, w=["ld.const"], m="su.e")
        su(V.tensor_scalar, ratio[:, 1:2], ratio[:, 0:1], 1.0, None, ALU.add, w=["su.e"])
        su(V.reciprocal, ratio[:, 2:3], ratio[:, 1:2])
        su(V.tensor_scalar, km16t[:, :], K["km16"][:, :], ratio[:, 2:3], None, ALU.mult)
        wqd = quantise("su.w", wdT[:, :], qv[5][:, 0:128], 128, rt[0][0], w=["ld.x"])
        pe(T.matmul, b7[:, 0:8], ones[:, :], csq[:, :], start=True, stop=True, w=["ld.const", "su.csq"], m="su.ny")
        su(V.tensor_copy, ny[:, :], b7[:, 0:8], w=["su.ny"], m="su.nyc")
        pe(T.transpose, b7[:, 0:128], qv[5][:, 0:128], ident[:, :], w=[wqd, "su.nyc"], m="su.wdT")
        su(V.tensor_copy, wdT[:, :], b7[:, 0:128], w=["su.wdT"])
        banks = [b0[:, :], b1p[:, :], b2p[:, :]]
        for g in range(8):
            bk = banks[g % 3]
            w = ["ld.ctx", "ld.const"] + ([f"su.cc{g - 3}"] if g >= 3 else [])
            for j in range(4):
                pe(T.transpose, bk[:, 128 * j:128 * j + 128], cin[:, 4 * g + j, :], ident[:, :], w=w,
                   m=f"su.ct{g}" if j == 3 else None)
            act(S.activation, CT[:, 512 * g:512 * g + 512], bk, ACT.Copy, w=[f"su.ct{g}"], m=f"su.cc{g}")

        def attention(L, kind):
            begin(L)
            two = kind == 3
            vv = [v.rearrange("p (c b h d) -> p c b h d", c=8, b=2, h=2) if not two else
                  v[:, 0:272].rearrange("p (h b d) -> p h b d", h=8, b=2) for v in Vb]
            for i in range(4):
                if two:
                    pool(G.memset, Vb[i][:, 0:272], 1.0, m=f"{L}.vi{i}")
                else:
                    pool(G.memset, Vb[i], 0.0, m=f"{L}.vz{i}")
                    pool(G.memset, vv[i][0:64, :, :, 0, 8:9], 1.0, w=[f"{L}.vz{i}"], m=f"{L}.vy{i}")
                    pool(G.memset, vv[i][64:128, :, :, 1, 8:9], 1.0, w=[f"{L}.vy{i}"], m=f"{L}.vi{i}")
            if kind == 2:
                ldm = P.dma_sem("ldm")
                P.dma(nc.sync.dma_start, big2[:, 0:2048].rearrange("p (t k) -> p t k", t=NT), mv_, ldm, "ld.mask", 1)
            if kind == 1:
                ldw = P.dma_sem("ldw1")
                P.dma(nc.sync.dma_start, B1[:, :, :], b1, ldw, "ld.b", 2)
                P.dma(nc.sync.dma_start, B2[:, :], b2, ldw, "ld.b", 2)

            def if_(t, key, back=0):
                return [f"{L}.{key}{t - back}"] if t - back >= 0 else []

            def LN(t):
                statistics(f"{L}.ln{t}", X[:, t, :], t % 4, w=["ld.x"] if kind == 0 else (),
                           free=if_(t, "T", 6) + (if_(t, "yb", 6) if kind == 3 else []))

            def LNb(t):
                normalise(f"{L}.ln{t}", X[:, t, :], xn[t % 6][:, :], t % 4)

            def TR(t):
                pe(T.transpose, b0[:, 0:128], xn[t % 6][:, :], ident[:, :],
                   w=[f"{L}.ln{t}.xn"] + if_(t, "Tc", 1) + (if_(t, "OTc", 5) if kind != 1 else []), m=f"{L}.T{t}")
                if kind == 1:
                    for j in range(4):
                        act(S.activation, Qx[:, 512 * (t % 4) + 128 * j:512 * (t % 4) + 128 * j + 128], b0[:, 0:128], ACT.Copy,
                            scale=K["jm"][:, j:j + 1], w=[f"{L}.T{t}"] + if_(t, "SC", 4), m=f"{L}.Tc{t}" if j == 3 else None)
                    return
                act(S.activation, xnT[t % 4][:, :], b0[:, 0:128], ACT.Copy,
                    w=[f"{L}.T{t}"] + if_(t, {0: "QK", 2: "QK", 3: "Q"}[kind], 4), m=f"{L}.Tc{t}")

            def PJ(t):
                ct = CT[:, 128 * t:128 * t + 128]
                xt = xnT[t % 4][:, :]
                if kind in (0, 2):
                    n = f"L{kind}"
                    pe(T.matmul, b1p[:, 0:128], w_(n + "k"), ct, start=True, stop=True, w=if_(t, "QTc", 1))
                    pe(T.matmul, b1p[:, 128:256], w_(n + "q"), xt, start=True, stop=True, w=[f"{L}.Tc{t}"], m=f"{L}.QK{t}")
                elif kind == 3:
                    for i, (a, b) in enumerate((("ka", ct), ("kar", ct), ("kt", ct), ("ktr", ct))):
                        pe(T.matmul, b1p[:, 128 * i:128 * i + 128], w_(a), b, start=True, stop=True,
                           w=if_(t, "rq", 1), m=f"{L}.K{t}" if i == 3 else None)
                wv = {0: "L0v", 2: "L2v"}
                for b in range(2):
                    for h in range(2):
                        rhs = ident[:, :] if kind == 1 else w_(wv[kind]) if kind != 3 else w_(("va", "vt")[h])
                        pe(T.matmul, b2p[64 * h:64 * h + 64, 128 * b:128 * b + 128], ct[:, 64 * b:64 * b + 64], rhs,
                           start=True, stop=True, w=if_(t, "Vc", 1) + (if_(t, "xr", 5) if kind != 1 else []) + (if_(t, "zb", 6) if two else []),
                           m=f"{L}.V{t}" if b == h == 1 else None)
                if kind == 3:
                    for i, (a, b) in enumerate((("qa", xt), ("qar", xt), ("qt", xt), ("qtr", xt))):
                        pe(T.matmul, b1p[:, 128 * i:128 * i + 128], w_(a), b, start=True, stop=True,
                           w=[f"{L}.Tc{t}", f"{L}.rk{t}"], m=f"{L}.Q{t}" if i == 3 else None)
                km = K["km8"][:, :].unsqueeze(2).to_broadcast([128, 4, 128])
                kx = Kx[t % 2].rearrange("p (i k) -> p i k", i=4)
                fr = if_(t, "SC", 2)
                if kind in (0, 2):
                    kin = b1p[:, 0:128].unsqueeze(1).to_broadcast([128, 4, 128])
                    if kind == 0:
                        dve(V.scalar_tensor_tensor, kx, kin, col("bk0"), km, ALU.add, ALU.mult,
                            w=[f"{L}.QK{t}"] + fr, m=f"{L}.Kx{t}")
                    else:
                        dve(V.tensor_tensor, kx, kin, km, ALU.mult, w=[f"{L}.QK{t}"] + fr, m=f"{L}.Kx{t}")
                    for j in range(4):
                        o = Qx[:, 512 * (t % 2) + 128 * j:512 * (t % 2) + 128 * j + 128]
                        act(S.activation, o, b1p[:, 128:256], ACT.Identity,
                            scale=(K["jm"] if kind == 0 else jm2)[:, j:j + 1], bias=bqm[:, j:j + 1] if kind == 0 else 0.0,
                            w=[f"{L}.QK{t}", f"{L}.Kx{t}"] + fr, m=f"{L}.QTc{t}" if j == 3 else None)
                elif kind == 1:
                    dve(V.tensor_tensor, kx, ct.unsqueeze(1).to_broadcast([128, 4, 128]), km, ALU.mult,
                        w=fr, m=f"{L}.Kx{t}")
                else:
                    A = ab[0]
                    for half, nm, src in ((0, "rk", "K"), (1, "rq", "Q")):
                        names = (("ka", "kar", "kt", "ktr"), ("qa", "qar", "qt", "qtr"))[half]
                        base = 512 * half
                        for i, n in enumerate(names):
                            tb = K["cos"] if i % 2 == 0 else K["sin"]
                            dve(V.scalar_tensor_tensor, A[:, base + 128 * i:base + 128 * i + 128],
                                b1p[:, 128 * i:128 * i + 128], col(n), tb[:, :], ALU.add, ALU.mult,
                                w=[f"{L}.{src}{t}"] + if_(t, "ks" if half == 0 else "qs", 1),
                                m=f"{L}.{nm}{t}" if i == 3 else None)
                        a4 = A[:, base:base + 512].rearrange("p (s r n) -> p s r n", s=2, r=2)
                        if half == 0:
                            kt_ = U[t % 2][:, 0:256].rearrange("p (s n) -> p s n", s=2)
                            pool(G.tensor_tensor, kt_, a4[:, :, 0, :], a4[:, :, 1, :], ALU.add,
                                 w=[f"{L}.rk{t}"], m=f"{L}.ks{t}")
                            kk = Kx[t % 2].rearrange("p (s i k) -> p s i k", s=2, i=2)
                            for s in range(2):
                                mk = (K["km16"], km16t)[s][:, :].unsqueeze(2).to_broadcast([128, 2, 128])
                                pool(G.tensor_tensor, kk[:, s], kt_[:, s, :].unsqueeze(1).to_broadcast([128, 2, 128]), mk,
                                     ALU.mult, w=[f"{L}.ks{t}"] + fr, m=f"{L}.Kx{t}" if s == 1 else None)
                        else:
                            qs_ = U[t % 2][:, 256:512]
                            pool(G.tensor_tensor, qs_.rearrange("p (s n) -> p s n", s=2), a4[:, :, 0, :], a4[:, :, 1, :],
                                 ALU.add, w=[f"{L}.rq{t}"] + if_(t, "QTc", 2), m=f"{L}.qs{t}")
                            for s in range(2):
                                for j in range(4):
                                    act(S.activation, Qx[:, 1024 * (t % 2) + 512 * s + 128 * j:1024 * (t % 2) + 512 * s + 128 * j + 128],
                                        qs_[:, 128 * s:128 * s + 128], ACT.Copy, scale=K["jm"][:, j:j + 1],
                                        w=[f"{L}.qs{t}"] + fr, m=f"{L}.QTc{t}" if s == 1 and j == 3 else None)
                vb = vv[t % 4]
                pv = b2p[:, 0:256].rearrange("p (b c h d) -> p c b h d", b=2, c=8, h=2)
                if kind == 3:
                    pv3 = b2p[:, 0:256].rearrange("p (b h d) -> p h b d", b=2, h=8)
                    rb = row("bv3").rearrange("p (h d) -> p h d", h=8)
                    for b in range(2):
                        dve(V.tensor_tensor, vb[:, :, b, 0:16], pv3[:, :, b, :], rb, ALU.add,
                            w=[f"{L}.V{t}", f"{L}.vi{t % 4}"] + if_(t, "AV", 4), m=f"{L}.Vc{t}" if b == 1 else None)
                else:
                    for h in range(2):
                        hp = slice(64 * h, 64 * h + 64)
                        wt = [f"{L}.V{t}", f"{L}.vi{t % 4}"] + if_(t, "AV", 4)
                        mk = f"{L}.Vc{t}" if h == 1 else None
                        if kind == 0:
                            rb = row("bv0").rearrange("p (c h d) -> p c h d", c=8, h=2)[hp, :, h, :]
                            dve(V.tensor_tensor, vb[hp, :, :, h, 0:8], pv[hp, :, :, h, :],
                                rb.unsqueeze(2).to_broadcast([64, 8, 2, 8]), ALU.add, w=wt, m=mk)
                        else:
                            act(S.activation, vb[hp, :, :, h, 0:8], pv[hp, :, :, h, :], ACT.Copy, w=wt, m=mk)

            def SC(t):
                n = {0: 512 * (t % 2), 1: 512 * (t % 4), 2: 512 * (t % 2), 3: 1024 * (t % 2)}[kind]
                q = Qx[:, n:n + (1024 if two else 512)].rearrange("p (s j n) -> p s j n", j=4, n=128)
                wt = [f"{L}.Kx{t}", f"{L}.Tc{t}" if kind == 1 else f"{L}.QTc{t}"] + if_(t, "Se", 1)
                for j in range(4):
                    for b in range(2):
                        tk = slice(64 * b, 64 * b + 64)
                        mk = f"{L}.SC{t}" if b == 1 and j == 3 else None
                        if two:
                            kk = Kx[t % 2].rearrange("p (s i k) -> p s i k", s=2, i=2)
                            o = bS[tk, :].rearrange("p (h s k) -> p h s k", h=8, s=2)
                            for s in range(2):
                                pe(T.matmul, o[:, 2 * j:2 * j + 2, s, :], q[:, s, j, tk], kk[:, s, :, tk],
                                   start=True, stop=True, w=wt, m=mk if s == 1 else None)
                        else:
                            kx = Kx[t % 2].rearrange("p (i k) -> p i k", i=4)
                            pe(T.matmul, bS[tk, 256 * j:256 * j + 256].rearrange("p (i k) -> p i k", i=4),
                               q[:, 0, j, tk], kx[:, :, tk], start=True, stop=True, w=wt, m=mk)
                nh = 8 if two else 16
                s_ = sS[t % 2]
                s3 = s_.rearrange("p (h k) -> p h k", h=nh)
                p3 = bS[:, :].rearrange("p (h k) -> p h k", h=nh)
                m_ = mx[t % 2][:, 0:nh]
                mb = m_.unsqueeze(2).to_broadcast([128, nh, 1024 // nh])
                fr = if_(t, "PT", 2)
                if kind == 0:
                    dve(V.scalar_tensor_tensor, s3, p3, 8 ** -0.5, dec[:, :].unsqueeze(1).to_broadcast([128, 16, 64]),
                        ALU.mult, ALU.add, w=[f"{L}.SC{t}"] + fr, m=f"{L}.Se{t}")
                elif kind == 2:
                    mk = big2[:, 64 * t:64 * t + 64].unsqueeze(1).to_broadcast([128, 16, 64])
                    dve(V.tensor_tensor, s3, p3, mk, ALU.add, w=[f"{L}.SC{t}", "ld.mask"] + fr, m=f"{L}.Se{t}")
                if kind in (0, 2):
                    dve(V.tensor_reduce, m_, s3, AX_X, ALU.max, w=[f"{L}.Se{t}"] + if_(t, "sb", 2), m=f"{L}.mx{t}")
                    pool(G.tensor_tensor, s3, s3, mb, ALU.subtract, w=[f"{L}.mx{t}"], m=f"{L}.sb{t}")
                elif kind == 1:
                    u_ = U[t % 2]
                    dve(V.tensor_tensor, s3, p3, K["causal"][:, :].unsqueeze(1).to_broadcast([128, 16, 64]), ALU.mult,
                        w=[f"{L}.SC{t}"] + fr, m=f"{L}.Se{t}")
                    pool(G.tensor_scalar, u_, s_, 0.0, NEG, ALU.is_equal, ALU.mult, w=[f"{L}.Se{t}"] + if_(t, "ad", 2), m=f"{L}.nz{t}")
                else:
                    dve(V.tensor_reduce, m_, p3, AX_X, ALU.max, w=[f"{L}.SC{t}"] + if_(t, "Se", 2), m=f"{L}.mx{t}")
                    dve(V.tensor_tensor, s3, p3, mb, ALU.subtract, w=[f"{L}.mx{t}"] + fr, m=f"{L}.Se{t}")

            def MX(t):
                if kind != 1:
                    return
                s_ = sS[t % 2]
                s3 = s_.rearrange("p (h k) -> p h k", h=16)
                m_ = mx[t % 2][:, 0:16]
                dve(V.tensor_tensor, s_, s_, U[t % 2], ALU.add, w=[f"{L}.nz{t}"], m=f"{L}.ad{t}")
                dve(V.tensor_reduce, m_, s3, AX_X, ALU.max, w=[f"{L}.ad{t}"] + if_(t, "sb", 2), m=f"{L}.mx{t}")
                pool(G.tensor_tensor, s3, s3, m_.unsqueeze(2).to_broadcast([128, 16, 64]), ALU.subtract,
                     w=[f"{L}.mx{t}"], m=f"{L}.sb{t}")

            def EX(t):
                act(S.activation, sS[t % 2], sS[t % 2], ACT.Exp, scale={0: 1.0, 1: 8 ** -0.5, 2: 1.0, 3: 0.25}[kind],
                    w=[f"{L}.Se{t}" if two else f"{L}.sb{t}"], m=f"{L}.ex{t}")

            def PTr(t):
                for c in range(8):
                    pe(T.transpose, bP[:, 128 * c:128 * c + 128], sS[t % 2][:, 128 * c:128 * c + 128], ident[:, :],
                       w=[f"{L}.ex{t}"] + if_(t, f"Pc{c // 4}.", 1),
                       m={3: f"{L}.PTa{t}", 7: f"{L}.PT{t}"}.get(c))
                for h in range(2):
                    act(S.activation, PT[t % 2][:, 512 * h:512 * h + 512], bP[:, 512 * h:512 * h + 512], ACT.Copy,
                        w=[f"{L}.PTa{t}" if h == 0 else f"{L}.PT{t}"] + if_(t, "AV", 2), m=f"{L}.Pc{h}.{t}")

            def AV(t):
                n = 34 if two else 36
                for c in range(8):
                    pe(T.matmul, b7[:, n * c:n * c + n], PT[t % 2][:, 128 * c:128 * c + 128],
                       Vb[t % 4][:, n * c:n * c + n], start=True, stop=True,
                       w=[f"{L}.Pc0.{t}", f"{L}.Pc1.{t}", f"{L}.Vc{t}"] + if_(t, "On", 1), m=f"{L}.AV{t}" if c == 7 else None)
                for b in range(2):
                    hp = slice(64 * b, 64 * b + 64)
                    if two:
                        av = b7[:, 0:272].rearrange("p (h b d) -> p h b d", h=8, b=2)[hp, :, b, :]
                        o = O[t % 2].rearrange("p (h d) -> p h d", h=8)[hp]
                        r = rd[t % 2][:, 0:8].unsqueeze(2)[hp]
                        sh, D = [64, 8, 16], 16
                    else:
                        av = b7[:, 0:288].rearrange("p (c b h d) -> p c b h d", c=8, b=2, h=2)[hp, :, b, :, :]
                        o = O[t % 2].rearrange("p (c h d) -> p c h d", c=8, h=2)[hp]
                        r = rd[t % 2].rearrange("p (c h d) -> p c h d", c=8, h=2)[hp]
                        sh, D = [64, 8, 2, 8], 8
                    dve(V.reciprocal, r, av[..., D:D + 1], w=[f"{L}.AV{t}"] + if_(t, "On", 2), m=f"{L}.rd{b}.{t}")
                    dve(V.tensor_tensor, o, av[..., 0:D], r.to_broadcast(sh), ALU.mult,
                        w=[f"{L}.rd{b}.{t}"] + if_(t, "xr" if kind == 1 else "OT", 2), m=f"{L}.On{t}" if b == 1 else None)

            def OTr(t):
                if kind == 1:
                    return
                pe(T.transpose, b0[:, 0:128], O[t % 2], ident[:, :],
                   w=[f"{L}.On{t}", f"{L}.Tc{min(t + 4, NT - 1)}"] + if_(t, "OTc", 1) + (if_(t, "Nc", 1) if two else []), m=f"{L}.OT{t}")
                act(S.activation, OT[t % 2], b0[:, 0:128], ACT.Copy, w=[f"{L}.OT{t}"] + if_(t, "Y", 2), m=f"{L}.OTc{t}")

            def Y(t):
                if kind == 1:
                    pool(G.tensor_tensor, X[:, t, :], X[:, t, :], O[t % 2], ALU.add, w=[f"{L}.On{t}", f"{L}.ln{t}.xn"], m=f"{L}.xr{t}")
                    return
                wt = [f"{L}.OTc{t}", f"{L}.Vc{min(t + 4, NT - 1)}"] + if_(t, "xr", 1) + (if_(t, "zb", 1) if two else [])
                pe(T.matmul, b2p[:, 0:128], OT[t % 2], w_({0: "L0o", 2: "L2o", 3: "o3"}[kind]), start=True, stop=True,
                   w=wt, m=f"{L}.Y{t}")
                if kind == 3:
                    y = ty[t % 2]
                    pool(G.tensor_tensor, ty[2 + t % 2], xn[t % 6][:, :], row("bo3"), ALU.add,
                         w=[f"{L}.ln{t}.xn"] + if_(t, "xr", 2), m=f"{L}.yb{t}")
                    dve(V.tensor_tensor, y, b2p[:, 0:128], ty[2 + t % 2], ALU.add,
                        w=[f"{L}.Y{t}", f"{L}.yb{t}"] + if_(t, "xz", 2), m=f"{L}.xr{t}")
                    layernorm(f"{L}.l2{t}", y, y, t % 4, w=[f"{L}.xr{t}"])
                else:
                    if kind == 0:
                        pool(G.tensor_tensor, X[:, t, :], X[:, t, :], row("bo0"), ALU.add,
                             w=[f"{L}.ln{t}.xn"], m=f"{L}.xb{t}")
                    dve(V.tensor_tensor, X[:, t, :], X[:, t, :], b2p[:, 0:128], ALU.add,
                        w=[f"{L}.Y{t}", f"{L}.xb{t}" if kind == 0 else f"{L}.ln{t}.xn"], m=f"{L}.xr{t}")

            def T2(t):
                if kind != 3:
                    return
                pe(T.transpose, b0[:, 0:128], ty[t % 2], ident[:, :],
                   w=[f"{L}.l2{t}.xn", f"{L}.Tc{min(t + 5, NT - 1)}", f"{L}.OTc{t}"], m=f"{L}.N{t}")
                act(S.activation, QTz[t % 2], b0[:, 0:128], ACT.Identity, scale=col("gamma"), bias=col("beta"),
                    w=[f"{L}.N{t}"] + if_(t, "Z", 2), m=f"{L}.Nc{t}")

            def Z(t):
                if kind != 3:
                    return
                pe(T.matmul, b2p[:, 0:128], QTz[t % 2], w_("ffn3"), start=True, stop=True,
                   w=[f"{L}.Nc{t}", f"{L}.Vc{min(t + 5, NT - 1)}", f"{L}.xr{t}"] + if_(t, "zb", 1), m=f"{L}.Z{t}")
                dve(V.tensor_tensor, ty[t % 2], b2p[:, 0:128], row("bffn3"), ALU.add, w=[f"{L}.Z{t}"], m=f"{L}.zb{t}")
                dve(V.scalar_tensor_tensor, X[:, t, :], ty[t % 2], 0.0, X[:, t, :], ALU.max, ALU.add,
                    w=[f"{L}.zb{t}"], m=f"{L}.xz{t}")

            QTz = [uni[:, 11392 + 128 * i:11520 + 128 * i] for i in range(2)]

            def at(f, t):
                if 0 <= t < NT:
                    f(t)
            for t in range(2):
                LN(t)
                LNb(t)
                TR(t)
            PJ(0)
            for s in range(NT + 5):
                at(T2, s - 4)
                at(LN, s + 2)
                at(MX, s - 1)
                at(PTr, s - 2)
                at(PJ, s + 1)
                at(LNb, s + 2)
                at(SC, s)
                at(OTr, s - 3)
                at(EX, s - 1)
                at(Z, s - 4)
                at(AV, s - 2)
                at(Y, s - 3)
                at(TR, s + 2)

        def moe(L, kind, w1, w2):
            begin(L)
            sems = P.dma_sem(f"ld_{L}")
            nf = 4 if kind != 3 else 2
            W1 = big1[:, :].rearrange("p (e f) -> p e f", e=8)
            W2 = big2[:, 0:8 * nf * 128].rearrange("p (e c d) -> p e c d", e=8, c=nf)
            for e in range(8):
                s1 = P.dma_sem(f"ld_{L}_{e}")
                P.dma(nc.sync.dma_start, W1[:, e, :], w1[e], s1, f"{L}.w{e}", 2)
                P.dma(nc.sync.dma_start, W2[:, e], w2[e].rearrange("(c p) d -> p c d", p=128), s1, f"{L}.w{e}", 2)
            dve(V.memset, carry[:, :], 0.0, m=f"{L}.cr-1")
            cap = 1281.0 if kind == 0 else 320.0
            nc_ = 8 if kind == 0 else 16

            def if_(t, key, back=0):
                return [f"{L}.{key}{t - back}"] if t - back >= 0 else []

            def prep(B):
                for j in range(4):
                    t = 4 * B + j
                    layernorm(f"{L}.ln{t}", X[:, t, :], bxn[B % 2][:, j, :], j,
                              free=(if_(B, "xT", 2) if kind != 3 else if_(B, "nx", 2)) + (if_(B, "xa", 2) if kind != 1 else []))
                src = bxn[B % 2]
                if kind == 3:
                    src = bxr[B % 2]
                    r = rt[B % 2]
                    for j in range(4):
                        t = 4 * B + j
                        act(S.activation, gs_j[:, :], bxn[B % 2][:, j, :], ACT.Square, accum_out=r[12][:, j:j + 1],
                            w=[f"{L}.ln{t}.xn"] + if_(B, "ar", 2) + ([f"{L}.sq{t - 1}"] if j else if_(B, "nx", 1)), m=f"{L}.sq{t}")
                    dve(V.tensor_scalar, r[12][:, 4:8], r[12][:, 0:4], 1.0 / 128.0, 1e-6, ALU.mult, ALU.add,
                        w=[f"{L}.sq{4 * B + 3}"], m=f"{L}.r1{B}")
                    pool(G.tensor_tensor, r[12][:, 8:12], r[12][:, 4:8], sm("nh")[:, 0:4], ALU.pow, w=[f"{L}.r1{B}"], m=f"{L}.r2{B}")
                    for j in range(4):
                        t = 4 * B + j
                        dve(V.scalar_tensor_tensor, src[:, j, :], bxn[B % 2][:, j, :], r[12][:, 8 + j:9 + j], row("scale3"),
                            ALU.mult, ALU.mult, w=[f"{L}.r2{B}"] + if_(B, "xT", 2) + if_(B, "nx", 2), m=f"{L}.xs{t}")
                        act(S.activation, gs_j[:, :], src[:, j, :], ACT.Square, accum_out=r[12][:, 12 + j:13 + j],
                            w=[f"{L}.xs{t}", f"{L}.ny{t - 1}" if j else f"{L}.sq{t + 3}"], m=f"{L}.nx{B}" if j == 3 else f"{L}.ny{t}")

            def turn(B):
                src = bxn[B % 2] if kind != 3 else bxr[B % 2]
                for j in range(4):
                    t = 4 * B + j
                    pe(T.transpose, b0[:, 128 * j:128 * j + 128], src[:, j, :], ident[:, :],
                       w=[f"{L}.ln{t}.xn" if kind != 3 else f"{L}.xs{t}"] + if_(B, "xc", 1), m=f"{L}.xT{B}" if j == 3 else None)
                act(S.activation, bxT[B % 2], b0[:, :], ACT.Copy, w=[f"{L}.xT{B}"] + if_(B, "up", 2), m=f"{L}.xc{B}")
                for j in range(4):
                    pe(T.matmul, b1p[:, 8 * j:8 * j + 8], bxT[B % 2][:, 128 * j:128 * j + 128], sm({0: "r0", 1: "r1", 3: "c3"}[kind]),
                       start=True, stop=True, w=[f"{L}.xc{B}"] + if_(B, "b1f", 1), m=f"{L}.lg{B}" if j == 3 else None)
                lg = b1p[:, 0:32].rearrange("p (t e) -> p t e", t=4)
                r = rt[B % 2]

                def v3(i, n=8):
                    return r[i][:, 0:4 * n].rearrange("p (t e) -> p t e", t=4)

                def s1(i):
                    return r[i][:, 0:4].unsqueeze(2)

                def bc(i):
                    return s1(i).to_broadcast([128, 4, 8])
                revi = sm("revi").unsqueeze(1).to_broadcast([128, 4, 8])
                go = link("dve", f"{L}.g{B}", first=[f"{L}.lg{B}"] + if_(B, "ar", 2))
                if kind == 3:
                    nx = r[12][:, 12:16].unsqueeze(2).to_broadcast([128, 4, 8])
                    go(V.tensor_tensor, v3(0), nx, ny[:, :].unsqueeze(1).to_broadcast([128, 4, 8]), ALU.add, w=[f"{L}.nx{B}"])
                    go(V.scalar_tensor_tensor, v3(1), lg, -2.0, v3(0), ALU.mult, ALU.add, m=f"{L}.b1f{B}")
                    go(V.tensor_reduce, s1(2), v3(1), AX_X, ALU.min)
                    go(V.tensor_tensor, v3(3), v3(1), bc(2), ALU.is_equal)
                    go(V.tensor_tensor, v3(3), v3(3), revi, ALU.mult)
                    go(V.tensor_reduce, s1(4), v3(3), AX_X, ALU.max)
                    go(V.tensor_tensor, gate[B % 2][:, :, :], v3(3), bc(4), ALU.is_equal, w=if_(B, "ar", 2), m=f"{L}.gt{B}")
                    return
                if kind == 1:
                    go(V.tensor_tensor, v3(0), lg, sm("gb").unsqueeze(1).to_broadcast([128, 4, 8]), ALU.add)
                else:
                    go(V.tensor_copy, v3(0), lg)
                go(V.tensor_reduce, s1(1), v3(0), AX_X, ALU.max)
                go(V.tensor_tensor, v3(0), v3(0), bc(1), ALU.subtract, m=f"{L}.ls{B}")
                act(S.activation, v3(2), v3(0), ACT.Exp, w=[f"{L}.ls{B}"], m=f"{L}.le{B}")
                go(V.tensor_reduce, s1(3), v3(2), AX_X, ALU.add, w=[f"{L}.le{B}"])
                go(V.reciprocal, s1(13), s1(3))
                go(V.tensor_tensor, v3(4), v3(2), bc(13), ALU.mult)
                oh = v3(8, 16)
                for c in range(2):
                    go(V.tensor_reduce, s1(5 + c), v3(4), AX_X, ALU.max)
                    go(V.tensor_tensor, v3(7), v3(4), bc(5 + c), ALU.is_equal)
                    go(V.tensor_tensor, v3(7), v3(7), revi, ALU.mult)
                    go(V.tensor_reduce, s1(9), v3(7), AX_X, ALU.max)
                    go(V.tensor_tensor, oh[:, :, 8 * c:8 * c + 8], v3(7), bc(9), ALU.is_equal)
                    if c == 0:
                        go(V.scalar_tensor_tensor, v3(4), oh[:, :, 0:8], -2.0, v3(4), ALU.mult, ALU.add)
                if kind == 0:
                    go(V.tensor_tensor, v3(10), oh[:, :, 0:8], oh[:, :, 8:16], ALU.add, m=f"{L}.oh{B}")
                    sel = v3(10)
                else:
                    go(V.tensor_copy, v3(10, 16), oh, m=f"{L}.oh{B}")
                    sel = v3(10, 16)
                go(V.tensor_tensor, v3(11), oh[:, :, 0:8], bc(5), ALU.mult)
                go(V.tensor_tensor, v3(12), oh[:, :, 8:16], bc(6), ALU.mult)
                if kind == 0:
                    go(V.tensor_tensor, s1(13), s1(5), s1(6), ALU.add)
                    go(V.tensor_tensor, v3(11), v3(11), v3(12), ALU.add)
                    go(V.reciprocal, s1(3), s1(13))
                    go(V.tensor_tensor, v3(11), v3(11), bc(3), ALU.mult)
                rk = b1p[:, 0:4 * nc_].rearrange("p (t e) -> p t e", t=4)
                for j in range(4):
                    pe(T.matmul, rk[:, j, :], tri[:, :], sel[:, j, :], start=True, stop=False, w=[f"{L}.oh{B}", f"{L}.cr{B - 1}"])
                    for i in range(j):
                        pe(T.matmul, rk[:, j, :], ones[:, :], sel[:, i, :], start=False, stop=False)
                    pe(T.matmul, rk[:, j, :], ones[:, :], carry[:, 0:nc_], start=False, stop=True,
                       m=f"{L}.rk{B}" if j == 3 else None)
                cs = r[13][:, 16:16 + nc_].unsqueeze(2)
                go(V.tensor_reduce, cs, r[10][:, 0:4 * nc_].rearrange("p (t e) -> p e t", t=4), AX_X, ALU.add)
                go(V.tensor_tensor, carry[:, 0:nc_], carry[:, 0:nc_], r[13][:, 16:16 + nc_], ALU.add,
                   w=[f"{L}.rk{B}"], m=f"{L}.cr{B}")
                fr = if_(B, "ar", 2)
                if kind == 0:
                    go(V.scalar_tensor_tensor, gate[B % 2][:, :, :], rk, cap, v3(11), ALU.is_lt, ALU.mult, w=fr, m=f"{L}.b1f{B}")
                    P.at[f"{L}.gt{B}"] = P.at[f"{L}.b1f{B}"]
                else:
                    go(V.scalar_tensor_tensor, v3(11), rk[:, :, 0:8], cap, v3(11), ALU.is_lt, ALU.mult)
                    go(V.scalar_tensor_tensor, v3(12), rk[:, :, 8:16], cap, v3(12), ALU.is_lt, ALU.mult)
                    go(V.tensor_tensor, gate[B % 2][:, :, :], v3(11), v3(12), ALU.add, w=fr, m=f"{L}.gt{B}")
                    for j in range(4):
                        pe(T.transpose, b1p[0:8, 128 * j:128 * j + 128], gate[B % 2][:, j, :], ident[:, :],
                           w=[f"{L}.gt{B}"], m=f"{L}.gT{B}" if j == 3 else None)
                    act(S.activation, gT[B % 2][:, :], b1p[0:8, :], ACT.Copy, w=[f"{L}.gT{B}"] + if_(B, "bb", 2), m=f"{L}.gc{B}")
                    for j in range(4):
                        pe(T.matmul, b1p[:, 128 * j:128 * j + 128], gT[B % 2][:, 128 * j:128 * j + 128], B2[:, :],
                           start=True, stop=True, w=[f"{L}.gc{B}", "ld.b"], m=f"{L}.bb{B}" if j == 3 else None)
                    for j in range(4):
                        t = 4 * B + j
                        dve(V.tensor_tensor, X[:, t, :], X[:, t, :], b1p[:, 128 * j:128 * j + 128], ALU.add,
                            w=[f"{L}.bb{B}", f"{L}.ln{t}.xn"], m=f"{L}.b1f{B}" if j == 3 else f"{L}.xq{t}")

            hc = [0]
            hfree = {}

            def up(B, e):
                i = 8 * B + e
                xt = bxT[B % 2]
                h = hS[i % 2]
                if kind == 3:
                    for j in range(2):
                        sg, sa = hc[0] % 4, (hc[0] + 1) % 4
                        pe(T.matmul, HB[sg], W1[:, e, 256 + 128 * j:384 + 128 * j], xt, start=True, stop=True,
                           w=[f"{L}.xc{B}", f"{L}.w{e}"] + ([hfree[sg]] if sg in hfree else []), m=f"{L}.ug{i}.{j}")
                        pe(T.matmul, HB[sa], W1[:, e, 128 * j:128 * j + 128], xt, start=True, stop=True,
                           w=([hfree[sa]] if sa in hfree else []), m=f"{L}.ua{i}.{j}")
                        g_ = gs[j]
                        act(S.activation, g_, HB[sg], ACT.Silu, w=[f"{L}.ug{i}.{j}"] + ([f"{L}.hm{i - 1}.{j}"] if i else []),
                            m=f"{L}.hg{i}.{j}")
                        dve(V.tensor_tensor, h[:, j, :], HB[sa], g_, ALU.mult,
                            w=[f"{L}.ua{i}.{j}", f"{L}.hg{i}.{j}"] + if_(i, "dn", 2), m=f"{L}.hm{i}.{j}")
                        hfree[sg] = f"{L}.hg{i}.{j}"
                        hfree[sa] = f"{L}.hm{i}.{j}"
                        hc[0] += 2
                    if e == 7:
                        P.at[f"{L}.up{B}"] = P.at[f"{L}.ua{i}.1"]
                    return
                for j in range(4):
                    sl = hc[0] % 4
                    pe(T.matmul, HB[sl], W1[:, e, 128 * j:128 * j + 128], xt, start=True, stop=True,
                       w=[f"{L}.xc{B}", f"{L}.w{e}"] + ([hfree[sl]] if sl in hfree else []), m=f"{L}.uh{i}.{j}")
                    if kind == 0:
                        act(S.activation, h[:, j, :], HB[sl], ACT.Silu, w=[f"{L}.uh{i}.{j}"] + if_(i, "dn", 2), m=f"{L}.hm{i}.{j}")
                    else:
                        act(S.activation, h[:, j, :], HB[sl], ACT.Relu, bias=B1[:, e, j:j + 1],
                            w=[f"{L}.uh{i}.{j}", "ld.b"] + if_(i, "dn", 2), m=f"{L}.hm{i}.{j}")
                    hfree[sl] = f"{L}.hm{i}.{j}"
                    hc[0] += 1
                if e == 7:
                    P.at[f"{L}.up{B}"] = P.at[f"{L}.uh{i}.3"]

            def down(B, e):
                i = 8 * B + e
                y = YB[i % 2]
                h = hS[i % 2]
                for j in range(4):
                    for c in range(nf):
                        pe(T.matmul, y[:, 128 * j:128 * j + 128], h[:, c, 128 * j:128 * j + 128], W2[:, e, c, :],
                           start=c == 0, stop=c == nf - 1, w=[f"{L}.hm{i}.{nf - 1}"] + if_(i, "ac", 2),
                           m=f"{L}.dn{i}" if j == 3 and c == nf - 1 else None)
                for j in range(4):
                    t = 4 * B + j
                    last = e == 7 and j == 3
                    dve(V.scalar_tensor_tensor, X[:, t, :], y[:, 128 * j:128 * j + 128], gate[B % 2][:, j, e:e + 1], X[:, t, :],
                        ALU.mult, ALU.add, w=[f"{L}.dn{i}", f"{L}.gt{B}"] + ([f"{L}.aj{i - 1}.{j}"] if e else [f"{L}.ln{t}.xn"])
                        + ([f"{L}.b1f{B}"] if kind == 1 and e == 0 else []),
                        m=f"{L}.aj{i}.{j}")
                P.at[f"{L}.ac{i}"] = P.at[f"{L}.aj{i}.3"]
                if e == 7:
                    P.at[f"{L}.ar{B}"] = P.at[f"{L}.aj{i}.3"]
                    if kind != 1:
                        pool(G.tensor_tensor, X[:, 4 * B:4 * B + 4, :], X[:, 4 * B:4 * B + 4, :], bxn[B % 2], ALU.add,
                             w=[f"{L}.aj{i}.3"], m=f"{L}.xa{B}")
                    if kind == 3:
                        P.dma(nc.sync.dma_start, ov[:, 4 * B:4 * B + 4, :], X[:, 4 * B:4 * B + 4, :], so, "out", 8, w=[f"{L}.xa{B}"])

            gs_j = sb(f"{L}_junk", [128, 128])
            if kind == 3:
                so = P.dma_sem("so")
            prep(0)
            turn(0)
            up(0, 0)
            for B in range(NBK):
                for e in range(8):
                    if e < 7:
                        up(B, e + 1)
                    elif B + 1 < NBK:
                        up(B + 1, 0)
                    down(B, e)
                    if e == 1 and B + 1 < NBK:
                        prep(B + 1)
                    if e == 3 and B + 1 < NBK:
                        turn(B + 1)

        def qlin(L):
            begin(L)

            def if_(t, key, back=0):
                return [f"{L}.{key}{t - back}"] if t - back >= 0 else []

            def first(B):
                for j in range(4):
                    t = 4 * B + j
                    layernorm(f"{L}.ln{t}", X[:, t, :], bxn[B % 2][:, j, :], j)
                flat = bxn[B % 2].rearrange("p t d -> p (t d)")
                key = quantise(f"{L}.{B}", flat, bxr[B % 2].rearrange("p t d -> p (t d)"), 512, rt[0][0],
                               w=[f"{L}.ln{4 * B + 3}.xn"] + if_(B, "xT", 2))
                P.at[f"{L}.qd{B}"] = P.at[key]

            def second(B):
                for j in range(4):
                    pe(T.transpose, b0[:, 128 * j:128 * j + 128], bxr[B % 2][:, j, :], ident[:, :],
                       w=[f"{L}.qd{B}"] + if_(B, "xc", 1), m=f"{L}.xT{B}" if j == 3 else None)
                act(S.activation, bxT[B % 2], b0[:, :], ACT.Copy, w=[f"{L}.xT{B}"] + if_(B, "Y", 2), m=f"{L}.xc{B}")
                for j in range(4):
                    pe(T.matmul, b1p[:, 128 * j:128 * j + 128], bxT[B % 2][:, 128 * j:128 * j + 128], wdT[:, :],
                       start=True, stop=True, w=[f"{L}.xc{B}"] + if_(B, "xr", 1), m=f"{L}.Y{B}" if j == 3 else None)
                xb = X[:, 4 * B:4 * B + 4, :]
                pool(G.tensor_tensor, xb, xb, row("b2ffn").unsqueeze(1).to_broadcast([128, 4, 128]), ALU.add,
                     w=[f"{L}.ln{4 * B + 3}.xn"], m=f"{L}.xb{B}")
                dve(V.tensor_tensor, xb.rearrange("p t d -> p (t d)"), xb.rearrange("p t d -> p (t d)"), b1p[:, :], ALU.add,
                    w=[f"{L}.Y{B}", f"{L}.xb{B}"], m=f"{L}.xr{B}")
            for B in range(NBK + 1):
                if B < NBK:
                    first(B)
                if B:
                    second(B - 1)

        attention("A0", 0)
        moe("F0", 0, w1a, w2a)
        attention("A1", 1)
        moe("F1", 1, w1b, w2b)
        attention("A2", 2)
        qlin("F2")
        attention("A3", 3)
        moe("F3", 3, upw, dnw)
        P.q["sp"].ops.append((None, (), {}, ("out",), None))

        block = es.enter_context(nc.Block())

        @block.sync
        def _(e):
            P.emit("sp", e)

        @block.gpsimd
        def _(e):
            P.emit("pool", e)

        @block.scalar
        def _(e):
            P.emit("act", e)

        @block.vector
        def _(e):
            P.emit("dve", e)

        @block.tensor
        def _(e):
            P.emit("pe", e)


def kernel(**inp):
    import numpy as np
    import concourse.bacc as bacc
    from concourse.bass_utils import run_bass_kernel_spmd as run

    a = {k: np.asarray(v) for k, v in inp.items()}
    f = np.float32
    swap = np.arange(128).reshape(64, 2)[:, ::-1].reshape(128)

    def l3(n):
        return a["L3_xattn_" + n][3]
    sq = {
        "L0q": a["L0_xattn_wq"].T, "L0k": a["L0_xattn_wk"].T, "L0v": a["L0_xattn_wv"].T, "L0o": a["L0_xattn_wo"].T,
        "L2q": a["L2_xattn_wq"].reshape(128, 128), "L2k": a["L2_xattn_wk"].reshape(128, 128),
        "L2v": a["L2_xattn_wv"].reshape(128, 128), "L2o": a["L2_xattn_wo"].reshape(128, 128),
        "va": l3("W_va").T, "vt": l3("W_vt").T, "o3": l3("W_o").T, "ffn3": l3("W_ffn").T,
    }
    cl = {"bq0": a["L0_xattn_bq"], "bk0": a["L0_xattn_bk"], "gamma": l3("gamma"), "beta": l3("beta"),
          "gf": np.broadcast_to(l3("gating_factor"), (128,)), "td": np.broadcast_to(a["L0_xattn_time_decay"], (128,))}
    for n in ("qa", "ka", "qt", "kt"):
        sq[n] = l3("W_" + n).T
        sq[n + "r"] = l3("W_" + n)[swap].T
        cl[n] = l3("b_" + n)
        cl[n + "r"] = l3("b_" + n)[swap]
    wide = np.broadcast_to
    rw = {"bv0": wide(a["L0_xattn_bv"], (128, 128)), "bo0": wide(a["L0_xattn_bo"], (128, 128)),
          "bv3": np.concatenate([wide(l3("b_va"), (64, 128)), wide(l3("b_vt"), (64, 128))]),
          "bo3": wide(l3("b_o"), (128, 128)), "bffn3": wide(l3("b_ffn"), (128, 128)),
          "b2ffn": wide(a["L2_ffn_bias"], (128, 128)), "scale3": wide(a["L3_ffn_scale"], (128, 128))}
    sml = {"r0": a["L0_ffn_router_w"].T, "r1": a["L1_ffn_gate_w"].T, "c3": a["L3_ffn_centroids"].T,
           "gb": wide(a["L1_ffn_gate_b"], (128, 8)), "revi": wide(np.arange(8, 0, -1).astype(f), (128, 8)),
           "nh": np.full((128, 8), -0.5, f)}
    p = np.arange(128)
    inv = (1.0 / 10000.0 ** (np.arange(0, 16, 2, dtype=f) / f(16))).astype(f)
    fr = (np.arange(64, dtype=f)[:, None] * inv[None, :]).astype(f)
    ang = fr[p % 64][:, (p % 16) % 8].T
    sign = np.where(p % 2 == 0, -1.0, 1.0).astype(f)[:, None]
    cst = {
        "ident": np.eye(128, dtype=f), "ones": np.ones((128, 128), f),
        "tri": (p[:, None] < p[None, :]).astype(f), "cos": np.cos(ang), "sin": np.sin(ang) * sign,
        "dist": np.abs((p % 64)[:, None] - np.arange(64)[None, :]).astype(f),
        "causal": (np.arange(64)[None, :] <= (p % 64)[:, None]).astype(f),
        "km8": ((p % 32)[:, None] // 8 == np.arange(4)[None, :]).astype(f),
        "jm": (p[:, None] // 32 == np.arange(4)[None, :]).astype(f),
        "km16": ((p % 32)[:, None] // 16 == np.arange(2)[None, :]).astype(f),
    }
    arrays = {
        "x": a["x"], "ctx": a["ctx_1024"], "mask": a["mask_Bx1xSxS2_ff0"],
        "wsq": np.stack([sq[n] for n in SQ], 1), "cols": np.stack([cl[n] for n in COL], 1),
        "rows": np.stack([rw[n] for n in ROW], 1), "smalls": np.stack([sml[n] for n in SM], 1),
        "wq2": a["L2_ffn_weight"], "w1a": a["L0_ffn_w1"], "w2a": a["L0_ffn_w2"], "w1b": a["L1_ffn_W1"],
        "w2b": a["L1_ffn_W2"], "b1": a["L1_ffn_b1"].reshape(8, 4, 128).transpose(2, 0, 1), "b2": a["L1_ffn_b2"],
        "upw": a["L3_ffn_up_w"], "dnw": a["L3_ffn_down_w"],
    }
    for n in CST:
        arrays["c_" + n] = cst[n]
    arrays = {k: np.ascontiguousarray(v) for k, v in arrays.items()}
    nc = bacc.Bacc("TRN2", target_bir_lowering=False, num_devices=1)
    d = {k: nc.dram_tensor(k + "_dram", v.shape, mybir.dt.from_np(v.dtype), kind="ExternalInput").ap()
         for k, v in arrays.items()}
    out = nc.dram_tensor("out_dram", (64, 64, 128), F32, kind="ExternalOutput").ap()
    build(nc, d["x"], d["ctx"], d["mask"], d["wsq"], d["cols"], d["rows"], d["smalls"], {n: d["c_" + n] for n in CST},
          d["wq2"], d["w1a"], d["w2a"], d["w1b"], d["w2b"], d["b1"], d["b2"], d["upw"], d["dnw"], out)
    r = run(nc, [{k + "_dram": v for k, v in arrays.items()}], core_ids=[0])
    return r.results[0]["out_dram"]
```

```python
from contextlib import ExitStack

import concourse.bass as bass
from concourse import mybir

ALU = mybir.AluOpType
ACT = mybir.ActivationFunctionType
F32 = mybir.dt.float32
AX_X = mybir.AxisListType.X

NT = 32
NBK = 8
NEG = -1000000000.0
MAGIC = 12582912.0

SQ = ["L0q", "L0k", "L0v", "L0o", "L2q", "L2k", "L2v", "L2o", "qa", "qar", "ka", "kar", "qt", "qtr", "kt", "ktr",
      "va", "vt", "o3", "ffn3"]
COL = ["bq0", "bk0", "qa", "qar", "ka", "kar", "qt", "qtr", "kt", "ktr", "gamma", "beta", "gf", "td"]
ROW = ["bv0", "bo0", "bv3", "bo3", "bffn3", "b2ffn", "scale3"]
SM = ["r0", "r1", "c3", "gb", "revi", "nh"]
CST = {"ident": 128, "ones": 128, "tri": 128, "cos": 128, "sin": 128, "dist": 64, "causal": 64, "km8": 4, "km16": 2, "jm": 4, "DS": 128, "DG": 1, "e0": 16, "e1": 16}


class Queue:

    def __init__(self, name):
        self.name = name
        self.ops = []
        self.sem = None
        self.count = 0


class Plan:

    def __init__(self, nc, ctx):
        self.nc = nc
        self.ctx = ctx
        self.q = {n: Queue(n) for n in ("pe", "act", "dve", "pool", "sp")}
        self.at = {}

    def phase(self, name):
        for n, q in self.q.items():
            if n != "sp":
                q.sem = self.ctx.enter_context(self.nc.semaphore(f"{name}_{n}"))
                q.count = 0

    def dma_sem(self, name):
        return self.ctx.enter_context(self.nc.semaphore(name))

    def op(self, eng, f, *a, w=(), m=None, **kw):
        q = self.q[eng]
        inc = None
        if m is not None:
            assert m not in self.at, m
            q.count += 1
            inc = (q.sem, 1)
            self.at[m] = (q.sem, q.count)
        q.ops.append((f, a, kw, tuple(w), inc))

    def dma(self, f, out, in_, sem, m, n, w=()):
        self.at[m] = (sem, 16 * n)
        self.q["sp"].ops.append((f, (out, in_), {}, tuple(w), (sem, 16)))

    def emit(self, name, eng):
        seen = {}
        for f, a, kw, waits, inc in self.q[name].ops:
            for key in waits:
                sem, v = self.at[key]
                if seen.get(sem.name, 0) < v:
                    eng.wait_ge(sem, v)
                    seen[sem.name] = v
            if f is None:
                continue
            ins = f(*a, **kw)
            if inc is not None:
                ins.then_inc(*inc)


def build(nc, x, ctx_in, mask, wsq, cols, rows, smalls, consts, wq2, w1a, w2a, w1b, w2b, b1, b2, upw, dnw, out):
    with ExitStack() as es:
        def sb(name, shape, dt=F32):
            return es.enter_context(nc.sbuf_tensor(name, shape, dt))

        def psum(name, n):
            return es.enter_context(nc.psum_tensor(name, [128, n], F32))

        P = Plan(nc, es)
        V, S, G, T = nc.vector, nc.scalar, nc.gpsimd, nc.tensor

        def pe(f, *a, **k):
            P.op("pe", f, *a, **k)

        def act(f, *a, **k):
            P.op("act", f, *a, **k)

        def dve(f, *a, **k):
            P.op("dve", f, *a, **k)

        before = []

        def pool(f, *a, w=(), m=None, **k):
            key = m or f"pool.{len(before)}"
            P.op("pool", f, *a, w=tuple(w) + tuple(before[-1:]), m=key, **k)
            before.append(key)

        def link(eng, prefix, first=()):
            state = [0, list(first)]

            def go(f, *a, w=(), m=None, **k):
                key = m or f"{prefix}.{state[0]}"
                P.op(eng, f, *a, w=tuple(state[1]) + tuple(w), m=key, **k)
                state[0] += 1
                state[1] = [key]
                return key
            return go

        X = sb("X", [128, NT, 128])
        CT = sb("CT", [128, NT * 128])
        W = sb("W", [128, len(SQ), 128])
        C = sb("C", [128, len(COL)])
        R = sb("R", [128, len(ROW), 128])
        M = sb("M", [128, len(SM), 8])
        K = {n: sb("k_" + n, [128, c]) for n, c in CST.items()}
        big1 = sb("big1", [128, 4096])
        big2 = sb("big2", [128, 4096])
        B1 = sb("B1", [128, 8, 4])
        B2 = sb("B2", [8, 128])
        dec = sb("dec", [128, 64])
        ratio = sb("ratio", [128, 4])
        km16t = sb("km16t", [128, 2])
        ny = sb("ny", [128, 8])
        csq = sb("csq", [128, 8])
        wdT = sb("wdT", [128, 128])
        xn = [sb(f"xn{i}", [128, 128]) for i in range(6)]
        xnT = [sb(f"xnT{i}", [128, 128]) for i in range(4)]
        stt_ = [sb(f"st{i}", [128, 6]) for i in range(6)]
        mv = [sb(f"mv{i}", [128, 2]) for i in range(6)]
        rs = [sb(f"rs{i}", [128, 1]) for i in range(6)]
        ve = [sb(f"ve{i}", [128, 1]) for i in range(6)]
        uni = sb("uni", [128, 12288])
        Qx = sb("Qx", [128, 2048])
        bqm = sb("bqm", [128, 4])
        jm2 = sb("jm2", [128, 4])
        Kx = [uni[:, 512 + 512 * i:1024 + 512 * i] for i in range(2)]
        sS = [uni[:, 1536 + 1024 * i:2560 + 1024 * i] for i in range(2)]
        PT = [uni[:, 3584 + 1024 * i:4608 + 1024 * i] for i in range(2)]
        Vb = [sb(f"Vb{i}", [128, 288])[:, :] for i in range(4)]
        O = [uni[:, 6208 + 128 * i:6336 + 128 * i] for i in range(2)]
        OT = [uni[:, 6464 + 128 * i:6592 + 128 * i] for i in range(2)]
        mx = [uni[:, 6720 + 16 * i:6736 + 16 * i] for i in range(2)]
        rd = [uni[:, 6752 + 16 * i:6768 + 16 * i] for i in range(2)]
        U = [uni[:, 6784 + 1024 * i:7808 + 1024 * i] for i in range(2)]
        ab = [uni[:, 8832 + 1024 * i:9856 + 1024 * i] for i in range(2)]
        ty = [uni[:, 10880 + 128 * i:11008 + 128 * i] for i in range(4)]
        hS = [uni[:, 2048 * i:2048 * (i + 1)].rearrange("p (c n) -> p c n", c=4) for i in range(2)]
        bxn = [uni[:, 4096 + 512 * i:4608 + 512 * i].rearrange("p (t d) -> p t d", t=4) for i in range(2)]
        bxT = [uni[:, 5120 + 512 * i:5632 + 512 * i] for i in range(2)]
        bxr = [uni[:, 6144 + 512 * i:6656 + 512 * i].rearrange("p (t d) -> p t d", t=4) for i in range(2)]
        gs = [uni[:, 7168 + 512 * i:7680 + 512 * i] for i in range(2)]
        qv = [uni[:, 8192 + 512 * i:8704 + 512 * i] for i in range(6)]
        rt = [[sb(f"rt{i}_{j}", [128, 64]) for j in range(14)] for i in range(2)]
        gate = [sb(f"gate{i}", [128, 4, 8]) for i in range(2)]
        gT = [sb(f"gT{i}", [8, 512]) for i in range(2)]
        carry = sb("carry", [128, 16])

        SP = {}
        for L, n in (("F0", 11), ("F1", 5)):
            SP[L] = (nc.dram_tensor(f"{L}_xbuf", (8 * n * 128 + 8192, 128), F32).ap(),
                     nc.dram_tensor(f"{L}_ybuf", (8 * n * 128 + 128, 128), F32).ap())
        idxS = sb("idxS", [128, NT, 2], mybir.dt.uint32)
        idxG = sb("idxG", [128, NT, 2], mybir.dt.uint32)
        mvb = [sb(f"mvb{i}", [128, 16]) for i in range(2)]
        gb = [sb(f"gb{i}", [128, 128]) for i in range(8)]
        gates = sb("gates", [128, NT, 2])
        b2r = sb("b2r", [128, 8, 128])
        zero = sb("zero", [128, 1024])
        b0, b1p, b2p = psum("b0", 512), psum("b1", 512), psum("b2", 512)
        bS = psum("bS", 1024)
        bP = psum("bP", 1024)
        b7 = psum("b7", 512)
        HB = [b2p[:, :], bS[:, 0:512], bS[:, 512:1024], b7[:, :]]
        YB = [bP[:, 0:512], bP[:, 512:1024]]

        ident, ones, tri = K["ident"], K["ones"], K["tri"]

        def w_(n):
            i = SQ.index(n)
            return W[:, i, :]

        def col(n):
            i = COL.index(n)
            return C[:, i:i + 1]

        def row(n):
            return R[:, ROW.index(n), :]

        def sm(n):
            return M[:, SM.index(n), :]

        ld = P.dma_sem("ld")
        ldn = [0]
        loads = [(K[n][:, :], consts[n]) for n in CST] + [
            (W[:, :, :], wsq), (C[:, :], cols), (R[:, :, :], rows), (M[:, :, :], smalls)]
        xv = x.rearrange("b s d -> (b s) d").rearrange("(t p) d -> p t d", p=128)
        cv = ctx_in.rearrange("b s d -> (b s) d").rearrange("(t p) d -> p t d", p=128)
        ov = out.rearrange("b s d -> (b s) d").rearrange("(t p) d -> p t d", p=128)
        mv_ = mask.rearrange("b o q k -> (b o q) k").rearrange("(t p) k -> p t k", p=128)
        for i, (o, s_) in enumerate(loads):
            P.dma(nc.sync.dma_start, o, s_, ld, "ld.const", len(loads))
        ldx = P.dma_sem("ldx")
        cin = big2[:, :].rearrange("p (t d) -> p t d", t=NT)
        for q in range(2):
            P.dma(nc.sync.dma_start, cin[:, 16 * q:16 * q + 16, :], cv[:, 16 * q:16 * q + 16, :], ldx, "ld.ctx", 2)
        ldy = P.dma_sem("ldy")
        P.dma(nc.sync.dma_start, X[:, :, :], xv, ldy, "ld.x", 2)
        P.dma(nc.sync.dma_start, wdT[:, :], wq2, ldy, "ld.x", 2)

        prev = [()]

        def begin(name):
            lasts = []
            for n, q in P.q.items():
                if n != "sp" and q.sem is not None and q.count:
                    key = f"end.{n}.{name}"
                    P.at[key] = (q.sem, q.count)
                    lasts.append(key)
            P.phase(name)
            for n in P.q:
                P.q[n].ops.append((None, (), {}, tuple(lasts), None))
            prev[0] = tuple(lasts)

        def layernorm(k, src, dst, r, w=(), free=()):
            statistics(k, src, r, w, free)
            normalise(k, src, dst, r)

        def statistics(k, src, r, w=(), free=()):
            dve(V.bn_stats, stt_[r][:, :], src, w=tuple(w) + tuple(free), m=f"{k}.st")
            dve(V.bn_aggr, mv[r][:, :], stt_[r][:, :], w=[f"{k}.st"], m=f"{k}.ag")
            dve(V.tensor_scalar, ve[r][:, :], mv[r][:, 1:2], 1e-5, None, ALU.add, w=[f"{k}.ag"], m=f"{k}.ve")
            pool(G.tensor_tensor, rs[r][:, :], ve[r][:, :], sm("nh")[:, 0:1], ALU.pow, w=[f"{k}.ve"], m=f"{k}.rs")

        def normalise(k, src, dst, r, free=()):
            dve(V.tensor_scalar, dst, src, mv[r][:, 0:1], rs[r][:, :], ALU.subtract, ALU.mult, w=[f"{k}.rs"] + list(free),
                m=f"{k}.xn")

        def quantise(k, src, dst, n, am, w=(), free=()):
            nb = n // 32
            a, b_, c, d, e = (q[:, 0:n] for q in qv[0:5])

            def blk(t):
                return t.rearrange("p (n k) -> p n k", k=32)
            go = link("dve", f"{k}.q", first=tuple(w) + tuple(free))
            scb = am[:, 0:nb].unsqueeze(2).to_broadcast([128, nb, 32])
            go(V.tensor_reduce, am[:, 0:nb], blk(src), AX_X, ALU.max, apply_absolute_value=True)
            go(V.tensor_scalar, am[:, 0:nb], am[:, 0:nb], 1.0 / 7.5, 1e-30, ALU.mult, ALU.max)
            go(V.reciprocal, am[:, 32:32 + nb], am[:, 0:nb])
            go(V.tensor_tensor, blk(a), blk(src), am[:, 32:32 + nb].unsqueeze(2).to_broadcast([128, nb, 32]), ALU.mult)
            go(V.scalar_tensor_tensor, b_, a, -1.0, a, ALU.mult, ALU.max)
            go(V.tensor_scalar, c, b_, 2.0, -4.0, ALU.is_ge, ALU.mult)
            go(V.tensor_scalar, d, b_, 4.0, -2.0, ALU.is_ge, ALU.mult)
            go(V.scalar_tensor_tensor, b_, c, 8.0, d, ALU.add, ALU.add)
            go(V.tensor_tensor, a, a, b_, ALU.mult)
            go(V.tensor_scalar, b_, a, MAGIC, MAGIC, ALU.add, ALU.subtract)
            go(V.tensor_tensor, e, b_, a, ALU.subtract)
            go(V.scalar_tensor_tensor, a, e, 0.5, b_, ALU.is_equal, ALU.subtract)
            go(V.tensor_scalar, c, c, 0.03125, -0.125, ALU.mult, ALU.add)
            go(V.scalar_tensor_tensor, b_, d, 0.125, c, ALU.mult, ALU.add)
            go(V.tensor_tensor, a, a, b_, ALU.mult)
            return go(V.tensor_tensor, blk(dst), blk(a), scb, ALU.mult)

        begin("su")
        su = link("dve", "su.v", first=["ld.const"])
        su(V.tensor_scalar, dec[:, :], K["dist"][:, :], col("td"), -1.0, ALU.mult, ALU.mult)
        su(V.tensor_scalar, bqm[:, :], K["jm"][:, :], col("bq0"), None, ALU.mult)
        su(V.tensor_scalar, jm2[:, :], K["jm"][:, :], 8 ** -0.5, None, ALU.mult)
        su(V.tensor_tensor, csq[:, :], sm("c3"), sm("c3"), ALU.mult, m="su.csq")
        act(S.activation, ratio[:, 0:1], col("gf"), ACT.Exp, scale=-1.0, w=["ld.const"], m="su.e")
        su(V.tensor_scalar, ratio[:, 1:2], ratio[:, 0:1], 1.0, None, ALU.add, w=["su.e"])
        su(V.reciprocal, ratio[:, 2:3], ratio[:, 1:2])
        su(V.tensor_scalar, km16t[:, :], K["km16"][:, :], ratio[:, 2:3], None, ALU.mult)
        wqd = quantise("su.w", wdT[:, :], qv[5][:, 0:128], 128, rt[0][0], w=["ld.x"])
        pe(T.matmul, b7[:, 0:8], ones[:, :], csq[:, :], start=True, stop=True, w=["ld.const", "su.csq"], m="su.ny")
        su(V.tensor_copy, ny[:, :], b7[:, 0:8], w=["su.ny"], m="su.nyc")
        pe(T.transpose, b7[:, 0:128], qv[5][:, 0:128], ident[:, :], w=[wqd, "su.nyc"], m="su.wdT")
        su(V.tensor_copy, wdT[:, :], b7[:, 0:128], w=["su.wdT"])
        zs = P.dma_sem("zero")
        dve(V.memset, zero[:, :], 0.0, m="su.zero")
        for L, n in (("F0", 11), ("F1", 5)):
            P.dma(nc.sync.dma_start, SP[L][0][0:1024 * n, :].rearrange("(p r c) d -> p r (c d)", p=128, c=8),
                  zero[:, :].unsqueeze(1).to_broadcast([128, n, 1024]), zs, "zeroed", 4, w=["su.zero"])
            P.dma(nc.sync.dma_start, SP[L][1][1024 * n:1024 * n + 128, :], zero[:, 0:128], zs, "zeroed", 4, w=["su.zero"])
        banks = [b0[:, :], b1p[:, :], b2p[:, :]]
        for g in range(8):
            bk = banks[g % 3]
            w = ["ld.ctx", "ld.const"] + ([f"su.cc{g - 3}"] if g >= 3 else [])
            for j in range(4):
                pe(T.transpose, bk[:, 128 * j:128 * j + 128], cin[:, 4 * g + j, :], ident[:, :], w=w,
                   m=f"su.ct{g}" if j == 3 else None)
            act(S.activation, CT[:, 512 * g:512 * g + 512], bk, ACT.Copy, w=[f"su.ct{g}"], m=f"su.cc{g}")

        def attention(L, kind, pending=None):
            begin(L)
            two = kind == 3
            vv = [v.rearrange("p (c b h d) -> p c b h d", c=8, b=2, h=2) if not two else
                  v[:, 0:272].rearrange("p (h b d) -> p h b d", h=8, b=2) for v in Vb]
            for i in range(4):
                if two:
                    pool(G.memset, Vb[i][:, 0:272], 1.0, m=f"{L}.vi{i}")
                else:
                    pool(G.memset, Vb[i], 0.0, m=f"{L}.vz{i}")
                    pool(G.memset, vv[i][0:64, :, :, 0, 8:9], 1.0, w=[f"{L}.vz{i}"], m=f"{L}.vy{i}")
                    pool(G.memset, vv[i][64:128, :, :, 1, 8:9], 1.0, w=[f"{L}.vy{i}"], m=f"{L}.vi{i}")
            if kind == 2:
                ldm = P.dma_sem("ldm")
                P.dma(nc.sync.dma_start, big2[:, 0:2048].rearrange("p (t k) -> p t k", t=NT), mv_, ldm, "ld.mask", 1)
            if kind == 1:
                ldw = P.dma_sem("ldw1")
                P.dma(nc.sync.dma_start, B1[:, :, :], b1, ldw, "ld.b", 2)
                P.dma(nc.sync.dma_start, b2r[:, :, :], b2.unsqueeze(0).to_broadcast([128, 8, 128]), ldw, "ld.b", 2)

            def if_(t, key, back=0):
                return [f"{L}.{key}{t - back}"] if t - back >= 0 else []

            def LN(t):
                w = []
                if pending:
                    pending[2](t)
                    w = [f"{pending[0]}.cb{2 * t + 1}"]
                statistics(f"{L}.ln{t}", X[:, t, :], t % 4, w=w + (["ld.x"] if kind == 0 else []))

            def LNb(t):
                normalise(f"{L}.ln{t}", X[:, t, :], xn[t % 6][:, :], t % 4,
                          free=if_(t, "T", 6) + (if_(t, "yb", 6) if kind == 3 else []))

            def TR(t):
                pe(T.transpose, b0[:, 0:128], xn[t % 6][:, :], ident[:, :],
                   w=[f"{L}.ln{t}.xn"] + if_(t, "Tc", 1) + (if_(t, "OTc", 5) if kind != 1 else []), m=f"{L}.T{t}")
                if kind == 1:
                    for j in range(4):
                        act(S.activation, Qx[:, 512 * (t % 4) + 128 * j:512 * (t % 4) + 128 * j + 128], b0[:, 0:128], ACT.Copy,
                            scale=K["jm"][:, j:j + 1], w=[f"{L}.T{t}"] + if_(t, "SC", 4), m=f"{L}.Tc{t}" if j == 3 else None)
                    return
                act(S.activation, xnT[t % 4][:, :], b0[:, 0:128], ACT.Copy,
                    w=[f"{L}.T{t}"] + if_(t, {0: "QK", 2: "QK", 3: "Q"}[kind], 4), m=f"{L}.Tc{t}")

            def PJ(t):
                ct = CT[:, 128 * t:128 * t + 128]
                xt = xnT[t % 4][:, :]
                if kind in (0, 2):
                    n = f"L{kind}"
                    pe(T.matmul, b1p[:, 0:128], w_(n + "k"), ct, start=True, stop=True, w=if_(t, "QTc", 1))
                    pe(T.matmul, b1p[:, 128:256], w_(n + "q"), xt, start=True, stop=True, w=[f"{L}.Tc{t}"], m=f"{L}.QK{t}")
                elif kind == 3:
                    for i, (a, b) in enumerate((("ka", ct), ("kar", ct), ("kt", ct), ("ktr", ct))):
                        pe(T.matmul, b1p[:, 128 * i:128 * i + 128], w_(a), b, start=True, stop=True,
                           w=if_(t, "rq", 1), m=f"{L}.K{t}" if i == 3 else None)
                wv = {0: "L0v", 2: "L2v"}
                for b in range(2):
                    for h in range(2):
                        rhs = ident[:, :] if kind == 1 else w_(wv[kind]) if kind != 3 else w_(("va", "vt")[h])
                        pe(T.matmul, b2p[64 * h:64 * h + 64, 128 * b:128 * b + 128], ct[:, 64 * b:64 * b + 64], rhs,
                           start=True, stop=True, w=if_(t, "Vc", 1) + (if_(t, "xr", 5) if kind != 1 else []) + (if_(t, "zb", 6) if two else []),
                           m=f"{L}.V{t}" if b == h == 1 else None)
                km = K["km8"][:, :].unsqueeze(2).to_broadcast([128, 4, 128])
                kx = Kx[t % 2].rearrange("p (i k) -> p i k", i=4)
                fr = if_(t, "SC", 2)
                if kind in (0, 2):
                    kin = b1p[:, 0:128].unsqueeze(1).to_broadcast([128, 4, 128])
                    if kind == 0:
                        dve(V.scalar_tensor_tensor, kx, kin, col("bk0"), km, ALU.add, ALU.mult,
                            w=[f"{L}.QK{t}"] + fr, m=f"{L}.Kx{t}")
                    else:
                        dve(V.tensor_tensor, kx, kin, km, ALU.mult, w=[f"{L}.QK{t}"] + fr, m=f"{L}.Kx{t}")
                    for j in range(4):
                        o = Qx[:, 512 * (t % 2) + 128 * j:512 * (t % 2) + 128 * j + 128]
                        act(S.activation, o, b1p[:, 128:256], ACT.Identity,
                            scale=(K["jm"] if kind == 0 else jm2)[:, j:j + 1], bias=bqm[:, j:j + 1] if kind == 0 else 0.0,
                            w=[f"{L}.QK{t}", f"{L}.Kx{t}"] + fr, m=f"{L}.QTc{t}" if j == 3 else None)
                elif kind == 1:
                    dve(V.tensor_tensor, kx, ct.unsqueeze(1).to_broadcast([128, 4, 128]), km, ALU.mult,
                        w=fr, m=f"{L}.Kx{t}")
                else:
                    A = ab[0]
                    for half, nm, src in ((0, "rk", "K"),):
                        names = (("ka", "kar", "kt", "ktr"), ("qa", "qar", "qt", "qtr"))[half]
                        base = 512 * half
                        for i, n in enumerate(names):
                            tb = K["cos"] if i % 2 == 0 else K["sin"]
                            dve(V.scalar_tensor_tensor, A[:, base + 128 * i:base + 128 * i + 128],
                                b1p[:, 128 * i:128 * i + 128], col(n), tb[:, :], ALU.add, ALU.mult,
                                w=[f"{L}.{src}{t}"] + if_(t, "ks" if half == 0 else "qs", 1),
                                m=f"{L}.{nm}{t}" if i == 3 else None)
                        a4 = A[:, base:base + 512].rearrange("p (s r n) -> p s r n", s=2, r=2)
                        if half == 0:
                            kt_ = U[t % 2][:, 0:256].rearrange("p (s n) -> p s n", s=2)
                            pool(G.tensor_tensor, kt_, a4[:, :, 0, :], a4[:, :, 1, :], ALU.add,
                                 w=[f"{L}.rk{t}"], m=f"{L}.ks{t}")
                            kk = Kx[t % 2].rearrange("p (s i k) -> p s i k", s=2, i=2)
                            for s in range(2):
                                mk = (K["km16"], km16t)[s][:, :].unsqueeze(2).to_broadcast([128, 2, 128])
                                pool(G.tensor_tensor, kk[:, s], kt_[:, s, :].unsqueeze(1).to_broadcast([128, 2, 128]), mk,
                                     ALU.mult, w=[f"{L}.ks{t}"] + fr, m=f"{L}.Kx{t}" if s == 1 else None)
                vb = vv[t % 4]
                pv = b2p[:, 0:256].rearrange("p (b c h d) -> p c b h d", b=2, c=8, h=2)
                if kind == 3:
                    pv3 = b2p[:, 0:256].rearrange("p (b h d) -> p h b d", b=2, h=8)
                    rb = row("bv3").rearrange("p (h d) -> p h d", h=8)
                    for b in range(2):
                        dve(V.tensor_tensor, vb[:, :, b, 0:16], pv3[:, :, b, :], rb, ALU.add,
                            w=[f"{L}.V{t}", f"{L}.vi{t % 4}"] + if_(t, "AV", 4), m=f"{L}.Vc{t}" if b == 1 else None)
                else:
                    for h in range(2):
                        hp = slice(64 * h, 64 * h + 64)
                        wt = [f"{L}.V{t}", f"{L}.vi{t % 4}"] + if_(t, "AV", 4)
                        mk = f"{L}.Vc{t}" if h == 1 else None
                        if kind == 0:
                            rb = row("bv0").rearrange("p (c h d) -> p c h d", c=8, h=2)[hp, :, h, :]
                            dve(V.tensor_tensor, vb[hp, :, :, h, 0:8], pv[hp, :, :, h, :],
                                rb.unsqueeze(2).to_broadcast([64, 8, 2, 8]), ALU.add, w=wt, m=mk)
                        else:
                            act(S.activation, vb[hp, :, :, h, 0:8], pv[hp, :, :, h, :], ACT.Copy, w=wt, m=mk)

            def PQ(t):
                if not two:
                    return
                xt = xnT[t % 4][:, :]
                fr = if_(t, "SC", 2)
                A = ab[0]
                for i, n in enumerate(("qa", "qar", "qt", "qtr")):
                    pe(T.matmul, b1p[:, 128 * i:128 * i + 128], w_(n), xt, start=True, stop=True,
                       w=[f"{L}.Tc{t}", f"{L}.rk{t}"], m=f"{L}.Q{t}" if i == 3 else None)
                for i, n in enumerate(("qa", "qar", "qt", "qtr")):
                    tb = K["cos"] if i % 2 == 0 else K["sin"]
                    dve(V.scalar_tensor_tensor, A[:, 512 + 128 * i:640 + 128 * i], b1p[:, 128 * i:128 * i + 128], col(n),
                        tb[:, :], ALU.add, ALU.mult, w=[f"{L}.Q{t}"] + if_(t, "qs", 1), m=f"{L}.rq{t}" if i == 3 else None)
                a4 = A[:, 512:1024].rearrange("p (s r n) -> p s r n", s=2, r=2)
                qs_ = U[t % 2][:, 256:512]
                pool(G.tensor_tensor, qs_.rearrange("p (s n) -> p s n", s=2), a4[:, :, 0, :], a4[:, :, 1, :],
                     ALU.add, w=[f"{L}.rq{t}"] + if_(t, "QTc", 2), m=f"{L}.qs{t}")
                for s in range(2):
                    for j in range(4):
                        n = 1024 * (t % 2) + 512 * s + 128 * j
                        act(S.activation, Qx[:, n:n + 128], qs_[:, 128 * s:128 * s + 128], ACT.Copy, scale=K["jm"][:, j:j + 1],
                            w=[f"{L}.qs{t}"] + fr, m=f"{L}.QTc{t}" if s == 1 and j == 3 else None)

            def SC(t):
                n = {0: 512 * (t % 2), 1: 512 * (t % 4), 2: 512 * (t % 2), 3: 1024 * (t % 2)}[kind]
                q = Qx[:, n:n + (1024 if two else 512)].rearrange("p (s j n) -> p s j n", j=4, n=128)
                wt = [f"{L}.Kx{t}", f"{L}.Tc{t}" if kind == 1 else f"{L}.QTc{t}"] + if_(t, "Se", 1)
                for j in range(4):
                    for b in range(2):
                        tk = slice(64 * b, 64 * b + 64)
                        mk = f"{L}.SC{t}" if b == 1 and j == 3 else None
                        if two:
                            kk = Kx[t % 2].rearrange("p (s i k) -> p s i k", s=2, i=2)
                            o = bS[tk, :].rearrange("p (h s k) -> p h s k", h=8, s=2)
                            for s in range(2):
                                pe(T.matmul, o[:, 2 * j:2 * j + 2, s, :], q[:, s, j, tk], kk[:, s, :, tk],
                                   start=True, stop=True, w=wt, m=mk if s == 1 else None)
                        else:
                            kx = Kx[t % 2].rearrange("p (i k) -> p i k", i=4)
                            pe(T.matmul, bS[tk, 256 * j:256 * j + 256].rearrange("p (i k) -> p i k", i=4),
                               q[:, 0, j, tk], kx[:, :, tk], start=True, stop=True, w=wt, m=mk)
                nh = 8 if two else 16
                s_ = sS[t % 2]
                s3 = s_.rearrange("p (h k) -> p h k", h=nh)
                p3 = bS[:, :].rearrange("p (h k) -> p h k", h=nh)
                m_ = mx[t % 2][:, 0:nh]
                mb = m_.unsqueeze(2).to_broadcast([128, nh, 1024 // nh])
                fr = if_(t, "PT", 2)
                if kind == 0:
                    dve(V.scalar_tensor_tensor, s3, p3, 8 ** -0.5, dec[:, :].unsqueeze(1).to_broadcast([128, 16, 64]),
                        ALU.mult, ALU.add, w=[f"{L}.SC{t}"] + fr, m=f"{L}.Se{t}")
                elif kind == 2:
                    mk = big2[:, 64 * t:64 * t + 64].unsqueeze(1).to_broadcast([128, 16, 64])
                    dve(V.tensor_tensor, s3, p3, mk, ALU.add, w=[f"{L}.SC{t}", "ld.mask"] + fr, m=f"{L}.Se{t}")
                if kind in (0, 2):
                    dve(V.tensor_reduce, m_, s3, AX_X, ALU.max, w=[f"{L}.Se{t}"] + if_(t, "sb", 2), m=f"{L}.mx{t}")
                    pool(G.tensor_tensor, s3, s3, mb, ALU.subtract, w=[f"{L}.mx{t}"], m=f"{L}.sb{t}")
                elif kind == 1:
                    u_ = U[t % 2]
                    dve(V.tensor_tensor, s3, p3, K["causal"][:, :].unsqueeze(1).to_broadcast([128, 16, 64]), ALU.mult,
                        w=[f"{L}.SC{t}"] + fr, m=f"{L}.Se{t}")
                    dve(V.tensor_scalar, u_, s_, 0.0, NEG, ALU.is_equal, ALU.mult, w=[f"{L}.Se{t}"] + if_(t, "ad", 2), m=f"{L}.nz{t}")
                else:
                    dve(V.tensor_reduce, m_, p3, AX_X, ALU.max, w=[f"{L}.SC{t}"] + if_(t, "Se", 2), m=f"{L}.mx{t}")
                    dve(V.tensor_tensor, s3, p3, mb, ALU.subtract, w=[f"{L}.mx{t}"] + fr, m=f"{L}.Se{t}")

            def MX(t):
                if kind != 1:
                    return
                s_ = sS[t % 2]
                s3 = s_.rearrange("p (h k) -> p h k", h=16)
                m_ = mx[t % 2][:, 0:16]
                dve(V.tensor_tensor, s_, s_, U[t % 2], ALU.add, w=[f"{L}.nz{t}"], m=f"{L}.ad{t}")
                dve(V.tensor_reduce, m_, s3, AX_X, ALU.max, w=[f"{L}.ad{t}"] + if_(t, "sb", 2), m=f"{L}.mx{t}")
                pool(G.tensor_tensor, s3, s3, m_.unsqueeze(2).to_broadcast([128, 16, 64]), ALU.subtract,
                     w=[f"{L}.mx{t}"], m=f"{L}.sb{t}")

            def EX(t):
                act(S.activation, sS[t % 2], sS[t % 2], ACT.Exp, scale={0: 1.0, 1: 8 ** -0.5, 2: 1.0, 3: 0.25}[kind],
                    w=[f"{L}.Se{t}" if two else f"{L}.sb{t}"], m=f"{L}.ex{t}")

            def PTr(t):
                for c in range(8):
                    pe(T.transpose, bP[:, 128 * c:128 * c + 128], sS[t % 2][:, 128 * c:128 * c + 128], ident[:, :],
                       w=[f"{L}.ex{t}"] + if_(t, f"Pc{c // 4}.", 1),
                       m={3: f"{L}.PTa{t}", 7: f"{L}.PT{t}"}.get(c))
                for h in range(2):
                    act(S.activation, PT[t % 2][:, 512 * h:512 * h + 512], bP[:, 512 * h:512 * h + 512], ACT.Copy,
                        w=[f"{L}.PTa{t}" if h == 0 else f"{L}.PT{t}"] + if_(t, "AV", 2), m=f"{L}.Pc{h}.{t}")

            def AV(t):
                n = 34 if two else 36
                for c in range(8):
                    pe(T.matmul, b7[:, n * c:n * c + n], PT[t % 2][:, 128 * c:128 * c + 128],
                       Vb[t % 4][:, n * c:n * c + n], start=True, stop=True,
                       w=[f"{L}.Pc0.{t}", f"{L}.Pc1.{t}", f"{L}.Vc{t}"] + if_(t, "On", 1), m=f"{L}.AV{t}" if c == 7 else None)
                for b in range(2):
                    hp = slice(64 * b, 64 * b + 64)
                    if two:
                        av = b7[:, 0:272].rearrange("p (h b d) -> p h b d", h=8, b=2)[hp, :, b, :]
                        o = O[t % 2].rearrange("p (h d) -> p h d", h=8)[hp]
                        r = rd[t % 2][:, 0:8].unsqueeze(2)[hp]
                        sh, D = [64, 8, 16], 16
                    else:
                        av = b7[:, 0:288].rearrange("p (c b h d) -> p c b h d", c=8, b=2, h=2)[hp, :, b, :, :]
                        o = O[t % 2].rearrange("p (c h d) -> p c h d", c=8, h=2)[hp]
                        r = rd[t % 2].rearrange("p (c h d) -> p c h d", c=8, h=2)[hp]
                        sh, D = [64, 8, 2, 8], 8
                    dve(V.reciprocal, r, av[..., D:D + 1], w=[f"{L}.AV{t}"] + if_(t, "On", 2), m=f"{L}.rd{b}.{t}")
                    dve(V.tensor_tensor, o, av[..., 0:D], r.to_broadcast(sh), ALU.mult,
                        w=[f"{L}.rd{b}.{t}"] + if_(t, "xr" if kind == 1 else "OT", 2), m=f"{L}.On{t}" if b == 1 else None)

            def OTr(t):
                if kind == 1:
                    return
                pe(T.transpose, b0[:, 0:128], O[t % 2], ident[:, :],
                   w=[f"{L}.On{t}", f"{L}.Tc{min(t + 4, NT - 1)}"] + if_(t, "OTc", 1) + (if_(t, "Nc", 1) if two else []), m=f"{L}.OT{t}")
                act(S.activation, OT[t % 2], b0[:, 0:128], ACT.Copy, w=[f"{L}.OT{t}"] + if_(t, "Y", 2), m=f"{L}.OTc{t}")

            def Y(t):
                if kind == 1:
                    pool(G.tensor_tensor, X[:, t, :], X[:, t, :], O[t % 2], ALU.add, w=[f"{L}.On{t}", f"{L}.ln{t}.xn"], m=f"{L}.xr{t}")
                    return
                wt = [f"{L}.OTc{t}", f"{L}.Vc{min(t + 4, NT - 1)}"] + if_(t, "xr", 1) + (if_(t, "zb", 1) if two else [])
                pe(T.matmul, b2p[:, 0:128], OT[t % 2], w_({0: "L0o", 2: "L2o", 3: "o3"}[kind]), start=True, stop=True,
                   w=wt, m=f"{L}.Y{t}")
                if kind == 3:
                    y = ty[t % 2]
                    pool(G.tensor_tensor, ty[2 + t % 2], xn[t % 6][:, :], row("bo3"), ALU.add,
                         w=[f"{L}.ln{t}.xn"] + if_(t, "xr", 2), m=f"{L}.yb{t}")
                    dve(V.tensor_tensor, y, b2p[:, 0:128], ty[2 + t % 2], ALU.add,
                        w=[f"{L}.Y{t}", f"{L}.yb{t}"] + if_(t, "xz", 2), m=f"{L}.xr{t}")
                    statistics(f"{L}.l2{t}", y, 4 + t % 2, w=[f"{L}.xr{t}"])
                else:
                    if kind == 0:
                        pool(G.tensor_tensor, X[:, t, :], X[:, t, :], row("bo0"), ALU.add,
                             w=[f"{L}.ln{t}.xn"], m=f"{L}.xb{t}")
                    dve(V.tensor_tensor, X[:, t, :], X[:, t, :], b2p[:, 0:128], ALU.add,
                        w=[f"{L}.Y{t}", f"{L}.xb{t}" if kind == 0 else f"{L}.ln{t}.xn"], m=f"{L}.xr{t}")

            def N2(t):
                if two:
                    normalise(f"{L}.l2{t}", ty[t % 2], ty[t % 2], 4 + t % 2)

            def T2(t):
                if kind != 3:
                    return
                pe(T.transpose, b0[:, 0:128], ty[t % 2], ident[:, :],
                   w=[f"{L}.l2{t}.xn", f"{L}.Tc{min(t + 5, NT - 1)}", f"{L}.OTc{t}"], m=f"{L}.N{t}")
                act(S.activation, QTz[t % 2], b0[:, 0:128], ACT.Identity, scale=col("gamma"), bias=col("beta"),
                    w=[f"{L}.N{t}"] + if_(t, "Z", 2), m=f"{L}.Nc{t}")

            def Z(t):
                if kind != 3:
                    return
                pe(T.matmul, b2p[:, 0:128], QTz[t % 2], w_("ffn3"), start=True, stop=True,
                   w=[f"{L}.Nc{t}", f"{L}.Vc{min(t + 5, NT - 1)}", f"{L}.xr{t}"] + if_(t, "zb", 1), m=f"{L}.Z{t}")
                dve(V.tensor_tensor, ty[t % 2], b2p[:, 0:128], row("bffn3"), ALU.add, w=[f"{L}.Z{t}"], m=f"{L}.zb{t}")
                dve(V.scalar_tensor_tensor, X[:, t, :], ty[t % 2], 0.0, X[:, t, :], ALU.max, ALU.add,
                    w=[f"{L}.zb{t}"], m=f"{L}.xz{t}")

            QTz = [uni[:, 11392 + 128 * i:11520 + 128 * i] for i in range(2)]

            def at(f, t):
                if 0 <= t < NT:
                    f(t)
            if pending:
                for t in range(4):
                    pending[1](t)
            for t in range(3):
                LN(t)
            for t in range(2):
                LNb(t)
                TR(t)
            PJ(0)
            PQ(0)
            for s in range(NT + 5):
                if pending:
                    at(pending[1], s + 4)
                at(N2, s - 4)
                at(MX, s - 1)
                at(PTr, s - 2)
                if two:
                    at(EX, s - 1)
                at(PJ, s + 1)
                at(LNb, s + 2)
                at(LN, s + 3)
                at(SC, s)
                at(T2, s - 4)
                at(OTr, s - 3)
                at(PQ, s + 1)
                if not two:
                    at(EX, s - 1)
                at(AV, s - 2)
                at(Z, s - 4)
                at(Y, s - 3)
                at(TR, s + 2)

        def moe(L, kind, w1, w2):
            begin(L)
            sems = P.dma_sem(f"ld_{L}")
            nf = 4 if kind != 3 else 2
            W1 = big1[:, :].rearrange("p (e f) -> p e f", e=8)
            W2 = big2[:, 0:8 * nf * 128].rearrange("p (e c d) -> p e c d", e=8, c=nf)
            for e in range(8):
                s1 = P.dma_sem(f"ld_{L}_{e}")
                P.dma(nc.sync.dma_start, W1[:, e, :], w1[e], s1, f"{L}.w{e}", 2)
                P.dma(nc.sync.dma_start, W2[:, e], w2[e].rearrange("(c p) d -> p c d", p=128), s1, f"{L}.w{e}", 2)
            dve(V.memset, carry[:, :], 0.0, m=f"{L}.cr-1")
            cap = 1281.0 if kind == 0 else 320.0
            nc_ = 8 if kind == 0 else 16

            def if_(t, key, back=0):
                return [f"{L}.{key}{t - back}"] if t - back >= 0 else []

            def prep(B):
                for j in range(4):
                    t = 4 * B + j
                    layernorm(f"{L}.ln{t}", X[:, t, :], bxn[B % 2][:, j, :], j,
                              free=(if_(B, "xT", 2) if kind != 3 else if_(B, "nx", 2)) + (if_(B, "xa", 2) if kind != 1 else []))
                src = bxn[B % 2]
                if kind == 3:
                    src = bxr[B % 2]
                    r = rt[B % 2]
                    for j in range(4):
                        t = 4 * B + j
                        act(S.activation, gs_j[:, :], bxn[B % 2][:, j, :], ACT.Square, accum_out=r[12][:, j:j + 1],
                            w=[f"{L}.ln{t}.xn"] + if_(B, "ar", 2) + ([f"{L}.sq{t - 1}"] if j else if_(B, "nx", 1)), m=f"{L}.sq{t}")
                    dve(V.tensor_scalar, r[12][:, 4:8], r[12][:, 0:4], 1.0 / 128.0, 1e-6, ALU.mult, ALU.add,
                        w=[f"{L}.sq{4 * B + 3}"], m=f"{L}.r1{B}")
                    pool(G.tensor_tensor, r[12][:, 8:12], r[12][:, 4:8], sm("nh")[:, 0:4], ALU.pow, w=[f"{L}.r1{B}"], m=f"{L}.r2{B}")
                    for j in range(4):
                        t = 4 * B + j
                        dve(V.scalar_tensor_tensor, src[:, j, :], bxn[B % 2][:, j, :], r[12][:, 8 + j:9 + j], row("scale3"),
                            ALU.mult, ALU.mult, w=[f"{L}.r2{B}"] + if_(B, "xT", 2) + if_(B, "nx", 2), m=f"{L}.xs{t}")
                        act(S.activation, gs_j[:, :], src[:, j, :], ACT.Square, accum_out=r[12][:, 12 + j:13 + j],
                            w=[f"{L}.xs{t}", f"{L}.ny{t - 1}" if j else f"{L}.sq{t + 3}"], m=f"{L}.nx{B}" if j == 3 else f"{L}.ny{t}")

            def turn(B):
                src = bxn[B % 2] if kind != 3 else bxr[B % 2]
                for j in range(4):
                    t = 4 * B + j
                    pe(T.transpose, b0[:, 128 * j:128 * j + 128], src[:, j, :], ident[:, :],
                       w=[f"{L}.ln{t}.xn" if kind != 3 else f"{L}.xs{t}"] + if_(B, "xc", 1), m=f"{L}.xT{B}" if j == 3 else None)
                act(S.activation, bxT[B % 2], b0[:, :], ACT.Copy, w=[f"{L}.xT{B}"] + if_(B, "up", 2), m=f"{L}.xc{B}")
                for j in range(4):
                    pe(T.matmul, b1p[:, 8 * j:8 * j + 8], bxT[B % 2][:, 128 * j:128 * j + 128], sm({0: "r0", 1: "r1", 3: "c3"}[kind]),
                       start=True, stop=True, w=[f"{L}.xc{B}"] + if_(B, "b1f", 1), m=f"{L}.lg{B}" if j == 3 else None)
                lg = b1p[:, 0:32].rearrange("p (t e) -> p t e", t=4)
                r = rt[B % 2]

                def v3(i, n=8):
                    return r[i][:, 0:4 * n].rearrange("p (t e) -> p t e", t=4)

                def s1(i):
                    return r[i][:, 0:4].unsqueeze(2)

                def bc(i):
                    return s1(i).to_broadcast([128, 4, 8])
                revi = sm("revi").unsqueeze(1).to_broadcast([128, 4, 8])
                go = link("dve", f"{L}.g{B}", first=[f"{L}.lg{B}"] + if_(B, "ar", 2))
                if kind == 3:
                    nx = r[12][:, 12:16].unsqueeze(2).to_broadcast([128, 4, 8])
                    go(V.tensor_tensor, v3(0), nx, ny[:, :].unsqueeze(1).to_broadcast([128, 4, 8]), ALU.add, w=[f"{L}.nx{B}"])
                    go(V.scalar_tensor_tensor, v3(1), lg, -2.0, v3(0), ALU.mult, ALU.add, m=f"{L}.b1f{B}")
                    go(V.tensor_reduce, s1(2), v3(1), AX_X, ALU.min)
                    go(V.tensor_tensor, v3(3), v3(1), bc(2), ALU.is_equal)
                    go(V.tensor_tensor, v3(3), v3(3), revi, ALU.mult)
                    go(V.tensor_reduce, s1(4), v3(3), AX_X, ALU.max)
                    go(V.tensor_tensor, gate[B % 2][:, :, :], v3(3), bc(4), ALU.is_equal, w=if_(B, "ar", 2), m=f"{L}.gt{B}")
                    return
                if kind == 1:
                    go(V.tensor_tensor, v3(0), lg, sm("gb").unsqueeze(1).to_broadcast([128, 4, 8]), ALU.add)
                else:
                    go(V.tensor_copy, v3(0), lg)
                go(V.tensor_reduce, s1(1), v3(0), AX_X, ALU.max)
                go(V.tensor_tensor, v3(0), v3(0), bc(1), ALU.subtract, m=f"{L}.ls{B}")
                act(S.activation, v3(2), v3(0), ACT.Exp, w=[f"{L}.ls{B}"], m=f"{L}.le{B}")
                go(V.tensor_reduce, s1(3), v3(2), AX_X, ALU.add, w=[f"{L}.le{B}"])
                go(V.reciprocal, s1(13), s1(3))
                go(V.tensor_tensor, v3(4), v3(2), bc(13), ALU.mult)
                oh = v3(8, 16)
                for c in range(2):
                    go(V.tensor_reduce, s1(5 + c), v3(4), AX_X, ALU.max)
                    go(V.tensor_tensor, v3(7), v3(4), bc(5 + c), ALU.is_equal)
                    go(V.tensor_tensor, v3(7), v3(7), revi, ALU.mult)
                    go(V.tensor_reduce, s1(9), v3(7), AX_X, ALU.max)
                    go(V.tensor_tensor, oh[:, :, 8 * c:8 * c + 8], v3(7), bc(9), ALU.is_equal)
                    if c == 0:
                        go(V.scalar_tensor_tensor, v3(4), oh[:, :, 0:8], -2.0, v3(4), ALU.mult, ALU.add)
                if kind == 0:
                    go(V.tensor_tensor, v3(10), oh[:, :, 0:8], oh[:, :, 8:16], ALU.add, m=f"{L}.oh{B}")
                    sel = v3(10)
                else:
                    go(V.tensor_copy, v3(10, 16), oh, m=f"{L}.oh{B}")
                    sel = v3(10, 16)
                go(V.tensor_tensor, v3(11), oh[:, :, 0:8], bc(5), ALU.mult)
                go(V.tensor_tensor, v3(12), oh[:, :, 8:16], bc(6), ALU.mult)
                if kind == 0:
                    go(V.tensor_tensor, s1(13), s1(5), s1(6), ALU.add)
                    go(V.tensor_tensor, v3(11), v3(11), v3(12), ALU.add)
                    go(V.reciprocal, s1(3), s1(13))
                    go(V.tensor_tensor, v3(11), v3(11), bc(3), ALU.mult)
                rk = b1p[:, 0:4 * nc_].rearrange("p (t e) -> p t e", t=4)
                for j in range(4):
                    pe(T.matmul, rk[:, j, :], tri[:, :], sel[:, j, :], start=True, stop=False, w=[f"{L}.oh{B}", f"{L}.cr{B - 1}"])
                    for i in range(j):
                        pe(T.matmul, rk[:, j, :], ones[:, :], sel[:, i, :], start=False, stop=False)
                    pe(T.matmul, rk[:, j, :], ones[:, :], carry[:, 0:nc_], start=False, stop=True,
                       m=f"{L}.rk{B}" if j == 3 else None)
                cs = r[13][:, 16:16 + nc_].unsqueeze(2)
                go(V.tensor_reduce, cs, r[10][:, 0:4 * nc_].rearrange("p (t e) -> p e t", t=4), AX_X, ALU.add)
                go(V.tensor_tensor, carry[:, 0:nc_], carry[:, 0:nc_], r[13][:, 16:16 + nc_], ALU.add,
                   w=[f"{L}.rk{B}"], m=f"{L}.cr{B}")
                fr = if_(B, "ar", 2)
                if kind == 0:
                    go(V.scalar_tensor_tensor, gate[B % 2][:, :, :], rk, cap, v3(11), ALU.is_lt, ALU.mult, w=fr, m=f"{L}.b1f{B}")
                    P.at[f"{L}.gt{B}"] = P.at[f"{L}.b1f{B}"]
                else:
                    go(V.scalar_tensor_tensor, v3(11), rk[:, :, 0:8], cap, v3(11), ALU.is_lt, ALU.mult)
                    go(V.scalar_tensor_tensor, v3(12), rk[:, :, 8:16], cap, v3(12), ALU.is_lt, ALU.mult)
                    go(V.tensor_tensor, gate[B % 2][:, :, :], v3(11), v3(12), ALU.add, w=fr, m=f"{L}.gt{B}")
                    for j in range(4):
                        pe(T.transpose, b1p[0:8, 128 * j:128 * j + 128], gate[B % 2][:, j, :], ident[:, :],
                           w=[f"{L}.gt{B}"], m=f"{L}.gT{B}" if j == 3 else None)
                    act(S.activation, gT[B % 2][:, :], b1p[0:8, :], ACT.Copy, w=[f"{L}.gT{B}"] + if_(B, "bb", 2), m=f"{L}.gc{B}")
                    for j in range(4):
                        pe(T.matmul, b1p[:, 128 * j:128 * j + 128], gT[B % 2][:, 128 * j:128 * j + 128], B2[:, :],
                           start=True, stop=True, w=[f"{L}.gc{B}", "ld.b"], m=f"{L}.bb{B}" if j == 3 else None)
                    for j in range(4):
                        t = 4 * B + j
                        dve(V.tensor_tensor, X[:, t, :], X[:, t, :], b1p[:, 128 * j:128 * j + 128], ALU.add,
                            w=[f"{L}.bb{B}", f"{L}.ln{t}.xn"], m=f"{L}.b1f{B}" if j == 3 else f"{L}.xq{t}")

            hc = [0]
            hfree = {}

            def up(B, e):
                i = 8 * B + e
                xt = bxT[B % 2]
                h = hS[i % 2]
                if kind == 3:
                    for j in range(2):
                        sg, sa = hc[0] % 4, (hc[0] + 1) % 4
                        pe(T.matmul, HB[sg], W1[:, e, 256 + 128 * j:384 + 128 * j], xt, start=True, stop=True,
                           w=[f"{L}.xc{B}", f"{L}.w{e}"] + ([hfree[sg]] if sg in hfree else []), m=f"{L}.ug{i}.{j}")
                        pe(T.matmul, HB[sa], W1[:, e, 128 * j:128 * j + 128], xt, start=True, stop=True,
                           w=([hfree[sa]] if sa in hfree else []), m=f"{L}.ua{i}.{j}")
                        g_ = gs[j]
                        act(S.activation, g_, HB[sg], ACT.Silu, w=[f"{L}.ug{i}.{j}"] + ([f"{L}.hm{i - 1}.{j}"] if i else []),
                            m=f"{L}.hg{i}.{j}")
                        dve(V.tensor_tensor, h[:, j, :], HB[sa], g_, ALU.mult,
                            w=[f"{L}.ua{i}.{j}", f"{L}.hg{i}.{j}"] + if_(i, "dn", 2), m=f"{L}.hm{i}.{j}")
                        hfree[sg] = f"{L}.hg{i}.{j}"
                        hfree[sa] = f"{L}.hm{i}.{j}"
                        hc[0] += 2
                    if e == 7:
                        P.at[f"{L}.up{B}"] = P.at[f"{L}.ua{i}.1"]
                    return
                for j in range(4):
                    sl = hc[0] % 4
                    pe(T.matmul, HB[sl], W1[:, e, 128 * j:128 * j + 128], xt, start=True, stop=True,
                       w=[f"{L}.xc{B}", f"{L}.w{e}"] + ([hfree[sl]] if sl in hfree else []), m=f"{L}.uh{i}.{j}")
                    if kind == 0:
                        act(S.activation, h[:, j, :], HB[sl], ACT.Silu, w=[f"{L}.uh{i}.{j}"] + if_(i, "dn", 2), m=f"{L}.hm{i}.{j}")
                    else:
                        act(S.activation, h[:, j, :], HB[sl], ACT.Relu, bias=B1[:, e, j:j + 1],
                            w=[f"{L}.uh{i}.{j}", "ld.b"] + if_(i, "dn", 2), m=f"{L}.hm{i}.{j}")
                    hfree[sl] = f"{L}.hm{i}.{j}"
                    hc[0] += 1
                if e == 7:
                    P.at[f"{L}.up{B}"] = P.at[f"{L}.uh{i}.3"]

            def down(B, e):
                i = 8 * B + e
                y = YB[i % 2]
                h = hS[i % 2]
                for j in range(4):
                    for c in range(nf):
                        pe(T.matmul, y[:, 128 * j:128 * j + 128], h[:, c, 128 * j:128 * j + 128], W2[:, e, c, :],
                           start=c == 0, stop=c == nf - 1, w=[f"{L}.hm{i}.{nf - 1}"] + if_(i, "ac", 2),
                           m=f"{L}.dn{i}" if j == 3 and c == nf - 1 else None)
                for j in range(4):
                    t = 4 * B + j
                    last = e == 7 and j == 3
                    dve(V.scalar_tensor_tensor, X[:, t, :], y[:, 128 * j:128 * j + 128], gate[B % 2][:, j, e:e + 1], X[:, t, :],
                        ALU.mult, ALU.add, w=[f"{L}.dn{i}", f"{L}.gt{B}"] + ([f"{L}.aj{i - 1}.{j}"] if e else [f"{L}.ln{t}.xn"])
                        + ([f"{L}.b1f{B}"] if kind == 1 and e == 0 else []),
                        m=f"{L}.aj{i}.{j}")
                P.at[f"{L}.ac{i}"] = P.at[f"{L}.aj{i}.3"]
                if e == 7:
                    P.at[f"{L}.ar{B}"] = P.at[f"{L}.aj{i}.3"]
                    if kind != 1:
                        pool(G.tensor_tensor, X[:, 4 * B:4 * B + 4, :], X[:, 4 * B:4 * B + 4, :], bxn[B % 2], ALU.add,
                             w=[f"{L}.aj{i}.3"], m=f"{L}.xa{B}")
                    if kind == 3:
                        P.dma(nc.sync.dma_start, ov[:, 4 * B:4 * B + 4, :], X[:, 4 * B:4 * B + 4, :], so, "out", 8, w=[f"{L}.xa{B}"])

            gs_j = sb(f"{L}_junk", [128, 128])
            if kind == 3:
                so = P.dma_sem("so")
            prep(0)
            turn(0)
            up(0, 0)
            for B in range(NBK):
                for e in range(8):
                    if e < 7:
                        up(B, e + 1)
                    elif B + 1 < NBK:
                        up(B + 1, 0)
                    down(B, e)
                    if e == 1 and B + 1 < NBK:
                        prep(B + 1)
                    if e == 3 and B + 1 < NBK:
                        turn(B + 1)

        def sparse(L, kind, w1, w2):
            begin(L)
            xbuf, ybuf = SP[L]
            nch = 11 if kind == 0 else 5
            rows = 1408 if kind == 0 else 640
            cap = 1281.0 if kind == 0 else 320.0
            nc_ = 8 if kind == 0 else 16
            W1 = big1[:, :].rearrange("p (e f) -> p e f", e=8)
            W2 = big2[:, :].rearrange("p (e c d) -> p e c d", e=8, c=4)
            for e in range(8):
                s1 = P.dma_sem(f"ld_{L}_{e}")
                P.dma(nc.sync.dma_start, W1[:, e, :], w1[e], s1, f"{L}.w{e}", 2)
                P.dma(nc.sync.dma_start, W2[:, e], w2[e].rearrange("(c p) d -> p c d", p=128), s1, f"{L}.w{e}", 2)
            dve(V.memset, carry[:, :], 0.0, m=f"{L}.cr-1")
            base = K["e0" if kind == 0 else "e1"]
            xall = uni[:, 0:4096].rearrange("p (t d) -> p t d", t=NT)
            xT2 = [uni[:, 4096 + 512 * i:4608 + 512 * i] for i in range(2)]
            r = [uni[:, 5120 + 256 * i:5376 + 256 * i] for i in range(14)]
            LG = [b1p, b7]

            def if_(t, key, back=0):
                return [f"{L}.{key}{t - back}"] if t - back >= 0 else []

            def prep(B):
                mb = mvb[B % 2]
                for j in range(4):
                    t = 4 * B + j
                    dve(V.bn_stats, stt_[j][:, :], X[:, t, :], m=f"{L}.st{t}")
                for j in range(4):
                    t = 4 * B + j
                    dve(V.bn_aggr, mb[:, 2 * j:2 * j + 2], stt_[j][:, :], w=[f"{L}.st{t}"], m=f"{L}.ag{t}")
                dve(V.tensor_scalar, mb[:, 8:12], mb[:, 1:8:2], 1e-5, None, ALU.add, w=[f"{L}.ag{4 * B + 3}"], m=f"{L}.ve{B}")
                pool(G.tensor_tensor, mb[:, 12:16], mb[:, 8:12], sm("nh")[:, 0:4], ALU.pow, w=[f"{L}.ve{B}"], m=f"{L}.rs{B}")

            def logits(B):
                mb = mvb[B % 2]
                for j in range(4):
                    t = 4 * B + j
                    dve(V.tensor_scalar, xall[:, t, :], X[:, t, :], mb[:, 2 * j:2 * j + 1], mb[:, 12 + j:13 + j],
                        ALU.subtract, ALU.mult, w=[f"{L}.rs{B}"], m=f"{L}.xn{t}")
                for j in range(4):
                    t = 4 * B + j
                    pe(T.transpose, b0[:, 128 * j:128 * j + 128], xall[:, t, :], ident[:, :],
                       w=[f"{L}.xn{t}"] + if_(B, "xc", 1), m=f"{L}.xT{B}" if j == 3 else None)
                act(S.activation, xT2[B % 2], b0[:, :], ACT.Copy, w=[f"{L}.xT{B}"] + if_(B, "lg", 2), m=f"{L}.xc{B}")
                if kind == 0:
                    dve(V.tensor_tensor, X[:, 4 * B:4 * B + 4, :], X[:, 4 * B:4 * B + 4, :], xall[:, 4 * B:4 * B + 4, :], ALU.add,
                        w=[f"{L}.xn{4 * B + 3}"], m=f"{L}.xa{B}")
                lb = LG[B // 4]
                for j in range(4):
                    c = 8 * (4 * (B % 4) + j)
                    pe(T.matmul, lb[:, c:c + 8], xT2[B % 2][:, 128 * j:128 * j + 128], sm({0: "r0", 1: "r1"}[kind]),
                       start=True, stop=True, w=[f"{L}.xc{B}"], m=f"{L}.lg{B}" if j == 3 else None)

            def route(H):
                lg = LG[H][:, 0:128].rearrange("p (t e) -> p t e", t=16)

                def v3(i, n=8):
                    return r[i][:, 0:16 * n].rearrange("p (t e) -> p t e", t=16)

                def s1(i):
                    return r[i][:, 0:16].unsqueeze(2)

                def bc(i):
                    return s1(i).to_broadcast([128, 16, 8])
                revi = sm("revi").unsqueeze(1).to_broadcast([128, 16, 8])
                go = link("dve", f"{L}.g{H}", first=[f"{L}.lg{4 * H + 3}"] + ([f"{L}.gt0"] if H else []))
                if kind == 1:
                    go(V.tensor_tensor, v3(0), lg, sm("gb").unsqueeze(1).to_broadcast([128, 16, 8]), ALU.add)
                else:
                    go(V.tensor_copy, v3(0), lg)
                go(V.tensor_reduce, s1(1), v3(0), AX_X, ALU.max)
                go(V.tensor_tensor, v3(0), v3(0), bc(1), ALU.subtract, m=f"{L}.ls{H}")
                act(S.activation, v3(2), v3(0), ACT.Exp, w=[f"{L}.ls{H}"], m=f"{L}.le{H}")
                go(V.tensor_reduce, s1(3), v3(2), AX_X, ALU.add, w=[f"{L}.le{H}"])
                go(V.reciprocal, s1(13), s1(3))
                go(V.tensor_tensor, v3(4), v3(2), bc(13), ALU.mult)
                oh = v3(8, 16)
                for c in range(2):
                    go(V.tensor_reduce, s1(5 + c), v3(4), AX_X, ALU.max)
                    go(V.tensor_tensor, v3(7), v3(4), bc(5 + c), ALU.is_equal)
                    go(V.tensor_tensor, v3(7), v3(7), revi, ALU.mult)
                    go(V.tensor_reduce, s1(9), v3(7), AX_X, ALU.max)
                    go(V.tensor_tensor, oh[:, :, 8 * c:8 * c + 8], v3(7), bc(9), ALU.is_equal, m=f"{L}.o{c}.{H}")
                    if c == 0:
                        go(V.scalar_tensor_tensor, v3(4), oh[:, :, 0:8], -2.0, v3(4), ALU.mult, ALU.add)
                if kind == 0:
                    go(V.tensor_tensor, v3(10), oh[:, :, 0:8], oh[:, :, 8:16], ALU.add, m=f"{L}.oh{H}")
                    sel, sf = v3(10), r[10][:, 0:128]
                else:
                    P.at[f"{L}.oh{H}"] = P.at[f"{L}.o1.{H}"]
                    sel, sf = oh, r[8]
                n = 16 * nc_
                rk = bP[:, 512 * H:512 * H + n].rearrange("p (t e) -> p t e", t=16)
                pe(T.matmul, bP[:, 512 * H:512 * H + n], tri[:, :], sf, start=True, stop=False,
                   w=[f"{L}.oh{H}", f"{L}.cr{H - 1}"], skip_group_check=True)
                for i in range(15):
                    pe(T.matmul, rk[:, i + 1:16, :], ones[:, :], sel[:, i:i + 1, :].to_broadcast([128, 15 - i, nc_]),
                       start=False, stop=False, skip_group_check=True)
                pe(T.matmul, rk, ones[:, :], carry[:, 0:nc_].unsqueeze(1).to_broadcast([128, 16, nc_]), start=False, stop=True,
                   skip_group_check=True, m=f"{L}.rk{H}")
                if kind == 0:
                    go(V.tensor_tensor, s1(13), s1(5), s1(6), ALU.add)
                    go(V.reciprocal, s1(3), s1(13))
                    go(V.tensor_tensor, s1(5), s1(5), s1(3), ALU.mult)
                    go(V.tensor_tensor, s1(6), s1(6), s1(3), ALU.mult)
                w16 = v3(11, 16)
                q = r[12]

                def pc(a):
                    return q[:, a:a + 32]
                go(V.tensor_tensor, w16, oh, base[:, :].unsqueeze(1).to_broadcast([128, 16, 16]), ALU.mult)
                go(V.tensor_reduce, pc(32).unsqueeze(2), r[11][:, 0:256].rearrange("p (c e) -> p c e", e=8), AX_X, ALU.add)
                ds, dg = pc(64), r[13][:, 32:33]
                go(V.tensor_scalar, ds, K["DS"][:, 32 * H:32 * H + 32], K["DG"][:, 0:1], float(8 * rows), ALU.add, ALU.add)
                go(V.tensor_scalar, dg, K["DG"][:, 0:1], float(8 * rows), None, ALU.add)
                cs = r[13][:, 16:16 + nc_]
                go(V.tensor_reduce, cs.unsqueeze(2), sf.rearrange("p (t e) -> p e t", t=16), AX_X, ALU.add)
                go(V.tensor_tensor, carry[:, 0:nc_], carry[:, 0:nc_], cs, ALU.add, w=[f"{L}.rk{H}"], m=f"{L}.cr{H}")
                if kind == 0:
                    for c in range(2):
                        go(V.tensor_tensor, w16[:, :, 8 * c:8 * c + 8], oh[:, :, 8 * c:8 * c + 8], rk, ALU.mult)
                else:
                    go(V.tensor_tensor, w16, oh, rk, ALU.mult)
                go(V.tensor_reduce, pc(0).unsqueeze(2), r[11][:, 0:256].rearrange("p (c e) -> p c e", e=8), AX_X, ALU.add,
                   m=f"{L}.rf{H}")
                kp = pc(96)
                go(V.tensor_scalar, kp, pc(0), cap, None, ALU.is_lt)
                go(V.tensor_tensor, pc(128), pc(0), pc(32), ALU.add)
                go(V.tensor_tensor, pc(160), pc(128), ds, ALU.subtract)
                go(V.tensor_tensor, pc(160), pc(160), kp, ALU.mult)
                go(V.tensor_tensor, idxS[:, 16 * H:16 * H + 16, :].rearrange("p t c -> p (t c)"), pc(160), ds, ALU.add,
                   m=f"{L}.is{H}")
                go(V.scalar_tensor_tensor, pc(192), pc(128), dg, kp, ALU.subtract, ALU.mult)
                go(V.tensor_scalar, idxG[:, 16 * H:16 * H + 16, :].rearrange("p t c -> p (t c)"), pc(192), dg, None, ALU.add)
                kc = kp.rearrange("p (t c) -> p t c", c=2)
                for c in range(2):
                    go(V.tensor_tensor, gates[:, 16 * H:16 * H + 16, c:c + 1], s1(5 + c), kc[:, :, c:c + 1], ALU.mult,
                       m=f"{L}.gt{H}" if c else None)
                sem = P.dma_sem(f"{L}_scatter{H}")
                for t in range(16 * H, 16 * H + 16):
                    for c in range(2):
                        P.op("pool", G.indirect_dma_start, xbuf, bass.IndirectOffsetOnAxis(ap=idxS[:, t, c:c + 1], axis=0),
                             xall[:, t, :], None, w=[f"{L}.is{H}", "zeroed"])
                        pq, last = P.q["pool"], P.q["pool"].ops.pop()
                        pq.ops.append(last[:4] + ((sem, 16),))
                P.at[f"{L}.sd{H}"] = (sem, 512)

            prep(0)
            for B in range(NBK):
                if B + 1 < NBK:
                    prep(B + 1)
                logits(B)
            route(0)
            route(1)

            groups = []
            for e in range(8):
                c = 0
                for n in (4, 4, 3) if kind == 0 else (3, 2):
                    groups.append((e, nch * e + c, n))
                    c += n
            NG = len(groups)
            ring = [uni[:, 9728 + 512 * i:10240 + 512 * i] for i in range(4)]
            yo = [uni[:, 7168 + 512 * i:7680 + 512 * i] for i in range(2)]
            xT3 = [uni[:, 8192 + 512 * i:8704 + 512 * i] for i in range(2)]
            rd_ = [P.dma_sem(f"{L}_rd{i}") for i in range(4)]
            wr_ = [P.dma_sem(f"{L}_wr{i}") for i in range(2)]
            hc = [0]
            hfree = {}

            def fetch(i):
                e, c, n = groups[i]
                P.dma(nc.sync.dma_start, ring[i % 4][:, 0:128 * n].rearrange("p (c d) -> p c d", c=n),
                      xbuf[128 * c:128 * (c + n), :].rearrange("(c p) d -> p c d", p=128), rd_[i % 4], f"{L}.fe{i}", i // 4 + 1,
                      w=[f"{L}.sd0", f"{L}.sd1"] + if_(i, "et", 4))

            def turn(i):
                e, c, n = groups[i]
                for j in range(n):
                    pe(T.transpose, b0[:, 128 * j:128 * j + 128], ring[i % 4][:, 128 * j:128 * j + 128], ident[:, :],
                       w=[f"{L}.fe{i}", f"{L}.xc{NBK - 1}"] + if_(i, "ec", 1), m=f"{L}.et{i}" if j == n - 1 else None)
                act(S.activation, xT3[i % 2][:, 0:128 * n], b0[:, 0:128 * n], ACT.Copy,
                    w=[f"{L}.et{i}", f"{L}.gt1"] + if_(i, "uh", 2), m=f"{L}.ec{i}")

            def up(i):
                e, c, n = groups[i]
                for j in range(4):
                    sl = hc[0] % 4
                    pe(T.matmul, HB[sl][:, 0:128 * n], W1[:, e, 128 * j:128 * j + 128], xT3[i % 2][:, 0:128 * n],
                       start=True, stop=True, w=[f"{L}.ec{i}", f"{L}.w{e}", f"{L}.rf1"]
                       + ([hfree[sl]] if sl in hfree else []), m=f"{L}.uj{i}.{j}" if j < 3 else f"{L}.uh{i}")
                    w = [f"{L}.uj{i}.{j}" if j < 3 else f"{L}.uh{i}"] + if_(i, "dn", 2)
                    h = hS[i % 2][:, j, 0:128 * n]
                    if kind == 0:
                        act(S.activation, h, HB[sl][:, 0:128 * n], ACT.Silu, w=w, m=f"{L}.hm{i}.{j}")
                    elif j % 2:
                        act(S.activation, h, HB[sl][:, 0:128 * n], ACT.Relu, bias=B1[:, e, j:j + 1], w=w + ["ld.b"], m=f"{L}.hm{i}.{j}")
                    else:
                        dve(V.tensor_scalar, h, HB[sl][:, 0:128 * n], B1[:, e, j:j + 1], 0.0, ALU.add, ALU.max,
                            w=w + ["ld.b"], m=f"{L}.hm{i}.{j}")
                    hfree[sl] = f"{L}.hm{i}.{j}"
                    hc[0] += 1

            def down(i):
                e, c, n = groups[i]
                y = YB[i % 2]
                for j in range(n):
                    for k in range(4):
                        pe(T.matmul, y[:, 128 * j:128 * j + 128], hS[i % 2][:, k, 128 * j:128 * j + 128], W2[:, e, k, :],
                           start=k == 0, stop=k == 3, w=[f"{L}.hm{i}.{q}" for q in range(4)] + if_(i, "yo", 2),
                           m=f"{L}.dn{i}" if j == n - 1 and k == 3 else None)
                o = yo[i % 2][:, 0:128 * n]
                w = [f"{L}.dn{i}"] + ([f"{L}.yw{i - 2}"] if i >= 2 else [])
                if kind == 0:
                    dve(V.tensor_copy, o, y[:, 0:128 * n], w=w, m=f"{L}.yo{i}")
                else:
                    dve(V.tensor_tensor, o.rearrange("p (c d) -> p c d", c=n), y[:, 0:128 * n].rearrange("p (c d) -> p c d", c=n),
                        b2r[:, e, :].unsqueeze(1).to_broadcast([128, n, 128]), ALU.add, w=w + ["ld.b"], m=f"{L}.yo{i}")
                P.dma(nc.sync.dma_start, ybuf[128 * c:128 * (c + n), :].rearrange("(c p) d -> p c d", p=128),
                      o.rearrange("p (c d) -> p c d", c=n), wr_[i % 2], f"{L}.yw{i}", i // 2 + 1, w=[f"{L}.yo{i}"])

            for i in range(3):
                fetch(i)
            turn(0)
            up(0)
            turn(1)
            for i in range(NG):
                if i + 1 < NG:
                    up(i + 1)
                if i + 3 < NG:
                    fetch(i + 3)
                if i + 2 < NG:
                    turn(i + 2)
                down(i)

            gsem = [P.dma_sem(f"{L}_g{i}") for i in range(8)]

            def gather(t):
                for c in range(2):
                    i = 2 * t + c
                    P.op("pool", G.indirect_dma_start, gb[i % 8][:, :], None, ybuf,
                         bass.IndirectOffsetOnAxis(ap=idxG[:, t, c:c + 1], axis=0),
                         w=[f"{L}.yw{NG - 1}", f"{L}.yw{NG - 2}", f"{L}.gt1", "zeroed"] + if_(i, "cb", 8))
                    pq, last = P.q["pool"], P.q["pool"].ops.pop()
                    pq.ops.append(last[:4] + ((gsem[i % 8], 16),))
                    P.at[f"{L}.ga{i}"] = (gsem[i % 8], 16 * (i // 8 + 1))

            def combine(t):
                for c in range(2):
                    i = 2 * t + c
                    dve(V.scalar_tensor_tensor, X[:, t, :], gb[i % 8][:, :], gates[:, t, c:c + 1], X[:, t, :], ALU.mult, ALU.add,
                        w=[f"{L}.ga{i}"] + ([f"{L}.cb{i - 1}"] if c else []) + ([f"{L}.xa{NBK - 1}"] if kind == 0 else []),
                        m=f"{L}.cb{i}")
            return L, gather, combine

        def qlin(L):
            begin(L)

            def if_(t, key, back=0):
                return [f"{L}.{key}{t - back}"] if t - back >= 0 else []

            def first(B):
                for j in range(4):
                    t = 4 * B + j
                    layernorm(f"{L}.ln{t}", X[:, t, :], bxn[B % 2][:, j, :], j)
                flat = bxn[B % 2].rearrange("p t d -> p (t d)")
                key = quantise(f"{L}.{B}", flat, bxr[B % 2].rearrange("p t d -> p (t d)"), 512, rt[0][0],
                               w=[f"{L}.ln{4 * B + 3}.xn"] + if_(B, "xT", 2))
                P.at[f"{L}.qd{B}"] = P.at[key]

            def second(B):
                for j in range(4):
                    pe(T.transpose, b0[:, 128 * j:128 * j + 128], bxr[B % 2][:, j, :], ident[:, :],
                       w=[f"{L}.qd{B}"] + if_(B, "xc", 1), m=f"{L}.xT{B}" if j == 3 else None)
                act(S.activation, bxT[B % 2], b0[:, :], ACT.Copy, w=[f"{L}.xT{B}"] + if_(B, "Y", 2), m=f"{L}.xc{B}")
                for j in range(4):
                    pe(T.matmul, b1p[:, 128 * j:128 * j + 128], bxT[B % 2][:, 128 * j:128 * j + 128], wdT[:, :],
                       start=True, stop=True, w=[f"{L}.xc{B}"] + if_(B, "xr", 1), m=f"{L}.Y{B}" if j == 3 else None)
                xb = X[:, 4 * B:4 * B + 4, :]
                pool(G.tensor_tensor, xb, xb, row("b2ffn").unsqueeze(1).to_broadcast([128, 4, 128]), ALU.add,
                     w=[f"{L}.ln{4 * B + 3}.xn"], m=f"{L}.xb{B}")
                dve(V.tensor_tensor, xb.rearrange("p t d -> p (t d)"), xb.rearrange("p t d -> p (t d)"), b1p[:, :], ALU.add,
                    w=[f"{L}.Y{B}", f"{L}.xb{B}"], m=f"{L}.xr{B}")
            for B in range(NBK + 1):
                if B < NBK:
                    first(B)
                if B:
                    second(B - 1)

        attention("A0", 0)
        r0 = sparse("F0", 0, w1a, w2a)
        attention("A1", 1, r0)
        r1 = sparse("F1", 1, w1b, w2b)
        attention("A2", 2, r1)
        qlin("F2")
        attention("A3", 3)
        moe("F3", 3, upw, dnw)
        P.q["sp"].ops.append((None, (), {}, ("out",), None))

        block = es.enter_context(nc.Block())

        @block.sync
        def _(e):
            P.emit("sp", e)

        @block.gpsimd
        def _(e):
            P.emit("pool", e)

        @block.scalar
        def _(e):
            P.emit("act", e)

        @block.vector
        def _(e):
            P.emit("dve", e)

        @block.tensor
        def _(e):
            P.emit("pe", e)


def kernel(**inp):
    import numpy as np
    import concourse.bacc as bacc
    from concourse.bass_utils import run_bass_kernel_spmd as run

    a = {k: np.asarray(v) for k, v in inp.items()}
    f = np.float32
    swap = np.arange(128).reshape(64, 2)[:, ::-1].reshape(128)

    def l3(n):
        return a["L3_xattn_" + n][3]
    sq = {
        "L0q": a["L0_xattn_wq"].T, "L0k": a["L0_xattn_wk"].T, "L0v": a["L0_xattn_wv"].T, "L0o": a["L0_xattn_wo"].T,
        "L2q": a["L2_xattn_wq"].reshape(128, 128), "L2k": a["L2_xattn_wk"].reshape(128, 128),
        "L2v": a["L2_xattn_wv"].reshape(128, 128), "L2o": a["L2_xattn_wo"].reshape(128, 128),
        "va": l3("W_va").T, "vt": l3("W_vt").T, "o3": l3("W_o").T, "ffn3": l3("W_ffn").T,
    }
    cl = {"bq0": a["L0_xattn_bq"], "bk0": a["L0_xattn_bk"], "gamma": l3("gamma"), "beta": l3("beta"),
          "gf": np.broadcast_to(l3("gating_factor"), (128,)), "td": np.broadcast_to(a["L0_xattn_time_decay"], (128,))}
    for n in ("qa", "ka", "qt", "kt"):
        sq[n] = l3("W_" + n).T
        sq[n + "r"] = l3("W_" + n)[swap].T
        cl[n] = l3("b_" + n)
        cl[n + "r"] = l3("b_" + n)[swap]
    wide = np.broadcast_to
    rw = {"bv0": wide(a["L0_xattn_bv"], (128, 128)), "bo0": wide(a["L0_xattn_bo"], (128, 128)),
          "bv3": np.concatenate([wide(l3("b_va"), (64, 128)), wide(l3("b_vt"), (64, 128))]),
          "bo3": wide(l3("b_o"), (128, 128)), "bffn3": wide(l3("b_ffn"), (128, 128)),
          "b2ffn": wide(a["L2_ffn_bias"], (128, 128)), "scale3": wide(a["L3_ffn_scale"], (128, 128))}
    sml = {"r0": a["L0_ffn_router_w"].T, "r1": a["L1_ffn_gate_w"].T, "c3": a["L3_ffn_centroids"].T,
           "gb": wide(a["L1_ffn_gate_b"], (128, 8)), "revi": wide(np.arange(8, 0, -1).astype(f), (128, 8)),
           "nh": np.full((128, 8), -0.5, f)}
    p = np.arange(128)
    inv = (1.0 / 10000.0 ** (np.arange(0, 16, 2, dtype=f) / f(16))).astype(f)
    fr = (np.arange(64, dtype=f)[:, None] * inv[None, :]).astype(f)
    ang = fr[p % 64][:, (p % 16) % 8].T
    sign = np.where(p % 2 == 0, -1.0, 1.0).astype(f)[:, None]
    cst = {
        "ident": np.eye(128, dtype=f), "ones": np.ones((128, 128), f),
        "tri": (p[:, None] < p[None, :]).astype(f), "cos": np.cos(ang), "sin": np.sin(ang) * sign,
        "dist": np.abs((p % 64)[:, None] - np.arange(64)[None, :]).astype(f),
        "causal": (np.arange(64)[None, :] <= (p % 64)[:, None]).astype(f),
        "km8": ((p % 32)[:, None] // 8 == np.arange(4)[None, :]).astype(f),
        "jm": (p[:, None] // 32 == np.arange(4)[None, :]).astype(f),
        "DS": (np.arange(128) // 2 * 128 + np.arange(128) % 2 * 4096)[None, :].repeat(128, 0).astype(f),
        "DG": p[:, None].astype(f),
        "e0": wide((np.arange(16) % 8 * 1408).astype(f), (128, 16)), "e1": wide((np.arange(16) % 8 * 640 + np.arange(16) // 8 * 320).astype(f), (128, 16)),
        "km16": ((p % 32)[:, None] // 16 == np.arange(2)[None, :]).astype(f),
    }
    arrays = {
        "x": a["x"], "ctx": a["ctx_1024"], "mask": a["mask_Bx1xSxS2_ff0"],
        "wsq": np.stack([sq[n] for n in SQ], 1), "cols": np.stack([cl[n] for n in COL], 1),
        "rows": np.stack([rw[n] for n in ROW], 1), "smalls": np.stack([sml[n] for n in SM], 1),
        "wq2": a["L2_ffn_weight"], "w1a": a["L0_ffn_w1"], "w2a": a["L0_ffn_w2"], "w1b": a["L1_ffn_W1"],
        "w2b": a["L1_ffn_W2"], "b1": a["L1_ffn_b1"].reshape(8, 4, 128).transpose(2, 0, 1), "b2": a["L1_ffn_b2"],
        "upw": a["L3_ffn_up_w"], "dnw": a["L3_ffn_down_w"],
    }
    for n in CST:
        arrays["c_" + n] = cst[n]
    arrays = {k: np.ascontiguousarray(v) for k, v in arrays.items()}
    nc = bacc.Bacc("TRN2", target_bir_lowering=False, num_devices=1)
    d = {k: nc.dram_tensor(k + "_dram", v.shape, mybir.dt.from_np(v.dtype), kind="ExternalInput").ap()
         for k, v in arrays.items()}
    out = nc.dram_tensor("out_dram", (64, 64, 128), F32, kind="ExternalOutput").ap()
    build(nc, d["x"], d["ctx"], d["mask"], d["wsq"], d["cols"], d["rows"], d["smalls"], {n: d["c_" + n] for n in CST},
          d["wq2"], d["w1a"], d["w2a"], d["w1b"], d["w2b"], d["b1"], d["b2"], d["upw"], d["dnw"], out)
    r = run(nc, [{k + "_dram": v for k, v in arrays.items()}], core_ids=[0])
    return r.results[0]["out_dram"]
```

```python
from contextlib import ExitStack

import concourse.bass as bass
from concourse import mybir

ALU = mybir.AluOpType
ACT = mybir.ActivationFunctionType
F32 = mybir.dt.float32
AX_X = mybir.AxisListType.X

NT = 32
NBK = 8
NEG = -1000000000.0
MAGIC = 12582912.0

SQ = ["L0q", "L0k", "L0v", "L0o", "L2q", "L2k", "L2v", "L2o", "qa", "qar", "ka", "kar", "qt", "qtr", "kt", "ktr",
      "va", "vt", "o3", "ffn3"]
COL = ["bq0", "bk0", "qa", "qar", "ka", "kar", "qt", "qtr", "kt", "ktr", "gamma", "beta", "gf", "td"]
ROW = ["bv0", "bo0", "bv3", "bo3", "bffn3", "b2ffn", "scale3"]
SM = ["r0", "r1", "c3", "gb", "revi", "nh"]
CST = {"ident": 128, "ones": 128, "tri": 128, "cos": 128, "sin": 128, "dist": 64, "causal": 64, "km8": 4, "km16": 2, "jm": 4, "DS": 128, "DG": 1, "e0": 16, "e1": 16, "chunk": 40}


class Queue:

    def __init__(self, name):
        self.name = name
        self.ops = []
        self.sem = None
        self.count = 0


class Plan:

    def __init__(self, nc, ctx):
        self.nc = nc
        self.ctx = ctx
        self.q = {n: Queue(n) for n in ("pe", "act", "dve", "pool", "sp")}
        self.at = {}

    def phase(self, name):
        for n, q in self.q.items():
            if n != "sp":
                q.sem = self.ctx.enter_context(self.nc.semaphore(f"{name}_{n}"))
                q.count = 0

    def dma_sem(self, name):
        return self.ctx.enter_context(self.nc.semaphore(name))

    def op(self, eng, f, *a, w=(), m=None, **kw):
        q = self.q[eng]
        inc = None
        if m is not None:
            assert m not in self.at, m
            q.count += 1
            inc = (q.sem, 1)
            self.at[m] = (q.sem, q.count)
        q.ops.append((f, a, kw, tuple(w), inc))

    def dma(self, f, out, in_, sem, m, n, w=()):
        self.at[m] = (sem, 16 * n)
        self.q["sp"].ops.append((f, (out, in_), {}, tuple(w), (sem, 16)))

    def emit(self, name, eng):
        seen = {}
        for f, a, kw, waits, inc in self.q[name].ops:
            for key in waits:
                sem, v = self.at[key]
                if seen.get(sem.name, 0) < v:
                    eng.wait_ge(sem, v)
                    seen[sem.name] = v
            if f is None:
                continue
            ins = f(*a, **kw)
            if inc is not None:
                ins.then_inc(*inc)


def build(nc, x, ctx_in, mask, wsq, cols, rows, smalls, consts, wq2, w1a, w2a, w1b, w2b, b1, b2, upw, dnw, out):
    with ExitStack() as es:
        def sb(name, shape, dt=F32):
            return es.enter_context(nc.sbuf_tensor(name, shape, dt))

        def psum(name, n):
            return es.enter_context(nc.psum_tensor(name, [128, n], F32))

        P = Plan(nc, es)
        V, S, G, T = nc.vector, nc.scalar, nc.gpsimd, nc.tensor

        def pe(f, *a, **k):
            P.op("pe", f, *a, **k)

        def act(f, *a, **k):
            P.op("act", f, *a, **k)

        def dve(f, *a, **k):
            P.op("dve", f, *a, **k)

        before = []

        def pool(f, *a, w=(), m=None, **k):
            key = m or f"pool.{len(before)}"
            P.op("pool", f, *a, w=tuple(w) + tuple(before[-1:]), m=key, **k)
            before.append(key)

        def link(eng, prefix, first=()):
            state = [0, list(first)]

            def go(f, *a, w=(), m=None, **k):
                key = m or f"{prefix}.{state[0]}"
                P.op(eng, f, *a, w=tuple(state[1]) + tuple(w), m=key, **k)
                state[0] += 1
                state[1] = [key]
                return key
            return go

        X = sb("X", [128, NT, 128])
        CT = sb("CT", [128, NT * 128])
        W = sb("W", [128, len(SQ), 128])
        C = sb("C", [128, len(COL)])
        R = sb("R", [128, len(ROW), 128])
        M = sb("M", [128, len(SM), 8])
        K = {n: sb("k_" + n, [128, c]) for n, c in CST.items()}
        big1 = sb("big1", [128, 4096])
        big2 = sb("big2", [128, 4096])
        B1 = sb("B1", [128, 8, 4])
        dec = sb("dec", [128, 64])
        ratio = sb("ratio", [128, 4])
        km16t = sb("km16t", [128, 2])
        ny = sb("ny", [128, 8])
        csq = sb("csq", [128, 8])
        wdT = sb("wdT", [128, 128])
        xn = [sb(f"xn{i}", [128, 128]) for i in range(6)]
        xnT = [sb(f"xnT{i}", [128, 128]) for i in range(4)]
        stt_ = [sb(f"st{i}", [128, 6]) for i in range(6)]
        stb = [sb(f"stb{i}", [128, 6]) for i in range(4)]
        mv = [sb(f"mv{i}", [128, 2]) for i in range(6)]
        rs = [sb(f"rs{i}", [128, 1]) for i in range(6)]
        ve = [sb(f"ve{i}", [128, 1]) for i in range(6)]
        uni = sb("uni", [128, 12288])
        Qx = sb("Qx", [128, 2048])
        bqm = sb("bqm", [128, 4])
        jm2 = sb("jm2", [128, 4])
        Kx = [uni[:, 512 + 512 * i:1024 + 512 * i] for i in range(2)]
        sS = [uni[:, 1536 + 1024 * i:2560 + 1024 * i] for i in range(2)]
        PT = [uni[:, 3584 + 1024 * i:4608 + 1024 * i] for i in range(2)]
        Vb = [sb(f"Vb{i}", [128, 288])[:, :] for i in range(4)]
        O = [uni[:, 6208 + 128 * i:6336 + 128 * i] for i in range(2)]
        OT = [uni[:, 6464 + 128 * i:6592 + 128 * i] for i in range(2)]
        mx = [uni[:, 6720 + 16 * i:6736 + 16 * i] for i in range(2)]
        rd = [uni[:, 6752 + 16 * i:6768 + 16 * i] for i in range(2)]
        U = [uni[:, 6784 + 1024 * i:7808 + 1024 * i] for i in range(2)]
        ab = [uni[:, 8832 + 1024 * i:9856 + 1024 * i] for i in range(2)]
        ty = [uni[:, 10880 + 128 * i:11008 + 128 * i] for i in range(4)]
        hS = [uni[:, 2048 * i:2048 * (i + 1)].rearrange("p (c n) -> p c n", c=4) for i in range(2)]
        qv = [uni[:, 8192 + 512 * i:8704 + 512 * i] for i in range(6)]
        rt = [[sb(f"rt{i}_{j}", [128, 64]) for j in range(14)] for i in range(2)]
        carry = sb("carry", [128, 16])
        small = sb("small", [128, 160])
        pads = sb("pads", [128, 48])
        etab = sb("etab", [128, 40], mybir.dt.int32)

        SP = {}
        for L, n in (("F0", 11), ("F1", 5)):
            SP[L] = (nc.dram_tensor(f"{L}_xbuf", (8 * n * 128 + 8192, 128), F32).ap(),
                     nc.dram_tensor(f"{L}_ybuf", (8 * n * 128 + 128, 128), F32).ap())
        SP["F3"] = (nc.dram_tensor("F3_xbuf", (4992, 128), F32).ap(), nc.dram_tensor("F3_ybuf", (4992, 128), F32).ap())
        idxS = sb("idxS", [128, NT, 2], mybir.dt.uint32)
        idxG = sb("idxG", [128, NT, 2], mybir.dt.uint32)
        mvb = [sb(f"mvb{i}", [128, 16]) for i in range(8)]
        gb = [sb(f"gb{i}", [128, 128]) for i in range(8)]
        gates = sb("gates", [128, NT, 2])
        b2r = sb("b2r", [128, 8, 128])
        zero = sb("zero", [128, 1024])
        b0, b1p, b2p = psum("b0", 512), psum("b1", 512), psum("b2", 512)
        bS = psum("bS", 1024)
        bP = psum("bP", 1024)
        b7 = psum("b7", 512)
        HB = [b2p[:, :], bS[:, 0:512], bS[:, 512:1024], b7[:, :]]
        YB = [bP[:, 0:512], bP[:, 512:1024]]

        ident, ones, tri = K["ident"], K["ones"], K["tri"]

        def w_(n):
            i = SQ.index(n)
            return W[:, i, :]

        def col(n):
            i = COL.index(n)
            return C[:, i:i + 1]

        def row(n):
            return R[:, ROW.index(n), :]

        def sm(n):
            return M[:, SM.index(n), :]

        xv = x.rearrange("b s d -> (b s) d").rearrange("(t p) d -> p t d", p=128)
        cv = ctx_in.rearrange("b s d -> (b s) d").rearrange("(t p) d -> p t d", p=128)
        ov = out.rearrange("b s d -> (b s) d").rearrange("(t p) d -> p t d", p=128)
        mv_ = mask.rearrange("b o q k -> (b o q) k").rearrange("(t p) k -> p t k", p=128)
        ldi = P.dma_sem("ldi")
        P.dma(nc.sync.dma_start, ident[:, :], consts["ident"], ldi, "ld.id", 2)
        P.dma(nc.sync.dma_start, wdT[:, :], wq2, ldi, "ld.id", 2)
        cin = big2[:, :].rearrange("p (t d) -> p t d", t=NT)
        for q in range(4):
            P.dma(nc.sync.dma_start, cin[:, 8 * q:8 * q + 8, :], cv[:, 8 * q:8 * q + 8, :], P.dma_sem(f"ldc{q}"), f"ld.ctx{q}", 1)
        loads = [(K[n][:, :], consts[n]) for n in CST if n != "ident"] + [
            (C[:, :], cols), (R[:, :, :], rows), (M[:, :, :], smalls), (W[:, :, :], wsq)]
        ld = P.dma_sem("ld")
        for o, s_ in loads:
            P.dma(nc.sync.dma_start, o, s_, ld, "ld.const", len(loads))
        for q in range(4):
            P.dma(nc.sync.dma_start, X[:, 8 * q:8 * q + 8, :], xv[:, 8 * q:8 * q + 8, :], P.dma_sem(f"ldx{q}"), f"ld.x{q}", 1)


        def begin(name):
            lasts = []
            for n, q in P.q.items():
                if n != "sp" and q.sem is not None and q.count:
                    key = f"end.{n}.{name}"
                    P.at[key] = (q.sem, q.count)
                    lasts.append(key)
            P.phase(name)
            for n in P.q:
                P.q[n].ops.append((None, (), {}, tuple(lasts), None))

        def statistics(k, src, r, w=(), free=()):
            dve(V.bn_stats, stt_[r][:, :], src, w=tuple(w) + tuple(free), m=f"{k}.st")
            dve(V.bn_aggr, mv[r][:, :], stt_[r][:, :], w=[f"{k}.st"], m=f"{k}.ag")
            dve(V.tensor_scalar, ve[r][:, :], mv[r][:, 1:2], 1e-5, None, ALU.add, w=[f"{k}.ag"], m=f"{k}.ve")
            pool(G.tensor_tensor, rs[r][:, :], ve[r][:, :], sm("nh")[:, 0:1], ALU.pow, w=[f"{k}.ve"], m=f"{k}.rs")

        def normalise(k, src, dst, r, free=()):
            dve(V.tensor_scalar, dst, src, mv[r][:, 0:1], rs[r][:, :], ALU.subtract, ALU.mult, w=[f"{k}.rs"] + list(free),
                m=f"{k}.xn")

        def moments(L, B, last):
            mb = mvb[B]
            for j in range(4):
                t = 4 * B + j
                dve(V.bn_stats, stb[j][:, :], X[:, t, :], w=[f"{last}{t}"], m=f"{L}.st{t}")
            for j in range(4):
                t = 4 * B + j
                dve(V.bn_aggr, mb[:, 2 * j:2 * j + 2], stb[j][:, :], w=[f"{L}.st{t}"], m=f"{L}.ag{t}")
            dve(V.tensor_scalar, mb[:, 8:12], mb[:, 1:8:2], 1e-5, None, ALU.add, w=[f"{L}.ag{4 * B + 3}"], m=f"{L}.ve{B}")
            pool(G.tensor_tensor, mb[:, 12:16], mb[:, 8:12], sm("nh")[:, 0:4], ALU.pow, w=[f"{L}.ve{B}"], m=f"{L}.rs{B}")

        def quantise(items, split=False):
            last = [tuple(it[6]) for it in items]

            def blk(t):
                return t.rearrange("p (n k) -> p n k", k=32)

            def steps(it):
                k, src, dst, n, am, bufs, w = it
                nb = n // 32
                a, b_, c, d, e = (q[:, 0:n] for q in bufs)
                wide_ = [128, nb, 32]
                return [
                    (0, V.tensor_reduce, (am[:, 0:nb], blk(src), AX_X, ALU.max), {"apply_absolute_value": True}),
                    (0, V.tensor_scalar, (am[:, 0:nb], am[:, 0:nb], 1.0 / 7.5, 1e-30, ALU.mult, ALU.max), {}),
                    (0, V.reciprocal, (am[:, 32:32 + nb], am[:, 0:nb]), {}),
                    (G.tensor_tensor, V.tensor_tensor,
                     (blk(a), blk(src), am[:, 32:32 + nb].unsqueeze(2).to_broadcast(wide_), ALU.mult), {}),
                    (0, V.scalar_tensor_tensor, (b_, a, -1.0, a, ALU.mult, ALU.max), {}),
                    (0, V.tensor_scalar, (c, b_, 2.0, -4.0, ALU.is_ge, ALU.mult), {}),
                    (0, V.tensor_scalar, (d, b_, 4.0, -2.0, ALU.is_ge, ALU.mult), {}),
                    (0, V.scalar_tensor_tensor, (b_, c, 8.0, d, ALU.add, ALU.add), {}),
                    (0, V.tensor_tensor, (a, a, b_, ALU.mult), {}),
                    (0, V.tensor_scalar, (b_, a, MAGIC, MAGIC, ALU.add, ALU.subtract), {}),
                    (0, V.tensor_tensor, (e, b_, a, ALU.subtract), {}),
                    (0, V.scalar_tensor_tensor, (a, e, 0.5, b_, ALU.is_equal, ALU.subtract), {}),
                    (0, V.tensor_scalar, (c, c, 0.03125, -0.125, ALU.mult, ALU.add), {}),
                    (0, V.scalar_tensor_tensor, (b_, d, 0.125, c, ALU.mult, ALU.add), {}),
                    (0, V.tensor_tensor, (a, a, b_, ALU.mult), {}),
                    (G.tensor_tensor, V.tensor_tensor,
                     (blk(dst), blk(a), am[:, 0:nb].unsqueeze(2).to_broadcast(wide_), ALU.mult), {})]
            for n, row_ in enumerate(zip(*[steps(it) for it in items])):
                for i, (g, v, a, kw) in enumerate(row_):
                    key = f"{items[i][0]}.q{n}"
                    if g and split:
                        pool(g, *a, w=last[i], m=key, **kw)
                    else:
                        dve(v, *a, w=last[i], m=key, **kw)
                    last[i] = (key,)
            return [k[0] for k in last]

        begin("su")
        su = link("dve", "su.v", first=["ld.const"])
        su(V.tensor_scalar, dec[:, :], K["dist"][:, :], col("td"), -1.0, ALU.mult, ALU.mult)
        su(V.tensor_scalar, bqm[:, :], K["jm"][:, :], col("bq0"), None, ALU.mult)
        su(V.tensor_scalar, jm2[:, :], K["jm"][:, :], 8 ** -0.5, None, ALU.mult)
        su(V.tensor_tensor, csq[:, :], sm("c3"), sm("c3"), ALU.mult, m="su.csq")
        act(S.activation, ratio[:, 0:1], col("gf"), ACT.Exp, scale=-1.0, w=["ld.const"], m="su.e")
        su(V.tensor_scalar, ratio[:, 1:2], ratio[:, 0:1], 1.0, None, ALU.add, w=["su.e"])
        su(V.reciprocal, ratio[:, 2:3], ratio[:, 1:2])
        su(V.tensor_scalar, km16t[:, :], K["km16"][:, :], ratio[:, 2:3], None, ALU.mult)
        wqd = quantise([("su.w", wdT[:, :], qv[5][:, 0:128], 128, rt[0][0], qv[0:5], ["ld.id"])])[0]
        zs = P.dma_sem("zero")
        dve(V.memset, zero[:, :], 0.0, m="su.zero")
        for L, n in (("F0", 11), ("F1", 5)):
            P.dma(nc.sync.dma_start, SP[L][0][0:1024 * n, :].rearrange("(p r c) d -> p r (c d)", p=128, c=8),
                  zero[:, :].unsqueeze(1).to_broadcast([128, n, 1024]), zs, "zeroed", 5, w=["su.zero"])
            P.dma(nc.sync.dma_start, SP[L][1][1024 * n:1024 * n + 128, :], zero[:, 0:128], zs, "zeroed", 5, w=["su.zero"])
        P.dma(nc.sync.dma_start, SP["F3"][0].rearrange("(p r) d -> p r d", p=128),
              zero[:, 0:128].unsqueeze(1).to_broadcast([128, 39, 128]), zs, "zeroed", 5, w=["su.zero"])
        banks = [b0[:, :], b1p[:, :], b2p[:, :]]
        for g in range(8):
            bk = banks[g % 3]
            w = [f"ld.ctx{g // 2}", "ld.id"] + ([f"su.cc{g - 3}"] if g >= 3 else [])
            for j in range(4):
                pe(T.transpose, bk[:, 128 * j:128 * j + 128], cin[:, 4 * g + j, :], ident[:, :], w=w,
                   m=f"su.ct{g}" if j == 3 else None)
            act(S.activation, CT[:, 512 * g:512 * g + 512], bk, ACT.Copy, w=[f"su.ct{g}"], m=f"su.cc{g}")

        pe(T.matmul, b7[:, 0:8], ones[:, :], csq[:, :], start=True, stop=True, w=["ld.const", "su.csq"], m="su.ny")
        su(V.tensor_copy, ny[:, :], b7[:, 0:8], w=["su.ny"], m="su.nyc")
        pe(T.transpose, b7[:, 0:128], qv[5][:, 0:128], ident[:, :], w=[wqd, "su.nyc", "ld.id"], m="su.wdT")
        su(V.tensor_copy, wdT[:, :], b7[:, 0:128], w=["su.wdT"])

        def weights(w1, w2, L=None, nf=4):
            W1 = big1[:, :].rearrange("p (e f) -> p e f", e=8)
            W2 = big2[:, 0:8 * nf * 128].rearrange("p (e c d) -> p e c d", e=8, c=nf)
            for e in range(8 if L else 0):
                s1 = P.dma_sem(f"ld_{L}_{e}")
                P.dma(nc.sync.dma_start, W1[:, e, :], w1[e], s1, f"{L}.w{e}", 2)
                P.dma(nc.sync.dma_start, W2[:, e], w2[e].rearrange("(c p) d -> p c d", p=128), s1, f"{L}.w{e}", 2)
            return W1, W2

        def attention(L, kind, pending=None):
            begin(L)
            if kind == 0:
                weights(w1a, w2a, "F0")
            if kind == 1:
                weights(w1b, w2b, "F1")
            two = kind == 3
            vv = [v.rearrange("p (c b h d) -> p c b h d", c=8, b=2, h=2) if not two else
                  v[:, 0:272].rearrange("p (h b d) -> p h b d", h=8, b=2) for v in Vb]
            for i in range(4):
                if two:
                    pool(G.memset, Vb[i][:, 0:272], 1.0, m=f"{L}.vi{i}")
                else:
                    pool(G.memset, Vb[i], 0.0, m=f"{L}.vz{i}")
                    pool(G.memset, vv[i][0:64, :, :, 0, 8:9], 1.0, w=[f"{L}.vz{i}"], m=f"{L}.vy{i}")
                    pool(G.memset, vv[i][64:128, :, :, 1, 8:9], 1.0, w=[f"{L}.vy{i}"], m=f"{L}.vi{i}")
            if kind == 2:
                ldm = P.dma_sem("ldm")
                P.dma(nc.sync.dma_start, big2[:, 0:2048].rearrange("p (t k) -> p t k", t=NT), mv_, ldm, "ld.mask", 1)
            if kind == 1:
                ldw = P.dma_sem("ldw1")
                P.dma(nc.sync.dma_start, B1[:, :, :], b1, ldw, "ld.b", 2)
                P.dma(nc.sync.dma_start, b2r[:, :, :], b2.unsqueeze(0).to_broadcast([128, 8, 128]), ldw, "ld.b", 2)

            def if_(t, key, back=0):
                return [f"{L}.{key}{t - back}"] if t - back >= 0 else []

            def CB(t, c):
                if pending and 0 <= t < NT:
                    pending[2](t, c)

            def LN(t):
                dve(V.bn_stats, stt_[t % 4][:, :], X[:, t, :], w=([f"{pending[0]}.cb{2 * t + 1}"] if pending else [])
                    + ([f"ld.x{t // 8}"] if kind == 0 else []), m=f"{L}.ln{t}.st")

            def LNa(t):
                dve(V.bn_aggr, mv[t % 4][:, :], stt_[t % 4][:, :], w=[f"{L}.ln{t}.st"], m=f"{L}.ln{t}.ag")

            def LNv(t):
                k, q = f"{L}.ln{t}", t % 4
                dve(V.tensor_scalar, ve[q][:, :], mv[q][:, 1:2], 1e-5, None, ALU.add, w=[f"{k}.ag"], m=f"{k}.ve")
                pool(G.tensor_tensor, rs[q][:, :], ve[q][:, :], sm("nh")[:, 0:1], ALU.pow, w=[f"{k}.ve"], m=f"{k}.rs")

            def XB(t):
                if kind == 0:
                    pool(G.tensor_tensor, X[:, t, :], X[:, t, :], row("bo0"), ALU.add, w=[f"{L}.ln{t}.xn"], m=f"{L}.xb{t}")

            def LNb(t):
                normalise(f"{L}.ln{t}", X[:, t, :], xn[t % 6][:, :], t % 4,
                          free=if_(t, "T", 6) + (if_(t, "yb", 6) if kind == 3 else []))

            def TR(t):
                pe(T.transpose, b0[:, 0:128], xn[t % 6][:, :], ident[:, :],
                   w=[f"{L}.ln{t}.xn"] + if_(t, "Tc", 1) + (if_(t, "OTc", 5) if kind != 1 else []), m=f"{L}.T{t}")
                if kind == 1:
                    for j in range(4):
                        act(S.activation, Qx[:, 512 * (t % 4) + 128 * j:512 * (t % 4) + 128 * j + 128], b0[:, 0:128], ACT.Copy,
                            scale=K["jm"][:, j:j + 1], w=[f"{L}.T{t}"] + if_(t, "SC", 4), m=f"{L}.Tc{t}" if j == 3 else None)
                    return
                act(S.activation, xnT[t % 4][:, :], b0[:, 0:128], ACT.Copy,
                    w=[f"{L}.T{t}"] + if_(t, {0: "QK", 2: "QK", 3: "Q"}[kind], 4), m=f"{L}.Tc{t}")

            def PJ(t):
                ct = CT[:, 128 * t:128 * t + 128]
                xt = xnT[t % 4][:, :]
                if kind in (0, 2):
                    n = f"L{kind}"
                    pe(T.matmul, b1p[:, 0:128], w_(n + "k"), ct, start=True, stop=True, w=if_(t, "QTc", 1))
                    pe(T.matmul, b1p[:, 128:256], w_(n + "q"), xt, start=True, stop=True, w=[f"{L}.Tc{t}"], m=f"{L}.QK{t}")
                elif kind == 3:
                    for i, (a, b) in enumerate((("ka", ct), ("kar", ct), ("kt", ct), ("ktr", ct))):
                        pe(T.matmul, b1p[:, 128 * i:128 * i + 128], w_(a), b, start=True, stop=True,
                           w=if_(t, "rq", 1), m=f"{L}.K{t}" if i == 3 else None)
                km = K["km8"][:, :].unsqueeze(2).to_broadcast([128, 4, 128])
                kx = Kx[t % 2].rearrange("p (i k) -> p i k", i=4)
                fr = if_(t, "SC", 2)
                if kind in (0, 2):
                    kin = b1p[:, 0:128].unsqueeze(1).to_broadcast([128, 4, 128])
                    if kind == 0:
                        dve(V.scalar_tensor_tensor, kx, kin, col("bk0"), km, ALU.add, ALU.mult,
                            w=[f"{L}.QK{t}"] + fr, m=f"{L}.Kx{t}")
                    else:
                        dve(V.tensor_tensor, kx, kin, km, ALU.mult, w=[f"{L}.QK{t}"] + fr, m=f"{L}.Kx{t}")
                    for j in range(4):
                        o = Qx[:, 512 * (t % 2) + 128 * j:512 * (t % 2) + 128 * j + 128]
                        act(S.activation, o, b1p[:, 128:256], ACT.Identity,
                            scale=(K["jm"] if kind == 0 else jm2)[:, j:j + 1], bias=bqm[:, j:j + 1] if kind == 0 else 0.0,
                            w=[f"{L}.QK{t}", f"{L}.Kx{t}"] + fr, m=f"{L}.QTc{t}" if j == 3 else None)
                elif kind == 1:
                    for i in range(4):
                        act(S.activation, kx[:, i, :], ct, ACT.Copy, scale=K["km8"][:, i:i + 1], w=fr,
                            m=f"{L}.Kx{t}" if i == 3 else None)
                else:
                    A = ab[0]
                    for half, nm, src in ((0, "rk", "K"),):
                        names = (("ka", "kar", "kt", "ktr"), ("qa", "qar", "qt", "qtr"))[half]
                        base = 512 * half
                        for i, n in enumerate(names):
                            tb = K["cos"] if i % 2 == 0 else K["sin"]
                            dve(V.scalar_tensor_tensor, A[:, base + 128 * i:base + 128 * i + 128],
                                b1p[:, 128 * i:128 * i + 128], col(n), tb[:, :], ALU.add, ALU.mult,
                                w=[f"{L}.{src}{t}"] + if_(t, "ks" if half == 0 else "qs", 1),
                                m=f"{L}.{nm}{t}" if i == 3 else None)
                        a4 = A[:, base:base + 512].rearrange("p (s r n) -> p s r n", s=2, r=2)
                        if half == 0:
                            kt_ = U[t % 2][:, 0:256].rearrange("p (s n) -> p s n", s=2)
                            pool(G.tensor_tensor, kt_, a4[:, :, 0, :], a4[:, :, 1, :], ALU.add,
                                 w=[f"{L}.rk{t}"], m=f"{L}.ks{t}")
                            kk = Kx[t % 2].rearrange("p (s i k) -> p s i k", s=2, i=2)
                            for s in range(2):
                                mk = (K["km16"], km16t)[s][:, :].unsqueeze(2).to_broadcast([128, 2, 128])
                                pool(G.tensor_tensor, kk[:, s], kt_[:, s, :].unsqueeze(1).to_broadcast([128, 2, 128]), mk,
                                     ALU.mult, w=[f"{L}.ks{t}"] + fr, m=f"{L}.Kx{t}" if s == 1 else None)

            def PV(t):
                ct = CT[:, 128 * t:128 * t + 128]
                wv = {0: "L0v", 2: "L2v"}
                for b in range(2):
                    for h in range(2):
                        rhs = ident[:, :] if kind == 1 else w_(wv[kind]) if kind != 3 else w_(("va", "vt")[h])
                        pe(T.matmul, b2p[64 * h:64 * h + 64, 128 * b:128 * b + 128], ct[:, 64 * b:64 * b + 64], rhs,
                           start=True, stop=True, w=if_(t, "Vc", 1) + (if_(t, "xr", 5) if kind != 1 else []) + (if_(t, "zb", 6) if two else []),
                           m=f"{L}.V{t}" if b == h == 1 else None)
                vb = vv[t % 4]
                pv = b2p[:, 0:256].rearrange("p (b c h d) -> p c b h d", b=2, c=8, h=2)
                if kind == 3:
                    pv3 = b2p[:, 0:256].rearrange("p (b h d) -> p h b d", b=2, h=8)
                    rb = row("bv3").rearrange("p (h d) -> p h d", h=8)
                    for b in range(2):
                        dve(V.tensor_tensor, vb[:, :, b, 0:16], pv3[:, :, b, :], rb, ALU.add,
                            w=[f"{L}.V{t}", f"{L}.vi{t % 4}"] + if_(t, "AV", 4), m=f"{L}.Vc{t}" if b == 1 else None)
                else:
                    for h in range(2):
                        hp = slice(64 * h, 64 * h + 64)
                        wt = [f"{L}.V{t}", f"{L}.vi{t % 4}"] + if_(t, "AV", 4)
                        mk = f"{L}.Vc{t}" if h == 1 else None
                        if kind == 0:
                            rb = row("bv0").rearrange("p (c h d) -> p c h d", c=8, h=2)[hp, :, h, :]
                            dve(V.tensor_tensor, vb[hp, :, :, h, 0:8], pv[hp, :, :, h, :],
                                rb.unsqueeze(2).to_broadcast([64, 8, 2, 8]), ALU.add, w=wt, m=mk)
                        else:
                            act(S.activation, vb[hp, :, :, h, 0:8], pv[hp, :, :, h, :], ACT.Copy, w=wt, m=mk)

            def PQ(t):
                if not two:
                    return
                xt = xnT[t % 4][:, :]
                for i, n in enumerate(("qa", "qar", "qt", "qtr")):
                    pe(T.matmul, b1p[:, 128 * i:128 * i + 128], w_(n), xt, start=True, stop=True,
                       w=[f"{L}.Tc{t}", f"{L}.rk{t}"], m=f"{L}.Q{t}" if i == 3 else None)

            def PR(t):
                if not two:
                    return
                fr = if_(t, "SC", 2)
                A = ab[0]
                for i, n in enumerate(("qa", "qar", "qt", "qtr")):
                    tb = K["cos"] if i % 2 == 0 else K["sin"]
                    dve(V.scalar_tensor_tensor, A[:, 512 + 128 * i:640 + 128 * i], b1p[:, 128 * i:128 * i + 128], col(n),
                        tb[:, :], ALU.add, ALU.mult, w=[f"{L}.Q{t}"] + if_(t, "qs", 1), m=f"{L}.rq{t}" if i == 3 else None)
                a4 = A[:, 512:1024].rearrange("p (s r n) -> p s r n", s=2, r=2)
                qs_ = U[t % 2][:, 256:512]
                pool(G.tensor_tensor, qs_.rearrange("p (s n) -> p s n", s=2), a4[:, :, 0, :], a4[:, :, 1, :],
                     ALU.add, w=[f"{L}.rq{t}"] + if_(t, "QTc", 2), m=f"{L}.qs{t}")
                qx = Qx[:, 1024 * (t % 2):1024 * (t % 2) + 1024].rearrange("p (s j n) -> p s j n", s=2, j=4)
                for j in range(4):
                    act(S.activation, qx[:, :, j, :], qs_.rearrange("p (s n) -> p s n", s=2), ACT.Copy,
                        scale=K["jm"][:, j:j + 1], w=[f"{L}.qs{t}"] + fr, m=f"{L}.QTc{t}" if j == 3 else None)

            def SC(t):
                n = {0: 512 * (t % 2), 1: 512 * (t % 4), 2: 512 * (t % 2), 3: 1024 * (t % 2)}[kind]
                q = Qx[:, n:n + (1024 if two else 512)].rearrange("p (s j n) -> p s j n", j=4, n=128)
                wt = [f"{L}.Kx{t}", f"{L}.Tc{t}" if kind == 1 else f"{L}.QTc{t}"] + if_(t, "Se", 1)
                for j in range(4):
                    for b in range(2):
                        tk = slice(64 * b, 64 * b + 64)
                        mk = f"{L}.SC{t}" if b == 1 and j == 3 else None
                        if two:
                            kk = Kx[t % 2].rearrange("p (s i k) -> p s i k", s=2, i=2)
                            o = bS[tk, :].rearrange("p (h s k) -> p h s k", h=8, s=2)
                            for s in range(2):
                                pe(T.matmul, o[:, 2 * j:2 * j + 2, s, :], q[:, s, j, tk], kk[:, s, :, tk],
                                   start=True, stop=True, w=wt, m=mk if s == 1 else None)
                        else:
                            kx = Kx[t % 2].rearrange("p (i k) -> p i k", i=4)
                            pe(T.matmul, bS[tk, 256 * j:256 * j + 256].rearrange("p (i k) -> p i k", i=4),
                               q[:, 0, j, tk], kx[:, :, tk], start=True, stop=True, w=wt, m=mk)
                nh = 8 if two else 16
                s_ = sS[t % 2]
                s3 = s_.rearrange("p (h k) -> p h k", h=nh)
                p3 = bS[:, :].rearrange("p (h k) -> p h k", h=nh)
                m_ = mx[t % 2][:, 0:nh]
                mb = m_.unsqueeze(2).to_broadcast([128, nh, 1024 // nh])
                fr = if_(t, "PT", 2)
                if kind == 0:
                    dve(V.scalar_tensor_tensor, s3, p3, 8 ** -0.5, dec[:, :].unsqueeze(1).to_broadcast([128, 16, 64]),
                        ALU.mult, ALU.add, w=[f"{L}.SC{t}"] + fr, m=f"{L}.Se{t}")
                elif kind == 2:
                    mk = big2[:, 64 * t:64 * t + 64].unsqueeze(1).to_broadcast([128, 16, 64])
                    dve(V.tensor_tensor, s3, p3, mk, ALU.add, w=[f"{L}.SC{t}", "ld.mask"] + fr, m=f"{L}.Se{t}")
                if kind in (0, 2):
                    dve(V.tensor_reduce, m_, s3, AX_X, ALU.max, w=[f"{L}.Se{t}"] + if_(t, "sb", 2), m=f"{L}.mx{t}")
                    pool(G.tensor_tensor, s3, s3, mb, ALU.subtract, w=[f"{L}.mx{t}"], m=f"{L}.sb{t}")
                elif kind == 1:
                    u_ = U[t % 2]
                    dve(V.tensor_tensor, s3, p3, K["causal"][:, :].unsqueeze(1).to_broadcast([128, 16, 64]), ALU.mult,
                        w=[f"{L}.SC{t}"] + fr, m=f"{L}.Se{t}")
                    dve(V.tensor_scalar, u_, s_, 0.0, NEG, ALU.is_equal, ALU.mult, w=[f"{L}.Se{t}"] + if_(t, "ad", 2), m=f"{L}.nz{t}")
                else:
                    dve(V.tensor_reduce, m_, p3, AX_X, ALU.max, w=[f"{L}.SC{t}"] + if_(t, "Se", 2), m=f"{L}.mx{t}")
                    dve(V.tensor_tensor, s3, p3, mb, ALU.subtract, w=[f"{L}.mx{t}"] + fr, m=f"{L}.Se{t}")

            def MX(t):
                if kind != 1:
                    return
                s_ = sS[t % 2]
                s3 = s_.rearrange("p (h k) -> p h k", h=16)
                m_ = mx[t % 2][:, 0:16]
                dve(V.tensor_tensor, s_, s_, U[t % 2], ALU.add, w=[f"{L}.nz{t}"], m=f"{L}.ad{t}")
                dve(V.tensor_reduce, m_, s3, AX_X, ALU.max, w=[f"{L}.ad{t}"] + if_(t, "sb", 2), m=f"{L}.mx{t}")
                pool(G.tensor_tensor, s3, s3, m_.unsqueeze(2).to_broadcast([128, 16, 64]), ALU.subtract,
                     w=[f"{L}.mx{t}"], m=f"{L}.sb{t}")

            def EX(t):
                act(S.activation, sS[t % 2], sS[t % 2], ACT.Exp, scale={0: 1.0, 1: 8 ** -0.5, 2: 1.0, 3: 0.25}[kind],
                    w=[f"{L}.Se{t}" if two else f"{L}.sb{t}"], m=f"{L}.ex{t}")

            def PTr(t):
                for c in range(8):
                    pe(T.transpose, bP[:, 128 * c:128 * c + 128], sS[t % 2][:, 128 * c:128 * c + 128], ident[:, :],
                       w=[f"{L}.ex{t}"] + if_(t, f"Pc{c // 4}.", 1),
                       m={3: f"{L}.PTa{t}", 7: f"{L}.PT{t}"}.get(c))
                for h in range(2):
                    act(S.activation, PT[t % 2][:, 512 * h:512 * h + 512], bP[:, 512 * h:512 * h + 512], ACT.Copy,
                        w=[f"{L}.PTa{t}" if h == 0 else f"{L}.PT{t}"] + if_(t, "AV", 2), m=f"{L}.Pc{h}.{t}")

            def AV(t):
                n = 34 if two else 36
                for c in range(8):
                    pe(T.matmul, b7[:, n * c:n * c + n], PT[t % 2][:, 128 * c:128 * c + 128],
                       Vb[t % 4][:, n * c:n * c + n], start=True, stop=True,
                       w=[f"{L}.Pc0.{t}", f"{L}.Pc1.{t}", f"{L}.Vc{t}"] + if_(t, "On", 1), m=f"{L}.AV{t}" if c == 7 else None)
                halves = []
                for b in range(2):
                    hp = slice(64 * b, 64 * b + 64)
                    if two:
                        av = b7[:, 0:272].rearrange("p (h b d) -> p h b d", h=8, b=2)[hp, :, b, :]
                        o = O[t % 2].rearrange("p (h d) -> p h d", h=8)[hp]
                        r = rd[t % 2][:, 0:8].unsqueeze(2)[hp]
                        sh, D = [64, 8, 16], 16
                    else:
                        av = b7[:, 0:288].rearrange("p (c b h d) -> p c b h d", c=8, b=2, h=2)[hp, :, b, :, :]
                        o = O[t % 2].rearrange("p (c h d) -> p c h d", c=8, h=2)[hp]
                        r = rd[t % 2].rearrange("p (c h d) -> p c h d", c=8, h=2)[hp]
                        sh, D = [64, 8, 2, 8], 8
                    dve(V.reciprocal, r, av[..., D:D + 1], w=[f"{L}.AV{t}"] + if_(t, "On", 2), m=f"{L}.rd{b}.{t}")
                    halves.append((o, av[..., 0:D], r.to_broadcast(sh)))
                for b in range(2):
                    o, v_, r = halves[b]
                    dve(V.tensor_tensor, o, v_, r, ALU.mult,
                        w=[f"{L}.rd{b}.{t}"] + if_(t, "xr" if kind == 1 else "OT", 2), m=f"{L}.On{t}" if b == 1 else None)

            def OTr(t):
                if kind == 1:
                    return
                pe(T.transpose, b0[:, 0:128], O[t % 2], ident[:, :],
                   w=[f"{L}.On{t}", f"{L}.Tc{min(t + 4, NT - 1)}"] + if_(t, "OTc", 1) + (if_(t, "Nc", 1) if two else []), m=f"{L}.OT{t}")
                act(S.activation, OT[t % 2], b0[:, 0:128], ACT.Copy, w=[f"{L}.OT{t}"] + if_(t, "Y", 2), m=f"{L}.OTc{t}")

            def Y(t):
                if kind == 1:
                    pool(G.tensor_tensor, X[:, t, :], X[:, t, :], O[t % 2], ALU.add, w=[f"{L}.On{t}", f"{L}.ln{t}.xn"], m=f"{L}.xr{t}")
                    return
                wt = [f"{L}.OTc{t}", f"{L}.Vc{min(t + 4, NT - 1)}"] + if_(t, "xr", 1) + (if_(t, "zb", 1) if two else [])
                pe(T.matmul, b2p[:, 0:128], OT[t % 2], w_({0: "L0o", 2: "L2o", 3: "o3"}[kind]), start=True, stop=True,
                   w=wt, m=f"{L}.Y{t}")
                if kind == 3:
                    y = ty[t % 2]
                    pool(G.tensor_tensor, ty[2 + t % 2], xn[t % 6][:, :], row("bo3"), ALU.add,
                         w=[f"{L}.ln{t}.xn"] + if_(t, "xr", 2), m=f"{L}.yb{t}")
                    dve(V.tensor_tensor, y, b2p[:, 0:128], ty[2 + t % 2], ALU.add,
                        w=[f"{L}.Y{t}", f"{L}.yb{t}"] + if_(t, "xz", 2), m=f"{L}.xr{t}")
                    statistics(f"{L}.l2{t}", y, 4 + t % 2, w=[f"{L}.xr{t}"])
                else:
                    dve(V.tensor_tensor, X[:, t, :], X[:, t, :], b2p[:, 0:128], ALU.add,
                        w=[f"{L}.Y{t}", f"{L}.xb{t}" if kind == 0 else f"{L}.ln{t}.xn"], m=f"{L}.xr{t}")

            def N2(t):
                if two:
                    normalise(f"{L}.l2{t}", ty[t % 2], ty[t % 2], 4 + t % 2)

            def T2(t):
                if kind != 3:
                    return
                pe(T.transpose, b0[:, 0:128], ty[t % 2], ident[:, :],
                   w=[f"{L}.l2{t}.xn", f"{L}.Tc{min(t + 5, NT - 1)}", f"{L}.OTc{t}"], m=f"{L}.N{t}")
                act(S.activation, QTz[t % 2], b0[:, 0:128], ACT.Identity, scale=col("gamma"), bias=col("beta"),
                    w=[f"{L}.N{t}"] + if_(t, "Z", 2), m=f"{L}.Nc{t}")

            def Z(t):
                if kind != 3:
                    return
                pe(T.matmul, b2p[:, 0:128], QTz[t % 2], w_("ffn3"), start=True, stop=True,
                   w=[f"{L}.Nc{t}", f"{L}.Vc{min(t + 5, NT - 1)}", f"{L}.xr{t}"] + if_(t, "zb", 1), m=f"{L}.Z{t}")
                dve(V.tensor_tensor, ty[t % 2], b2p[:, 0:128], row("bffn3"), ALU.add, w=[f"{L}.Z{t}"], m=f"{L}.zb{t}")
                dve(V.scalar_tensor_tensor, X[:, t, :], ty[t % 2], 0.0, X[:, t, :], ALU.max, ALU.add,
                    w=[f"{L}.zb{t}"], m=f"{L}.xz{t}")

            QTz = [uni[:, 11392 + 128 * i:11520 + 128 * i] for i in range(2)]

            def at(f, t):
                if 0 <= t < NT:
                    f(t)
            if pending:
                for t in range(5):
                    pending[1](t)
            for t in range(4):
                CB(t, 0)
                CB(t, 1)
            for f in (LN, LNa, LNv):
                for t in range(3):
                    f(t)
            for t in range(2):
                LNb(t)
                TR(t)
            PJ(0)
            PV(0)
            PQ(0)
            PR(0)
            XB(0)
            for s in range(NT + 5):
                if pending:
                    at(pending[1], s + 5)
                at(MX, s - 1)
                at(PTr, s - 2)
                at(Y, s - 4)
                if two:
                    at(EX, s - 1)
                at(PJ, s + 1)
                at(XB, s + 1)
                at(LNb, s + 2)
                CB(s + 4, 0)
                at(LN, s + 3)
                CB(s + 4, 1)
                at(N2, s - 4)
                at(LNa, s + 3)
                at(LNv, s + 3)
                at(SC, s)
                at(PV, s + 1)
                at(T2, s - 4)
                at(PQ, s + 1)
                at(OTr, s - 3)
                at(PR, s + 1)
                if not two:
                    at(EX, s - 1)
                at(AV, s - 2)
                at(Z, s - 4)
                at(TR, s + 2)
                if s >= 8 and s % 4 == 0 and not two:
                    moments(L.replace("A", "F"), s // 4 - 2, f"{L}.x{'z' if two else 'r'}")

        def sparse(L, kind, w1, w2):
            begin(L)
            xbuf, ybuf = SP[L]
            nch = 11 if kind == 0 else 5
            rows = 1408 if kind == 0 else 640
            cap = 1281.0 if kind == 0 else 320.0
            nc_ = 8 if kind == 0 else 16
            W1, W2 = weights(w1, w2)
            dve(V.memset, carry[:, :], 0.0, m=f"{L}.cr-1")
            base = K["e0" if kind == 0 else "e1"]
            xall = uni[:, 0:4096].rearrange("p (t d) -> p t d", t=NT)
            xT2 = [uni[:, 4096 + 512 * i:4608 + 512 * i] for i in range(2)]
            r = [uni[:, 5120 + 256 * i:5376 + 256 * i] for i in range(14)]
            LG = [b1p, b7]
            pre = [uni[:, 8704 + 384 * i:9088 + 384 * i] for i in range(2)]
            for i in range(2):
                dve(V.memset, pre[i][:, 0:8 * nc_], 0.0, m=f"{L}.pz{i}")

            def if_(t, key, back=0):
                return [f"{L}.{key}{t - back}"] if t - back >= 0 else []

            def logits(B):
                mb = mvb[B]
                for j in range(4):
                    t = 4 * B + j
                    dve(V.tensor_scalar, xall[:, t, :], X[:, t, :], mb[:, 2 * j:2 * j + 1], mb[:, 12 + j:13 + j],
                        ALU.subtract, ALU.mult, w=[f"{L}.rs{B}"], m=f"{L}.xn{t}")
                tb = (b0, b2p)[B % 2]
                for j in range(4):
                    t = 4 * B + j
                    pe(T.transpose, tb[:, 128 * j:128 * j + 128], xall[:, t, :], ident[:, :],
                       w=[f"{L}.xn{t}"] + if_(B, "xc", 2), m=f"{L}.xT{B}" if j == 3 else None)
                act(S.activation, xT2[B % 2], tb[:, :], ACT.Copy, w=[f"{L}.xT{B}"] + if_(B, "lg", 2), m=f"{L}.xc{B}")
                if kind == 0:
                    dve(V.tensor_tensor, X[:, 4 * B:4 * B + 4, :], X[:, 4 * B:4 * B + 4, :], xall[:, 4 * B:4 * B + 4, :], ALU.add,
                        w=[f"{L}.xn{4 * B + 3}"], m=f"{L}.xa{B}")
                if B % 4:
                    products(B - 1)
                if B % 4 == 3:
                    products(B)

            def products(B):
                lb = LG[B // 4]
                for j in range(4):
                    c = 8 * (4 * (B % 4) + j)
                    pe(T.matmul, lb[:, c:c + 8], xT2[B % 2][:, 128 * j:128 * j + 128], sm({0: "r0", 1: "r1"}[kind]),
                       start=True, stop=True, w=[f"{L}.xc{B}"], m=f"{L}.lg{B}" if j == 3 else None)

            def route(H):
                lg = LG[H][:, 0:128].rearrange("p (t e) -> p t e", t=16)

                def v3(i, n=8):
                    return r[i][:, 0:16 * n].rearrange("p (t e) -> p t e", t=16)

                def s1(i):
                    return r[i][:, 0:16].unsqueeze(2)

                def bc(i):
                    return s1(i).to_broadcast([128, 16, 8])
                revi = sm("revi").unsqueeze(1).to_broadcast([128, 16, 8])
                go = link("dve", f"{L}.g{H}", first=[f"{L}.lg{4 * H + 3}", f"{L}.cr-1", f"{L}.pz1"] + ([f"{L}.gt0"] if H else []))
                if kind == 1:
                    go(V.tensor_tensor, v3(0), lg, sm("gb").unsqueeze(1).to_broadcast([128, 16, 8]), ALU.add)
                else:
                    go(V.tensor_copy, v3(0), lg)
                go(V.tensor_reduce, s1(1), v3(0), AX_X, ALU.max)
                go(V.tensor_tensor, v3(0), v3(0), bc(1), ALU.subtract, m=f"{L}.ls{H}")
                act(S.activation, v3(2), v3(0), ACT.Exp, w=[f"{L}.ls{H}"], m=f"{L}.le{H}")
                go(V.tensor_reduce, s1(3), v3(2), AX_X, ALU.add, w=[f"{L}.le{H}"])
                go(V.reciprocal, s1(13), s1(3))
                go(V.tensor_tensor, v3(4), v3(2), bc(13), ALU.mult)
                oh = v3(8, 16)
                for c in range(2):
                    go(V.tensor_reduce, s1(5 + c), v3(4), AX_X, ALU.max)
                    go(V.tensor_tensor, v3(7), v3(4), bc(5 + c), ALU.is_equal)
                    go(V.tensor_tensor, v3(7), v3(7), revi, ALU.mult)
                    go(V.tensor_reduce, s1(9), v3(7), AX_X, ALU.max)
                    go(V.tensor_tensor, oh[:, :, 8 * c:8 * c + 8], v3(7), bc(9), ALU.is_equal, m=f"{L}.o{c}.{H}")
                    if c == 0:
                        go(V.scalar_tensor_tensor, v3(4), oh[:, :, 0:8], -2.0, v3(4), ALU.mult, ALU.add)
                if kind == 0:
                    go(V.tensor_tensor, v3(10), oh[:, :, 0:8], oh[:, :, 8:16], ALU.add, m=f"{L}.oh{H}")
                    sel, sf = v3(10), r[10][:, 0:128]
                else:
                    P.at[f"{L}.oh{H}"] = P.at[f"{L}.o1.{H}"]
                    sel, sf = oh, r[8]
                n = 16 * nc_
                pe(T.matmul, bP[:, 512 * H + 256:512 * H + 256 + n], ones[:, :], sf, start=True, stop=True, w=[f"{L}.oh{H}"])
                pe(T.matmul, bP[:, 512 * H:512 * H + n], tri[:, :], sf, start=True, stop=True, m=f"{L}.rk{H}")
                pad = 8 * nc_
                go(V.tensor_copy, pre[0][:, pad:pad + n], bP[:, 512 * H + 256:512 * H + 256 + n], w=[f"{L}.rk{H}"])
                for k, st in enumerate((1, 2, 4, 8)):
                    u, v = pre[k % 2], pre[(k + 1) % 2]
                    go(V.tensor_tensor, v[:, pad:pad + n], u[:, pad:pad + n], u[:, pad - nc_ * st:pad + n - nc_ * st], ALU.add)
                go(V.tensor_tensor, pre[1][:, pad:pad + n], bP[:, 512 * H:512 * H + n], pre[0][:, pad - nc_:pad + n - nc_], ALU.add)
                rk = pre[1][:, pad:pad + n].rearrange("p (t e) -> p t e", t=16)
                go(V.tensor_tensor, rk, rk, carry[:, 0:nc_].unsqueeze(1).to_broadcast([128, 16, nc_]), ALU.add)
                if H == 0:
                    go(V.tensor_copy, carry[:, 0:nc_], pre[0][:, pad + n - nc_:pad + n])
                if kind == 0:
                    go(V.tensor_tensor, s1(13), s1(5), s1(6), ALU.add)
                    go(V.reciprocal, s1(3), s1(13))
                    go(V.tensor_tensor, s1(5), s1(5), s1(3), ALU.mult)
                    go(V.tensor_tensor, s1(6), s1(6), s1(3), ALU.mult)
                w16 = v3(11, 16)
                q = r[12]

                def pc(a):
                    return q[:, a:a + 32]
                go(V.tensor_tensor, w16, oh, base[:, :].unsqueeze(1).to_broadcast([128, 16, 16]), ALU.mult)
                go(V.tensor_reduce, pc(32).unsqueeze(2), r[11][:, 0:256].rearrange("p (c e) -> p c e", e=8), AX_X, ALU.add)
                ds, dg = pc(64), r[13][:, 32:33]
                go(V.tensor_scalar, ds, K["DS"][:, 32 * H:32 * H + 32], K["DG"][:, 0:1], float(8 * rows), ALU.add, ALU.add)
                go(V.tensor_scalar, dg, K["DG"][:, 0:1], float(8 * rows), None, ALU.add)
                if kind == 0:
                    for c in range(2):
                        go(V.tensor_tensor, w16[:, :, 8 * c:8 * c + 8], oh[:, :, 8 * c:8 * c + 8], rk, ALU.mult)
                else:
                    go(V.tensor_tensor, w16, oh, rk, ALU.mult)
                go(V.tensor_reduce, pc(0).unsqueeze(2), r[11][:, 0:256].rearrange("p (c e) -> p c e", e=8), AX_X, ALU.add,
                   m=f"{L}.rf{H}")
                kp = pc(96)
                go(V.tensor_scalar, kp, pc(0), cap, None, ALU.is_lt)
                go(V.tensor_tensor, pc(128), pc(0), pc(32), ALU.add)
                go(V.tensor_tensor, pc(160), pc(128), ds, ALU.subtract)
                go(V.tensor_tensor, pc(160), pc(160), kp, ALU.mult)
                go(V.tensor_tensor, idxS[:, 16 * H:16 * H + 16, :].rearrange("p t c -> p (t c)"), pc(160), ds, ALU.add,
                   m=f"{L}.is{H}")
                go(V.scalar_tensor_tensor, pc(192), pc(128), dg, kp, ALU.subtract, ALU.mult)
                go(V.tensor_scalar, idxG[:, 16 * H:16 * H + 16, :].rearrange("p t c -> p (t c)"), pc(192), dg, None, ALU.add)
                kc = kp.rearrange("p (t c) -> p t c", c=2)
                for c in range(2):
                    go(V.tensor_tensor, gates[:, 16 * H:16 * H + 16, c:c + 1], s1(5 + c), kc[:, :, c:c + 1], ALU.mult,
                       m=f"{L}.gt{H}" if c else None)
                sem = P.dma_sem(f"{L}_scatter{H}")
                for t in range(16 * H, 16 * H + 16):
                    for c in range(2):
                        P.op("pool", G.indirect_dma_start, xbuf, bass.IndirectOffsetOnAxis(ap=idxS[:, t, c:c + 1], axis=0),
                             xall[:, t, :], None, w=[f"{L}.is{H}", "zeroed"])
                        pq, last = P.q["pool"], P.q["pool"].ops.pop()
                        pq.ops.append(last[:4] + ((sem, 16),))
                P.at[f"{L}.sd{H}"] = (sem, 512)

            for B in range(4):
                logits(B)
            route(0)
            for B in range(4, NBK):
                logits(B)
            route(1)

            groups = []
            for e in range(8):
                c = 0
                for n in (4, 4, 3) if kind == 0 else (3, 2):
                    groups.append((e, nch * e + c, n))
                    c += n
            NG = len(groups)
            ring = [uni[:, 9728 + 512 * i:10240 + 512 * i] for i in range(4)]
            yo = [uni[:, 7168 + 512 * i:7680 + 512 * i] for i in range(2)]
            xT3 = [uni[:, 8192 + 512 * i:8704 + 512 * i] for i in range(2)]
            rd_ = [P.dma_sem(f"{L}_rd{i}") for i in range(4)]
            wr_ = [P.dma_sem(f"{L}_wr{i}") for i in range(2)]
            hc = [0]
            hfree = {}

            def fetch(i):
                e, c, n = groups[i]
                P.dma(nc.sync.dma_start, ring[i % 4][:, 0:128 * n].rearrange("p (c d) -> p c d", c=n),
                      xbuf[128 * c:128 * (c + n), :].rearrange("(c p) d -> p c d", p=128), rd_[i % 4], f"{L}.fe{i}", i // 4 + 1,
                      w=[f"{L}.sd0", f"{L}.sd1"] + if_(i, "et", 4))

            def turn(i):
                e, c, n = groups[i]
                for j in range(n):
                    pe(T.transpose, b0[:, 128 * j:128 * j + 128], ring[i % 4][:, 128 * j:128 * j + 128], ident[:, :],
                       w=[f"{L}.fe{i}", f"{L}.xc{NBK - 1}"] + if_(i, "ec", 1), m=f"{L}.et{i}" if j == n - 1 else None)
                act(S.activation, xT3[i % 2][:, 0:128 * n], b0[:, 0:128 * n], ACT.Copy,
                    w=[f"{L}.et{i}", f"{L}.gt1"] + if_(i, "uh", 2), m=f"{L}.ec{i}")

            def up(i):
                e, c, n = groups[i]
                nt = 257 if kind == 0 and n == 3 else 128 * n
                for j in range(4):
                    sl = hc[0] % 4
                    pe(T.matmul, HB[sl][:, 0:nt], W1[:, e, 128 * j:128 * j + 128], xT3[i % 2][:, 0:nt],
                       start=True, stop=True, w=[f"{L}.ec{i}", f"{L}.w{e}", f"{L}.rf1"]
                       + ([hfree[sl]] if sl in hfree else []), m=f"{L}.uj{i}.{j}" if j < 3 else f"{L}.uh{i}")
                    w = [f"{L}.uj{i}.{j}" if j < 3 else f"{L}.uh{i}"] + if_(i, "dn", 2)
                    h = hS[i % 2][:, j, 0:nt]
                    if kind == 0:
                        act(S.activation, h, HB[sl][:, 0:nt], ACT.Silu, w=w, m=f"{L}.hm{i}.{j}")
                    elif j % 2:
                        act(S.activation, h, HB[sl][:, 0:nt], ACT.Relu, bias=B1[:, e, j:j + 1], w=w + ["ld.b"], m=f"{L}.hm{i}.{j}")
                    else:
                        dve(V.tensor_scalar, h, HB[sl][:, 0:nt], B1[:, e, j:j + 1], 0.0, ALU.add, ALU.max,
                            w=w + ["ld.b"], m=f"{L}.hm{i}.{j}")
                    hfree[sl] = f"{L}.hm{i}.{j}"
                    hc[0] += 1

            def down(i):
                e, c, n = groups[i]
                y = YB[i % 2]
                for j in range(n):
                    for k in range(4):
                        pe(T.matmul, y[:, 128 * j:128 * j + 128], hS[i % 2][:, k, 128 * j:128 * j + 128], W2[:, e, k, :],
                           start=k == 0, stop=k == 3, w=[f"{L}.hm{i}.{q}" for q in range(4)] + if_(i, "yo", 2),
                           m=f"{L}.dn{i}" if j == n - 1 and k == 3 else None)
                o = yo[i % 2][:, 0:128 * n]
                w = [f"{L}.dn{i}"] + ([f"{L}.yw{i - 2}"] if i >= 2 else [])
                if kind == 0:
                    dve(V.tensor_copy, o, y[:, 0:128 * n], w=w, m=f"{L}.yo{i}")
                else:
                    dve(V.tensor_tensor, o.rearrange("p (c d) -> p c d", c=n), y[:, 0:128 * n].rearrange("p (c d) -> p c d", c=n),
                        b2r[:, e, :].unsqueeze(1).to_broadcast([128, n, 128]), ALU.add, w=w + ["ld.b"], m=f"{L}.yo{i}")
                P.dma(nc.sync.dma_start, ybuf[128 * c:128 * (c + n), :].rearrange("(c p) d -> p c d", p=128),
                      o.rearrange("p (c d) -> p c d", c=n), wr_[i % 2], f"{L}.yw{i}", i // 2 + 1, w=[f"{L}.yo{i}"])

            for i in range(3):
                fetch(i)
            turn(0)
            up(0)
            turn(1)
            for i in range(NG):
                if i + 1 < NG:
                    up(i + 1)
                if i + 3 < NG:
                    fetch(i + 3)
                if i + 2 < NG:
                    turn(i + 2)
                down(i)

            gsem = [P.dma_sem(f"{L}_g{i}") for i in range(8)]

            def gather(t):
                for c in range(2):
                    i = 2 * t + c
                    P.op("pool", G.indirect_dma_start, gb[i % 8][:, :], None, ybuf,
                         bass.IndirectOffsetOnAxis(ap=idxG[:, t, c:c + 1], axis=0),
                         w=[f"{L}.yw{NG - 1}", f"{L}.yw{NG - 2}", f"{L}.gt1", "zeroed"] + if_(i, "cb", 8))
                    pq, last = P.q["pool"], P.q["pool"].ops.pop()
                    pq.ops.append(last[:4] + ((gsem[i % 8], 16),))
                    P.at[f"{L}.ga{i}"] = (gsem[i % 8], 16 * (i // 8 + 1))

            def combine(t, c):
                i = 2 * t + c
                dve(V.scalar_tensor_tensor, X[:, t, :], gb[i % 8][:, :], gates[:, t, c:c + 1], X[:, t, :], ALU.mult, ALU.add,
                    w=[f"{L}.ga{i}"] + ([f"{L}.cb{i - 1}"] if c else []) + ([f"{L}.xa{NBK - 1}"] if kind == 0 else []),
                    m=f"{L}.cb{i}")
            return L, gather, combine

        def nearest(L, w1, w2):
            begin(L)
            xbuf, ybuf = SP[L]
            W1, W2 = weights(w1, w2, nf=2)
            NC = 39
            xr = uni[:, 0:4096].rearrange("p (t d) -> p t d", t=NT)
            xnb = [uni[:, 4096 + 512 * i:4608 + 512 * i].rearrange("p (t d) -> p t d", t=4) for i in range(4)]
            xT2 = [uni[:, 6144 + 512 * i:6656 + 512 * i] for i in range(2)]
            junk = uni[:, 7168:7296]
            tmp = [uni[:, 7296 + 256 * i:7552 + 256 * i] for i in range(8)]
            pre = [uni[:, 9344 + 384 * i:9728 + 384 * i] for i in range(2)]
            sq, r1, rr, nx = (small[:, 32 * i:32 * i + 32] for i in range(4))
            mn = small[:, 128:160]

            def if_(t, key, back=0):
                return [f"{L}.{key}{t - back}"] if t - back >= 0 else []

            square = link("act", f"{L}.s")

            def stA(B):
                moments(L, B, "A3.xz")

            def stB(B):
                mb = mvb[B]
                for j in range(4):
                    t = 4 * B + j
                    dve(V.tensor_scalar, xnb[B % 4][:, j, :], X[:, t, :], mb[:, 2 * j:2 * j + 1], mb[:, 12 + j:13 + j],
                        ALU.subtract, ALU.mult, w=[f"{L}.rs{B}"] + if_(B, "sq", 4) + if_(B, "xa", 4) + if_(4 * B + 3, "xs", 16), m=f"{L}.xn{t}")
                for j in range(4):
                    t = 4 * B + j
                    square(S.activation, junk, xnb[B % 4][:, j, :], ACT.Square, accum_out=sq[:, t:t + 1],
                           w=[f"{L}.xn{t}"], m=f"{L}.sq{B}" if j == 3 else None)
                xb = X[:, 4 * B:4 * B + 4, :]
                pool(G.tensor_tensor, xb, xb, xnb[B % 4], ALU.add, w=[f"{L}.xn{4 * B + 3}"], m=f"{L}.xa{B}")

            def stC(B):
                c = slice(4 * B, 4 * B + 4)
                dve(V.tensor_scalar, r1[:, c], sq[:, c], 1.0 / 128.0, 1e-6, ALU.mult, ALU.add, w=[f"{L}.sq{B}"], m=f"{L}.r1{B}")
                pool(G.tensor_tensor, rr[:, c], r1[:, c], sm("nh")[:, 0:4], ALU.pow, w=[f"{L}.r1{B}"], m=f"{L}.r2{B}")

            def stD(B):
                for j in range(4):
                    t = 4 * B + j
                    dve(V.scalar_tensor_tensor, xr[:, t, :], xnb[B % 4][:, j, :], rr[:, t:t + 1], row("scale3"),
                        ALU.mult, ALU.mult, w=[f"{L}.r2{B}"], m=f"{L}.xs{t}")
                for j in range(4):
                    t = 4 * B + j
                    square(S.activation, junk, xr[:, t, :], ACT.Square, accum_out=nx[:, t:t + 1],
                           w=[f"{L}.xs{t}"], m=f"{L}.nx{B}" if j == 3 else None)

            def stE(B):
                tb = (b0, b2p)[B % 2]
                for j in range(4):
                    t = 4 * B + j
                    pe(T.transpose, tb[:, 128 * j:128 * j + 128], xr[:, t, :], ident[:, :],
                       w=[f"{L}.xs{t}"] + if_(B, "xc", 2), m=f"{L}.xT{B}" if j == 3 else None)
                act(S.activation, xT2[B % 2], tb[:, :], ACT.Copy, w=[f"{L}.xT{B}"] + if_(B, "lg", 2), m=f"{L}.xc{B}")

            def stF(B):
                for j in range(4):
                    c = 8 * (4 * B + j)
                    pe(T.matmul, b1p[:, c:c + 8], xT2[B % 2][:, 128 * j:128 * j + 128], sm("c3"),
                       start=True, stop=True, w=[f"{L}.xc{B}"], m=f"{L}.lg{B}" if j == 3 else None)
            for p_ in pre:
                dve(V.memset, p_[:, 0:128], 0.0, m=f"{L}.pz{int(p_ is pre[1])}")
            dve(V.memset, pads[:, :], 0.0, m=f"{L}.pz")
            for i in range(NBK + 5):
                for f, d in ((stA, 0), (stB, 1), (stC, 2), (stD, 3), (stE, 4), (stF, 5)):
                    if 0 <= i - d < NBK:
                        f(i - d)

            def v3(a):
                return a.rearrange("p (t e) -> p t e", e=8)

            def over(a):
                return a.unsqueeze(1).to_broadcast([128, NT, 8])

            def along(a):
                return a.unsqueeze(2).to_broadcast([128, NT, 8])
            go = link("dve", f"{L}.g", first=[f"{L}.lg{NBK - 1}", f"{L}.nx{NBK - 1}"])
            go(V.tensor_tensor, v3(tmp[0]), along(nx), over(ny[:, :]), ALU.add)
            go(V.scalar_tensor_tensor, tmp[1], b1p[:, 0:256], -2.0, tmp[0], ALU.mult, ALU.add)
            go(V.tensor_reduce, mn.unsqueeze(2), v3(tmp[1]), AX_X, ALU.min)
            go(V.tensor_tensor, v3(tmp[2]), v3(tmp[1]), along(mn), ALU.is_equal)
            go(V.tensor_tensor, v3(tmp[2]), v3(tmp[2]), over(sm("revi")), ALU.mult)
            go(V.tensor_reduce, mn.unsqueeze(2), v3(tmp[2]), AX_X, ALU.max)
            go(V.tensor_tensor, v3(tmp[3]), v3(tmp[2]), along(mn), ALU.is_equal, m=f"{L}.oh")
            pe(T.matmul, b7[:, 0:256], ones[:, :], tmp[3], start=True, stop=True, w=[f"{L}.oh"], m=f"{L}.cn")
            pe(T.matmul, b2p[:, 0:256], tri[:, :], tmp[3], start=True, stop=True, m=f"{L}.rk")
            go(V.tensor_copy, pre[0][:, 128:384], b7[:, 0:256], w=[f"{L}.cn"])
            for i, st in enumerate((1, 2, 4, 8, 16)):
                a, b_ = pre[i % 2], pre[(i + 1) % 2]
                go(V.tensor_tensor, b_[:, 128:384], a[:, 128:384], a[:, 128 - 8 * st:384 - 8 * st], ALU.add)
            inc = pre[1]
            pa, pb = pads[:, 0:16], pads[:, 16:32]
            go(V.tensor_scalar, pb[:, 0:8], inc[:, 376:384], 1.0 / 128.0, 0.5 - 1.0 / 256.0, ALU.mult, ALU.add)
            go(V.tensor_scalar, pa[:, 8:16], pb[:, 0:8], MAGIC, MAGIC, ALU.add, ALU.subtract)
            go(V.memset, pb[:, 0:8], 0.0)
            go(V.tensor_tensor, pb[:, 8:16], pa[:, 8:16], pa[:, 7:15], ALU.add)
            go(V.tensor_tensor, pa[:, 8:16], pb[:, 8:16], pb[:, 6:14], ALU.add)
            go(V.tensor_tensor, pb[:, 8:16], pa[:, 8:16], pa[:, 4:12], ALU.add)
            go(V.tensor_scalar, pads[:, 32:40], pb[:, 7:15], 128.0, None, ALU.mult)
            go(V.tensor_tensor, tmp[4], b2p[:, 0:256], inc[:, 120:376], ALU.add, w=[f"{L}.rk"])
            go(V.tensor_tensor, v3(tmp[5]), v3(tmp[4]), over(pads[:, 32:40]), ALU.add)
            go(V.tensor_tensor, tmp[6], tmp[5], tmp[3], ALU.mult)
            go(V.tensor_reduce, mn.unsqueeze(2), v3(tmp[6]), AX_X, ALU.add)
            go(V.tensor_copy, idxS[:, :, 0], mn, m=f"{L}.is")
            ct = uni[:, 7296:7616].rearrange("p (c e) -> p c e", e=8)
            go(V.tensor_tensor, ct, pb[:, 8:16].unsqueeze(1).to_broadcast([128, 40, 8]),
               K["chunk"][:, :].unsqueeze(2).to_broadcast([128, 40, 8]), ALU.is_le)
            go(V.tensor_reduce, uni[:, 7616:7656].unsqueeze(2), ct, AX_X, ALU.add)
            go(V.tensor_scalar, uni[:, 7616:7656], uni[:, 7616:7656], 7.0, None, ALU.min)
            go(V.tensor_copy, etab[:, :], uni[:, 7616:7656], m=f"{L}.tab")
            sem = P.dma_sem(f"{L}_scatter")
            for t in range(NT):
                P.op("pool", G.indirect_dma_start, xbuf, bass.IndirectOffsetOnAxis(ap=idxS[:, t, 0:1], axis=0),
                     xr[:, t, :], None, w=[f"{L}.is", "zeroed", f"{L}.xa{NBK - 1}"])
                pq, last = P.q["pool"], P.q["pool"].ops.pop()
                pq.ops.append(last[:4] + ((sem, 16),))
            P.at[f"{L}.sd"] = (sem, 16 * NT)

            NG = 10
            ring = [uni[:, 4096 + 512 * i:4608 + 512 * i] for i in range(4)]
            xT3 = [uni[:, 6144 + 512 * i:6656 + 512 * i] for i in range(2)]
            gs = [uni[:, 7168 + 256 * i:7424 + 256 * i] for i in range(3)]
            hm = [uni[:, 7936 + 256 * i:8192 + 256 * i] for i in range(3)]
            hT = [uni[:, 8704 + 256 * i:8960 + 256 * i] for i in range(3)]
            yo = [uni[:, 9472 + 512 * i:9984 + 512 * i] for i in range(2)]
            HB = [b2p[:, :], bS[:, 0:512], bS[:, 512:1024]]
            TB = [b1p[:, 0:256], b7[:, 0:256]]
            YB = [bP[:, 0:512], bP[:, 512:1024]]
            rd_ = [P.dma_sem(f"{L}_rd{i}") for i in range(4)]
            wr_ = [P.dma_sem(f"{L}_wr{i}") for i in range(2)]
            reg = {}

            def size(g):
                return min(4, NC - 4 * g)

            def fetch(g):
                n = size(g)
                P.dma(nc.sync.dma_start, ring[g % 4][:, 0:128 * n].rearrange("p (c d) -> p c d", c=n),
                      xbuf[512 * g:512 * g + 128 * n, :].rearrange("(c p) d -> p c d", p=128), rd_[g % 4], f"{L}.fe{g}", g // 4 + 1,
                      w=[f"{L}.sd", f"{L}.xc{NBK - 1}"] + if_(g, "et", 4))

            def turn(g):
                n = size(g)
                for j in range(n):
                    pe(T.transpose, b0[:, 128 * j:128 * j + 128], ring[g % 4][:, 128 * j:128 * j + 128], ident[:, :],
                       w=[f"{L}.fe{g}"] + if_(g, "ec", 1), m=f"{L}.et{g}" if j == n - 1 else None)
                act(S.activation, xT3[g % 2][:, 0:128 * n], b0[:, 0:128 * n], ACT.Copy,
                    w=[f"{L}.et{g}"] + if_(4 * g + 3, "up", 8), m=f"{L}.ec{g}")

            def load(c):
                reg[c] = nc.tensor.value_load(etab[0:1, c:c + 1], min_val=0, max_val=7)

            def up_(c, b):
                return T.matmul(HB[b], xT3[c // 4 % 2][:, 128 * (c % 4):128 * (c % 4) + 128],
                                big1[:, bass.ds(reg[c] * 512, 512)], start=True, stop=True)

            def down_(c, k):
                return T.matmul(YB[c // 4 % 2][:, 128 * (c % 4):128 * (c % 4) + 128], hT[c % 3][:, 128 * k:128 * k + 128],
                                big2[:, bass.ds(reg[c] * 256 + 128 * k, 128)], start=k == 0, stop=k == 1)

            def register(c):
                P.op("pe", load, c, w=[f"{L}.tab"])

            def up(c):
                b = c % 3
                pe(up_, c, b, w=[f"{L}.ec{c // 4}", f"{L}.tab", f"{L}.is"] + [f"{L}.w{e}" for e in range(8)] + if_(c, "hg", 3)
                   + if_(c, "hm", 3), m=f"{L}.up{c}")
                act(S.activation, gs[b], HB[b][:, 256:512], ACT.Silu, w=[f"{L}.up{c}"] + if_(c, "hm", 3), m=f"{L}.hg{c}")
                dve(V.tensor_tensor, hm[b], HB[b][:, 0:256], gs[b], ALU.mult, w=[f"{L}.hg{c}"] + if_(c, "ht", 3), m=f"{L}.hm{c}")

            def mid(c):
                for k in range(2):
                    pe(T.transpose, TB[c % 2][:, 128 * k:128 * k + 128], hm[c % 3][:, 128 * k:128 * k + 128], ident[:, :],
                       w=[f"{L}.hm{c}"] + if_(c, "hc", 2), m=f"{L}.ht{c}" if k else None)
                if c % 2:
                    act(S.activation, hT[c % 3], TB[c % 2], ACT.Copy, w=[f"{L}.ht{c}"] + if_(c, "dn", 3), m=f"{L}.hc{c}")
                else:
                    dve(V.tensor_copy, hT[c % 3], TB[c % 2], w=[f"{L}.ht{c}"] + if_(c, "dn", 3), m=f"{L}.hc{c}")

            def down(c):
                g = c // 4
                for k in range(2):
                    pe(down_, c, k, w=[f"{L}.hc{c}"] + if_(g, "yo", 2), m=f"{L}.dn{c}" if k else None)
                n = size(g)
                if c % 4 == n - 1:
                    o = yo[g % 2][:, 0:128 * n]
                    dve(V.tensor_copy, o, YB[g % 2][:, 0:128 * n], w=[f"{L}.dn{c}"] + if_(g, "yw", 2), m=f"{L}.yo{g}")
                    P.dma(nc.sync.dma_start, ybuf[512 * g:512 * g + 128 * n, :].rearrange("(c p) d -> p c d", p=128),
                          o.rearrange("p (c d) -> p c d", c=n), wr_[g % 2], f"{L}.yw{g}", g // 2 + 1, w=[f"{L}.yo{g}"])
            for g in range(3):
                fetch(g)
            turn(0)
            for i in range(NC + 4):
                if i < NC:
                    register(i)
                    if i % 4 == 1 and i // 4 + 1 < NG:
                        turn(i // 4 + 1)
                        if i // 4 + 3 < NG:
                            fetch(i // 4 + 3)
                    up(i)
                if 0 <= i - 2 < NC:
                    mid(i - 2)
                if 0 <= i - 4 < NC:
                    down(i - 4)

            gsem = [P.dma_sem(f"{L}_g{i}") for i in range(8)]
            so = P.dma_sem("so")
            for t in range(NT):
                P.op("pool", G.indirect_dma_start, gb[t % 8][:, :], None, ybuf,
                     bass.IndirectOffsetOnAxis(ap=idxS[:, t, 0:1], axis=0),
                     w=[f"{L}.yw{NG - 1}", f"{L}.yw{NG - 2}"] + if_(t, "cb", 8))
                pq, last = P.q["pool"], P.q["pool"].ops.pop()
                pq.ops.append(last[:4] + ((gsem[t % 8], 16),))
                P.at[f"{L}.ga{t}"] = (gsem[t % 8], 16 * (t // 8 + 1))
                dve(V.tensor_tensor, X[:, t, :], X[:, t, :], gb[t % 8][:, :], ALU.add, w=[f"{L}.ga{t}", f"{L}.xa{t // 4}"],
                    m=f"{L}.cb{t}")
                if t % 4 == 3:
                    P.dma(nc.sync.dma_start, ov[:, t - 3:t + 1, :], X[:, t - 3:t + 1, :], so, "out", 8, w=[f"{L}.cb{t}"])

        def qlin(L):
            begin(L)
            weights(upw, dnw, "F3", 2)

            def if_(t, key, back=0):
                return [f"{L}.{key}{t - back}"] if t - back >= 0 else []

            fxT = [uni[:, 9216 + 512 * i:9728 + 512 * i] for i in range(2)]
            xn2 = [uni[:, 512 * i:512 * i + 512].rearrange("p (t d) -> p t d", t=4) for i in range(4)]
            xq = [uni[:, 2048 + 512 * i:2560 + 512 * i].rearrange("p (t d) -> p t d", t=4) for i in range(4)]
            bufs = [[uni[:, 4096 + 512 * (5 * i + j):4608 + 512 * (5 * i + j)] for j in range(5)] for i in range(2)]

            def norm(B):
                mb = mvb[B]
                for j in range(4):
                    t = 4 * B + j
                    dve(V.tensor_scalar, xn2[B % 4][:, j, :], X[:, t, :], mb[:, 2 * j:2 * j + 1], mb[:, 12 + j:13 + j],
                        ALU.subtract, ALU.mult, w=[f"{L}.rs{B}"] + if_(B, "qd", 4), m=f"{L}.ln{t}.xn")

            def quant(Bs):
                keys = quantise([(f"{L}.{B}", xn2[B % 4].rearrange("p t d -> p (t d)"), xq[B % 4].rearrange("p t d -> p (t d)"),
                                  512, rt[B % 2][0], bufs[B % 2], [f"{L}.ln{4 * B + 3}.xn"] + if_(B, "xT", 4) + if_(B, "qd", 2))
                                 for B in Bs], True)
                for B, key in zip(Bs, keys):
                    P.at[f"{L}.qd{B}"] = P.at[key]

            def second(B):
                for j in range(4):
                    pe(T.transpose, b0[:, 128 * j:128 * j + 128], xq[B % 4][:, j, :], ident[:, :],
                       w=[f"{L}.qd{B}"] + if_(B, "xc", 1), m=f"{L}.xT{B}" if j == 3 else None)
                act(S.activation, fxT[B % 2], b0[:, :], ACT.Copy, w=[f"{L}.xT{B}"] + if_(B, "Y", 2), m=f"{L}.xc{B}")
                for j in range(4):
                    pe(T.matmul, b1p[:, 128 * j:128 * j + 128], fxT[B % 2][:, 128 * j:128 * j + 128], wdT[:, :],
                       start=True, stop=True, w=[f"{L}.xc{B}"] + if_(B, "xr", 1), m=f"{L}.Y{B}" if j == 3 else None)
                xb = X[:, 4 * B:4 * B + 4, :]
                pool(G.tensor_tensor, xb, xb, row("b2ffn").unsqueeze(1).to_broadcast([128, 4, 128]), ALU.add,
                     w=[f"{L}.ln{4 * B + 3}.xn"], m=f"{L}.xb{B}")
                dve(V.tensor_tensor, xb.rearrange("p t d -> p (t d)"), xb.rearrange("p t d -> p (t d)"), b1p[:, :], ALU.add,
                    w=[f"{L}.Y{B}", f"{L}.xb{B}"], m=f"{L}.xr{B}")
            norm(0)
            norm(1)
            for i in range(NBK // 2):
                quant((2 * i, 2 * i + 1))
                for B in (2 * i + 2, 2 * i + 3):
                    if B < NBK:
                        norm(B)
                if i:
                    second(2 * i - 2)
                    second(2 * i - 1)
            second(NBK - 2)
            second(NBK - 1)

        attention("A0", 0)
        r0 = sparse("F0", 0, w1a, w2a)
        attention("A1", 1, r0)
        r1 = sparse("F1", 1, w1b, w2b)
        attention("A2", 2, r1)
        qlin("F2")
        attention("A3", 3)
        nearest("F3", upw, dnw)
        P.q["sp"].ops.append((None, (), {}, ("out",), None))

        block = es.enter_context(nc.Block())

        @block.sync
        def _(e):
            P.emit("sp", e)

        @block.gpsimd
        def _(e):
            P.emit("pool", e)

        @block.scalar
        def _(e):
            P.emit("act", e)

        @block.vector
        def _(e):
            P.emit("dve", e)

        @block.tensor
        def _(e):
            P.emit("pe", e)


def kernel(**inp):
    import numpy as np
    import concourse.bacc as bacc
    from concourse.bass_utils import run_bass_kernel_spmd as run

    a = {k: np.asarray(v) for k, v in inp.items()}
    f = np.float32
    swap = np.arange(128).reshape(64, 2)[:, ::-1].reshape(128)

    def l3(n):
        return a["L3_xattn_" + n][3]
    sq = {
        "L0q": a["L0_xattn_wq"].T, "L0k": a["L0_xattn_wk"].T, "L0v": a["L0_xattn_wv"].T, "L0o": a["L0_xattn_wo"].T,
        "L2q": a["L2_xattn_wq"].reshape(128, 128), "L2k": a["L2_xattn_wk"].reshape(128, 128),
        "L2v": a["L2_xattn_wv"].reshape(128, 128), "L2o": a["L2_xattn_wo"].reshape(128, 128),
        "va": l3("W_va").T, "vt": l3("W_vt").T, "o3": l3("W_o").T, "ffn3": l3("W_ffn").T,
    }
    cl = {"bq0": a["L0_xattn_bq"], "bk0": a["L0_xattn_bk"], "gamma": l3("gamma"), "beta": l3("beta"),
          "gf": np.broadcast_to(l3("gating_factor"), (128,)), "td": np.broadcast_to(a["L0_xattn_time_decay"], (128,))}
    for n in ("qa", "ka", "qt", "kt"):
        sq[n] = l3("W_" + n).T
        sq[n + "r"] = l3("W_" + n)[swap].T
        cl[n] = l3("b_" + n)
        cl[n + "r"] = l3("b_" + n)[swap]
    wide = np.broadcast_to
    rw = {"bv0": wide(a["L0_xattn_bv"], (128, 128)), "bo0": wide(a["L0_xattn_bo"], (128, 128)),
          "bv3": np.concatenate([wide(l3("b_va"), (64, 128)), wide(l3("b_vt"), (64, 128))]),
          "bo3": wide(l3("b_o"), (128, 128)), "bffn3": wide(l3("b_ffn"), (128, 128)),
          "b2ffn": wide(a["L2_ffn_bias"], (128, 128)), "scale3": wide(a["L3_ffn_scale"], (128, 128))}
    sml = {"r0": a["L0_ffn_router_w"].T, "r1": a["L1_ffn_gate_w"].T, "c3": a["L3_ffn_centroids"].T,
           "gb": wide(a["L1_ffn_gate_b"], (128, 8)), "revi": wide(np.arange(8, 0, -1).astype(f), (128, 8)),
           "nh": np.full((128, 8), -0.5, f)}
    p = np.arange(128)
    inv = (1.0 / 10000.0 ** (np.arange(0, 16, 2, dtype=f) / f(16))).astype(f)
    fr = (np.arange(64, dtype=f)[:, None] * inv[None, :]).astype(f)
    ang = fr[p % 64][:, (p % 16) % 8].T
    sign = np.where(p % 2 == 0, -1.0, 1.0).astype(f)[:, None]
    cst = {
        "ident": np.eye(128, dtype=f), "ones": np.ones((128, 128), f),
        "tri": (p[:, None] < p[None, :]).astype(f), "cos": np.cos(ang), "sin": np.sin(ang) * sign,
        "dist": np.abs((p % 64)[:, None] - np.arange(64)[None, :]).astype(f),
        "causal": (np.arange(64)[None, :] <= (p % 64)[:, None]).astype(f),
        "km8": ((p % 32)[:, None] // 8 == np.arange(4)[None, :]).astype(f),
        "jm": (p[:, None] // 32 == np.arange(4)[None, :]).astype(f),
        "DS": (np.arange(128) // 2 * 128 + np.arange(128) % 2 * 4096)[None, :].repeat(128, 0).astype(f),
        "chunk": wide(np.arange(40).astype(f), (128, 40)),
        "DG": p[:, None].astype(f),
        "e0": wide((np.arange(16) % 8 * 1408).astype(f), (128, 16)), "e1": wide((np.arange(16) % 8 * 640 + np.arange(16) // 8 * 320).astype(f), (128, 16)),
        "km16": ((p % 32)[:, None] // 16 == np.arange(2)[None, :]).astype(f),
    }
    arrays = {
        "x": a["x"], "ctx": a["ctx_1024"], "mask": a["mask_Bx1xSxS2_ff0"],
        "wsq": np.stack([sq[n] for n in SQ], 1), "cols": np.stack([cl[n] for n in COL], 1),
        "rows": np.stack([rw[n] for n in ROW], 1), "smalls": np.stack([sml[n] for n in SM], 1),
        "wq2": a["L2_ffn_weight"], "w1a": a["L0_ffn_w1"], "w2a": a["L0_ffn_w2"], "w1b": a["L1_ffn_W1"],
        "w2b": a["L1_ffn_W2"], "b1": a["L1_ffn_b1"].reshape(8, 4, 128).transpose(2, 0, 1), "b2": a["L1_ffn_b2"],
        "upw": a["L3_ffn_up_w"], "dnw": a["L3_ffn_down_w"],
    }
    for n in CST:
        arrays["c_" + n] = cst[n]
    arrays = {k: np.ascontiguousarray(v) for k, v in arrays.items()}
    nc = bacc.Bacc("TRN2", target_bir_lowering=False, num_devices=1)
    d = {k: nc.dram_tensor(k + "_dram", v.shape, mybir.dt.from_np(v.dtype), kind="ExternalInput").ap()
         for k, v in arrays.items()}
    out = nc.dram_tensor("out_dram", (64, 64, 128), F32, kind="ExternalOutput").ap()
    build(nc, d["x"], d["ctx"], d["mask"], d["wsq"], d["cols"], d["rows"], d["smalls"], {n: d["c_" + n] for n in CST},
          d["wq2"], d["w1a"], d["w2a"], d["w1b"], d["w2b"], d["b1"], d["b2"], d["upw"], d["dnw"], out)
    r = run(nc, [{k + "_dram": v for k, v in arrays.items()}], core_ids=[0])
    return r.results[0]["out_dram"]
```
